# Optimizing a Trainium2 kernel written in Bass

```python
import numpy as np
import jax
import jax.numpy as jnp

def _softmax(x, axis=-1):
    return jax.nn.softmax(x, axis=axis)

def _gelu(x):
    return jax.nn.gelu(x, approximate=True)

def _silu(x):
    return jax.nn.silu(x)

def _sigmoid(x):
    return jax.nn.sigmoid(x)

def _layernorm(x, axis=-1, eps=1e-05):
    m = jnp.mean(x, axis=axis, keepdims=True)
    v = jnp.var(x, axis=axis, keepdims=True)
    return (x - m) / jnp.sqrt(v + eps)

def _scatter_add(tgt, idx, src, axis=0):
    return tgt.at[idx].add(src)

def _segment_sum(src, seg, n):
    return jax.ops.segment_sum(src, seg, n)
kernel_name = 'mk_flamingo_gated_d2_seqx_r8_30edf2'

def setup_inputs(seed: int=0):
    np.random.seed(seed)
    _w = jnp.asarray

    def _rec_inputs():
        import jax
        import jax.numpy as jnp
        _rk = jax.random.key(seed)
        x = -0.0003929 + 0.9999 * jax.random.normal(jax.random.fold_in(_rk, 1), (8, 256, 256), jnp.float32)
        _lenS = 256 - jax.random.randint(jax.random.fold_in(_rk, 7), (8,), 0, max(1, 256 // 4) + 1, jnp.int32)
        _lenS2 = 64 - jax.random.randint(jax.random.fold_in(_rk, 8), (8,), 0, max(1, 64 // 4) + 1, jnp.int32)
        _ctx_1024P = jax.random.normal(jax.random.fold_in(_rk, 11), (8, 16, 128), jnp.float32)
        _ctx_1024c = jax.random.dirichlet(jax.random.fold_in(_rk, 511), 0.3 * jnp.ones((16,), jnp.float32), (8, 64))
        _ctx_1024t = jnp.einsum('bsk,bkd->bsd', _ctx_1024c, _ctx_1024P)
        _ctx_1024t = _ctx_1024t * jax.lax.rsqrt(jnp.mean(jnp.square(_ctx_1024t)) + 1e-12) * 0.953939
        ctx_1024 = 0.000227908 + 0.99994 * (_ctx_1024t + 0.3 * jax.random.normal(jax.random.fold_in(_rk, 611), (8, 64, 128), jnp.float32))
        _g = jax.random.normal(jax.random.fold_in(_rk, 9001), (2, 2), jnp.float32)
        _g = jnp.sign(_g) * jnp.maximum(jnp.abs(_g), 1.0) + (_g == 0) * 1.0
        g_xattn = _g[0]
        g_ffn = _g[1]
        return (x, ctx_1024, g_xattn, g_ffn)
    x, ctx_1024, g_xattn, g_ffn = _rec_inputs()

    def _L0_xattn_setup():
        import jax, jax.numpy as jnp
        import numpy as np
        EPS = 1e-05

        def rmsnorm(x, g, eps=EPS):
            var = jnp.mean(jnp.square(x), axis=-1, keepdims=True)
            return x * jax.lax.rsqrt(var + eps) * g
        key = jax.random.key(seed)
        ks = jax.random.split(key, 8)
        B, Sq, Skv = (2, 512, 64)
        dim, cdim, H, D = (256, 128, 16, 128)
        inner = H * D
        s = lambda f: 1.0 / np.sqrt(f)
        return {'hidden_states': jax.random.normal(ks[0], (B, Sq, dim), jnp.float32), 'encoder_hidden_states': jax.random.normal(ks[1], (B, Skv, cdim), jnp.float32), 'Wq': jax.random.normal(ks[2], (dim, inner), jnp.float32) * s(dim), 'Wk': jax.random.normal(ks[3], (cdim, inner), jnp.float32) * s(cdim), 'Wv': jax.random.normal(ks[4], (cdim, inner), jnp.float32) * s(cdim), 'Wo': jax.random.normal(ks[5], (inner, dim), jnp.float32) * s(inner), 'gq': jnp.ones((D,), jnp.float32), 'gk': jnp.ones((D,), jnp.float32)}
    _L0_xattn_all = _L0_xattn_setup()
    _L0_xattn_in = {k: v for k, v in _L0_xattn_all.items() if k in ('Wq', 'Wk', 'Wv', 'Wo', 'gq', 'gk')}
    del _L0_xattn_all

    def _L0_ffn_setup():
        import jax, jax.numpy as jnp
        import numpy as np
        from jax import lax
        E = 64
        H = 256
        I = 88
        G = 8
        TOPK_GROUP = 4
        K = 8
        B, S = (2, 256)
        N = B * S
        CAP = 2 * N * K // E
        SCALE = 2.5

        def _route(x, router_weight, e_bias):
            logits = x.astype(jnp.float32) @ router_weight.astype(jnp.float32).T
            scores = jax.nn.sigmoid(logits)
            sc = scores + e_bias
            n = x.shape[0]
            group_scores = lax.top_k(sc.reshape(n, G, E // G), 2)[0].sum(-1)
            grp_idx = lax.top_k(group_scores, TOPK_GROUP)[1]
            group_mask = jnp.zeros((n, G), jnp.float32).at[jnp.arange(n)[:, None], grp_idx].set(1.0)
            score_mask = jnp.repeat(group_mask, E // G, axis=1)
            masked = jnp.where(score_mask > 0, sc, 0.0)
            topk_idx = lax.top_k(masked, K)[1]
            topk_w = jnp.take_along_axis(scores, topk_idx, axis=1)
            topk_w = topk_w / (topk_w.sum(-1, keepdims=True) + 1e-20)
            return (topk_idx, topk_w * SCALE)

        def _moe_experts(x, topk_idx, topk_w, w_gate, w_up, w_down):
            n = x.shape[0]
            flat_e = topk_idx.reshape(-1)
            rows = jnp.repeat(jnp.arange(n), K)
            oh = jax.nn.one_hot(flat_e, E, dtype=jnp.int32)
            pos = jnp.cumsum(oh, axis=0) - oh
            pos = jnp.take_along_axis(pos, flat_e[:, None], axis=1)[:, 0]
            valid = (pos < CAP).astype(x.dtype)
            p = jnp.minimum(pos, CAP - 1)
            buf = jnp.zeros((E, CAP, H), x.dtype).at[flat_e, p].add(x[rows] * valid[:, None])
            g = jnp.einsum('ech,ehi->eci', buf, w_gate)
            u = jnp.einsum('ech,ehi->eci', buf, w_up)
            y = jnp.einsum('eci,eih->ech', jax.nn.silu(g) * u, w_down)
            y_tok = y[flat_e, p] * (topk_w.reshape(-1) * valid)[:, None]
            return jnp.zeros((n, H), x.dtype).at[rows].add(y_tok)

        def _shared_mlp(x, sh_gate, sh_up, sh_down):
            return jax.nn.silu(x @ sh_gate) * (x @ sh_up) @ sh_down
        key = jax.random.key(seed)
        ks = jax.random.split(key, 9)
        f32 = jnp.float32
        return {'hidden_states': jax.random.normal(ks[0], (B, S, H), f32), 'router_weight': jax.random.normal(ks[1], (E, H), f32) * (2.0 / H) ** 0.5, 'e_bias': jnp.zeros((E,), f32), 'w_gate': jax.random.normal(ks[2], (E, H, I), f32) * (1.0 / H) ** 0.5, 'w_up': jax.random.normal(ks[3], (E, H, I), f32) * (1.0 / H) ** 0.5, 'w_down': jax.random.normal(ks[4], (E, I, H), f32) * (1.0 / I) ** 0.5, 'sh_gate': jax.random.normal(ks[5], (H, I), f32) * (1.0 / H) ** 0.5, 'sh_up': jax.random.normal(ks[6], (H, I), f32) * (1.0 / H) ** 0.5, 'sh_down': jax.random.normal(ks[7], (I, H), f32) * (1.0 / I) ** 0.5}
    _L0_ffn_all = _L0_ffn_setup()
    _L0_ffn_in = {k: v for k, v in _L0_ffn_all.items() if k in ('router_weight', 'e_bias', 'w_gate', 'w_up', 'w_down', 'sh_gate', 'sh_up', 'sh_down')}
    del _L0_ffn_all

    def _L1_xattn_setup():
        import jax, jax.numpy as jnp
        import numpy as np
        B, S1, S2, DCA = (2, 256, 128, 16)
        QDIM, KDIM, H = (256, 128, 16)
        HD = QDIM // H
        SCALE = HD ** (-0.5)
        EPS = 1e-06
        DCA_WEIGHT = 1.0

        def _ln(t, w, b):
            m = jnp.mean(t, axis=-1, keepdims=True)
            v = jnp.var(t, axis=-1, keepdims=True)
            return (t - m) * jax.lax.rsqrt(v + EPS) * w + b

        def _attn(q, k, v):
            s = jnp.einsum('bhqd,bhkd->bhqk', q, k) * SCALE
            p = jax.nn.softmax(s, axis=-1)
            return jnp.einsum('bhqk,bhkd->bhqd', p, v)
        key = jax.random.key(seed)
        ks = jax.random.split(key, 8)
        w = lambda k, shape: jax.random.normal(k, shape, jnp.float32) * 0.02
        return {'x': jax.random.normal(ks[0], (B, S1, QDIM), jnp.float32), 'y': jax.random.normal(ks[1], (B, S2 + DCA, KDIM), jnp.float32), 'Wq': w(ks[2], (QDIM, QDIM)), 'bq': jnp.zeros((QDIM,), jnp.float32), 'Wk': w(ks[3], (KDIM, QDIM)), 'bk': jnp.zeros((QDIM,), jnp.float32), 'Wv': w(ks[4], (KDIM, QDIM)), 'bv': jnp.zeros((QDIM,), jnp.float32), 'Wkv_dca': w(ks[5], (KDIM, 2 * QDIM)), 'bkv_dca': jnp.zeros((2 * QDIM,), jnp.float32), 'qn_w': jnp.ones((HD,), jnp.float32), 'qn_b': jnp.zeros((HD,), jnp.float32), 'kn_w': jnp.ones((HD,), jnp.float32), 'kn_b': jnp.zeros((HD,), jnp.float32), 'kn_dca_w': jnp.ones((HD,), jnp.float32), 'kn_dca_b': jnp.zeros((HD,), jnp.float32), 'Wo': w(ks[6], (QDIM, QDIM)), 'bo': jnp.zeros((QDIM,), jnp.float32)}
    _L1_xattn_all = _L1_xattn_setup()
    _L1_xattn_in = {k: v for k, v in _L1_xattn_all.items() if k in ('Wq', 'bq', 'Wk', 'bk', 'Wv', 'bv', 'Wkv_dca', 'bkv_dca', 'qn_w', 'qn_b', 'kn_w', 'kn_b', 'kn_dca_w', 'kn_dca_b', 'Wo', 'bo')}
    del _L1_xattn_all

    def _L1_ffn_setup():
        import jax, jax.numpy as jnp
        import numpy as np
        TOP_K = 2
        key = jax.random.key(seed)
        ks = jax.random.split(key, 6)
        B, S, H, F, E = (1, 256, 256, 176, 8)
        Fs = 2 * F
        std = jnp.float32(0.02)
        return {'hidden_states': jax.random.normal(ks[0], (B, S, H), jnp.float32), 'gate_weight': jax.random.normal(ks[1], (E, H), jnp.float32) * std, 'gate_up_weights': jax.random.normal(ks[2], (E, 2 * F, H), jnp.float32) * std, 'down_weights': jax.random.normal(ks[3], (E, H, F), jnp.float32) * std, 'shared_gate_up': jax.random.normal(ks[4], (2 * Fs, H), jnp.float32) * std, 'shared_down': jax.random.normal(ks[5], (H, Fs), jnp.float32) * std}
    _L1_ffn_all = _L1_ffn_setup()
    _L1_ffn_in = {k: v for k, v in _L1_ffn_all.items() if k in ('gate_weight', 'gate_up_weights', 'down_weights', 'shared_gate_up', 'shared_down')}
    del _L1_ffn_all
    return {'x': x, 'ctx_1024': ctx_1024, 'g_xattn': g_xattn, 'g_ffn': g_ffn, 'L0_xattn_Wq': _L0_xattn_in['Wq'], 'L0_xattn_Wk': _L0_xattn_in['Wk'], 'L0_xattn_Wv': _L0_xattn_in['Wv'], 'L0_xattn_Wo': _L0_xattn_in['Wo'], 'L0_xattn_gq': _L0_xattn_in['gq'], 'L0_xattn_gk': _L0_xattn_in['gk'], 'L0_ffn_router_weight': _L0_ffn_in['router_weight'], 'L0_ffn_e_bias': _L0_ffn_in['e_bias'], 'L0_ffn_w_gate': _L0_ffn_in['w_gate'], 'L0_ffn_w_up': _L0_ffn_in['w_up'], 'L0_ffn_w_down': _L0_ffn_in['w_down'], 'L0_ffn_sh_gate': _L0_ffn_in['sh_gate'], 'L0_ffn_sh_up': _L0_ffn_in['sh_up'], 'L0_ffn_sh_down': _L0_ffn_in['sh_down'], 'L1_xattn_Wq': _L1_xattn_in['Wq'], 'L1_xattn_bq': _L1_xattn_in['bq'], 'L1_xattn_Wk': _L1_xattn_in['Wk'], 'L1_xattn_bk': _L1_xattn_in['bk'], 'L1_xattn_Wv': _L1_xattn_in['Wv'], 'L1_xattn_bv': _L1_xattn_in['bv'], 'L1_xattn_Wkv_dca': _L1_xattn_in['Wkv_dca'], 'L1_xattn_bkv_dca': _L1_xattn_in['bkv_dca'], 'L1_xattn_qn_w': _L1_xattn_in['qn_w'], 'L1_xattn_qn_b': _L1_xattn_in['qn_b'], 'L1_xattn_kn_w': _L1_xattn_in['kn_w'], 'L1_xattn_kn_b': _L1_xattn_in['kn_b'], 'L1_xattn_kn_dca_w': _L1_xattn_in['kn_dca_w'], 'L1_xattn_kn_dca_b': _L1_xattn_in['kn_dca_b'], 'L1_xattn_Wo': _L1_xattn_in['Wo'], 'L1_xattn_bo': _L1_xattn_in['bo'], 'L1_ffn_gate_weight': _L1_ffn_in['gate_weight'], 'L1_ffn_gate_up_weights': _L1_ffn_in['gate_up_weights'], 'L1_ffn_down_weights': _L1_ffn_in['down_weights'], 'L1_ffn_shared_gate_up': _L1_ffn_in['shared_gate_up'], 'L1_ffn_shared_down': _L1_ffn_in['shared_down']}

def reference(x, ctx_1024, g_xattn, g_ffn, L0_xattn_Wq, L0_xattn_Wk, L0_xattn_Wv, L0_xattn_Wo, L0_xattn_gq, L0_xattn_gk, L0_ffn_router_weight, L0_ffn_e_bias, L0_ffn_w_gate, L0_ffn_w_up, L0_ffn_w_down, L0_ffn_sh_gate, L0_ffn_sh_up, L0_ffn_sh_down, L1_xattn_Wq, L1_xattn_bq, L1_xattn_Wk, L1_xattn_bk, L1_xattn_Wv, L1_xattn_bv, L1_xattn_Wkv_dca, L1_xattn_bkv_dca, L1_xattn_qn_w, L1_xattn_qn_b, L1_xattn_kn_w, L1_xattn_kn_b, L1_xattn_kn_dca_w, L1_xattn_kn_dca_b, L1_xattn_Wo, L1_xattn_bo, L1_ffn_gate_weight, L1_ffn_gate_up_weights, L1_ffn_down_weights, L1_ffn_shared_gate_up, L1_ffn_shared_down):
    import jax
    import jax.numpy as jnp

    def _L0_xattn_ref(hidden_states, encoder_hidden_states, Wq, Wk, Wv, Wo, gq, gk):
        import jax, jax.numpy as jnp
        import numpy as np
        EPS = 1e-05

        def rmsnorm(x, g, eps=EPS):
            var = jnp.mean(jnp.square(x), axis=-1, keepdims=True)
            return x * jax.lax.rsqrt(var + eps) * g
        B, Sq, _ = hidden_states.shape
        Skv = encoder_hidden_states.shape[1]
        D = gq.shape[0]
        H = Wq.shape[1] // D
        scale = 1.0 / np.sqrt(D)
        q = (hidden_states @ Wq).reshape(B, Sq, H, D)
        k = (encoder_hidden_states @ Wk).reshape(B, Skv, H, D)
        v = (encoder_hidden_states @ Wv).reshape(B, Skv, H, D)
        q = rmsnorm(q, gq)
        k = rmsnorm(k, gk)
        scores = jnp.einsum('bqhd,bkhd->bhqk', q, k) * scale
        attn = jax.nn.softmax(scores, axis=-1)
        out = jnp.einsum('bhqk,bkhd->bqhd', attn, v)
        out = out.reshape(B, Sq, H * D)
        return out @ Wo

    def _L0_ffn_ref(hidden_states, router_weight, e_bias, w_gate, w_up, w_down, sh_gate, sh_up, sh_down):
        import jax, jax.numpy as jnp
        import numpy as np
        from jax import lax
        E = 64
        H = 256
        I = 88
        G = 8
        TOPK_GROUP = 4
        K = 8
        B, S = (2, 256)
        N = B * S
        CAP = 2 * N * K // E
        SCALE = 2.5

        def _route(x, router_weight, e_bias):
            logits = x.astype(jnp.float32) @ router_weight.astype(jnp.float32).T
            scores = jax.nn.sigmoid(logits)
            sc = scores + e_bias
            n = x.shape[0]
            group_scores = lax.top_k(sc.reshape(n, G, E // G), 2)[0].sum(-1)
            grp_idx = lax.top_k(group_scores, TOPK_GROUP)[1]
            group_mask = jnp.zeros((n, G), jnp.float32).at[jnp.arange(n)[:, None], grp_idx].set(1.0)
            score_mask = jnp.repeat(group_mask, E // G, axis=1)
            masked = jnp.where(score_mask > 0, sc, 0.0)
            topk_idx = lax.top_k(masked, K)[1]
            topk_w = jnp.take_along_axis(scores, topk_idx, axis=1)
            topk_w = topk_w / (topk_w.sum(-1, keepdims=True) + 1e-20)
            return (topk_idx, topk_w * SCALE)

        def _moe_experts(x, topk_idx, topk_w, w_gate, w_up, w_down):
            n = x.shape[0]
            flat_e = topk_idx.reshape(-1)
            rows = jnp.repeat(jnp.arange(n), K)
            oh = jax.nn.one_hot(flat_e, E, dtype=jnp.int32)
            pos = jnp.cumsum(oh, axis=0) - oh
            pos = jnp.take_along_axis(pos, flat_e[:, None], axis=1)[:, 0]
            valid = (pos < CAP).astype(x.dtype)
            p = jnp.minimum(pos, CAP - 1)
            buf = jnp.zeros((E, CAP, H), x.dtype).at[flat_e, p].add(x[rows] * valid[:, None])
            g = jnp.einsum('ech,ehi->eci', buf, w_gate)
            u = jnp.einsum('ech,ehi->eci', buf, w_up)
            y = jnp.einsum('eci,eih->ech', jax.nn.silu(g) * u, w_down)
            y_tok = y[flat_e, p] * (topk_w.reshape(-1) * valid)[:, None]
            return jnp.zeros((n, H), x.dtype).at[rows].add(y_tok)

        def _shared_mlp(x, sh_gate, sh_up, sh_down):
            return jax.nn.silu(x @ sh_gate) * (x @ sh_up) @ sh_down
        orig_shape = hidden_states.shape
        x = hidden_states.reshape(-1, H)
        topk_idx, topk_w = _route(x, router_weight, e_bias)
        moe_out = _moe_experts(x, topk_idx, topk_w.astype(x.dtype), w_gate, w_up, w_down)
        out = moe_out + _shared_mlp(x, sh_gate, sh_up, sh_down)
        return out.reshape(orig_shape)

    def _L1_xattn_ref(x, y, Wq, bq, Wk, bk, Wv, bv, Wkv_dca, bkv_dca, qn_w, qn_b, kn_w, kn_b, kn_dca_w, kn_dca_b, Wo, bo):
        import jax, jax.numpy as jnp
        import numpy as np
        B, S1, S2, DCA = (2, 256, 128, 16)
        QDIM, KDIM, H = (256, 128, 16)
        HD = QDIM // H
        SCALE = HD ** (-0.5)
        EPS = 1e-06
        DCA_WEIGHT = 1.0

        def _ln(t, w, b):
            m = jnp.mean(t, axis=-1, keepdims=True)
            v = jnp.var(t, axis=-1, keepdims=True)
            return (t - m) * jax.lax.rsqrt(v + EPS) * w + b

        def _attn(q, k, v):
            s = jnp.einsum('bhqd,bhkd->bhqk', q, k) * SCALE
            p = jax.nn.softmax(s, axis=-1)
            return jnp.einsum('bhqk,bhkd->bhqd', p, v)
        b, s1, _ = x.shape
        y_dca = y[:, -DCA:, :]
        y_main = y[:, :-DCA, :]
        kv_dca = (y_dca @ Wkv_dca + bkv_dca).reshape(b, DCA, 2, H, HD)
        k_dca = _ln(kv_dca[:, :, 0], kn_dca_w, kn_dca_b)
        v_dca = kv_dca[:, :, 1]
        s2 = y_main.shape[1]
        q = _ln((x @ Wq + bq).reshape(b, s1, H, HD), qn_w, qn_b)
        kv = jnp.concatenate([y_main @ Wk + bk, y_main @ Wv + bv], axis=-1)
        kv = kv.reshape(b, s2, H, 2 * HD)
        k = _ln(kv[..., :HD], kn_w, kn_b)
        v = kv[..., HD:]
        qT = q.transpose(0, 2, 1, 3)
        ctx = _attn(qT, k.transpose(0, 2, 1, 3), v.transpose(0, 2, 1, 3))
        ctx = ctx.transpose(0, 2, 1, 3).reshape(b, s1, QDIM)
        ctx_dca = _attn(qT, k_dca.transpose(0, 2, 1, 3), v_dca.transpose(0, 2, 1, 3))
        ctx_dca = ctx_dca.transpose(0, 2, 1, 3).reshape(b, s1, QDIM)
        ctx = ctx + DCA_WEIGHT * ctx_dca
        return ctx @ Wo + bo

    def _L1_ffn_ref(hidden_states, gate_weight, gate_up_weights, down_weights, shared_gate_up, shared_down):
        import jax, jax.numpy as jnp
        import numpy as np
        TOP_K = 2
        B, S, H = hidden_states.shape
        E, twoF, _ = gate_up_weights.shape
        F = twoF // 2
        T = B * S
        x = hidden_states.reshape(T, H)
        logits = x @ gate_weight.T
        scores = jax.nn.softmax(logits, axis=-1)
        topk_w, topk_idx = jax.lax.top_k(scores, TOP_K)
        combine = jnp.zeros((T, E), x.dtype).at[jnp.arange(T)[:, None], topk_idx].add(topk_w)
        gu = jnp.einsum('th,efh->tef', x, gate_up_weights)
        act = jax.nn.silu(gu[..., :F]) * gu[..., F:]
        y = jnp.einsum('tef,te,ehf->th', act, combine, down_weights)
        Fs = shared_gate_up.shape[0] // 2
        sgu = x @ shared_gate_up.T
        sact = jax.nn.silu(sgu[:, :Fs]) * sgu[:, Fs:]
        y = y + sact @ shared_down.T
        return y.reshape(B, S, H)
    x = x + jnp.tanh(g_xattn[0]) * _L0_xattn_ref(_layernorm(x, axis=-1), ctx_1024, L0_xattn_Wq, L0_xattn_Wk, L0_xattn_Wv, L0_xattn_Wo, L0_xattn_gq, L0_xattn_gk)
    x = x + jnp.tanh(g_ffn[0]) * _L0_ffn_ref(_layernorm(x, axis=-1), L0_ffn_router_weight, L0_ffn_e_bias, L0_ffn_w_gate, L0_ffn_w_up, L0_ffn_w_down, L0_ffn_sh_gate, L0_ffn_sh_up, L0_ffn_sh_down)
    x = x + jnp.tanh(g_xattn[1]) * _L1_xattn_ref(_layernorm(x, axis=-1), ctx_1024, L1_xattn_Wq, L1_xattn_bq, L1_xattn_Wk, L1_xattn_bk, L1_xattn_Wv, L1_xattn_bv, L1_xattn_Wkv_dca, L1_xattn_bkv_dca, L1_xattn_qn_w, L1_xattn_qn_b, L1_xattn_kn_w, L1_xattn_kn_b, L1_xattn_kn_dca_w, L1_xattn_kn_dca_b, L1_xattn_Wo, L1_xattn_bo)
    x = x + jnp.tanh(g_ffn[1]) * _L1_ffn_ref(_layernorm(x, axis=-1), L1_ffn_gate_weight, L1_ffn_gate_up_weights, L1_ffn_down_weights, L1_ffn_shared_gate_up, L1_ffn_shared_down)
    return x

_drawn_inputs = setup_inputs


def setup_inputs(seed=0):
    import zlib

    import numpy as np

    out = dict(_drawn_inputs(seed))
    spreads = {'g_ffn': (-1.0, 0.6),
     'L0_xattn_gq': (1.0, 0.2),
     'L0_xattn_gk': (1.0, 0.2),
     'L0_ffn_e_bias': (0.0, 0.1),
     'L1_xattn_bq': (0.0, 0.8),
     'L1_xattn_bk': (0.0, 0.435),
     'L1_xattn_bv': (0.0, 0.467),
     'L1_xattn_bkv_dca': (0.0, 0.293),
     'L1_xattn_qn_w': (1.0, 0.6),
     'L1_xattn_qn_b': (0.0, 0.8),
     'L1_xattn_kn_w': (1.0, 0.6),
     'L1_xattn_kn_b': (0.0, 0.8),
     'L1_xattn_kn_dca_w': (1.0, 0.6),
     'L1_xattn_kn_dca_b': (0.0, 0.8),
     'L1_xattn_bo': (0.0, 0.1)}
    factors = {'L1_xattn_Wq': 3.001,
     'L1_xattn_Wv': 2.709,
     'L1_ffn_gate_weight': 8.0,
     'L1_ffn_gate_up_weights': 8.0,
     'L1_ffn_down_weights': 8.0,
     'L1_ffn_shared_gate_up': 4.15,
     'L1_ffn_shared_down': 4.147}
    for name, (base, spread) in spreads.items():
        noise = np.random.default_rng([zlib.crc32(name.encode()), seed]).standard_normal(out[name].shape)
        drawn = base * np.exp(spread * noise) if base else spread * noise
        out[name] = jnp.asarray(drawn.astype(out[name].dtype))
    for name, factor in factors.items():
        out[name] = (out[name] * factor).astype(out[name].dtype)
    return out
```

```python
from contextlib import ExitStack

import concourse.bass as bass
from concourse import mybir

F32 = mybir.dt.float32
I32 = mybir.dt.int32
ACT = mybir.ActivationFunctionType
ALU = mybir.AluOpType
AX = mybir.AxisListType

P = 128
B, SQ, DIM = 8, 256, 256
SKV, CDIM = 64, 128
T = B * SQ
NT = T // P
G = 4
NG = NT // G
C = DIM // P
H0, D0 = 16, 128
E0, I0, K0 = 64, 88, 8
CAP = 128
ROW = DIM + E0
H1, D1, MAIN = 16, 16, 48
E1, F1 = 8, 176
W1 = (E1 + 2) * F1
FC = -(-W1 // P)
FAR = 1e30
EPS0 = 1e-5
EPS1 = 1e-6


class Ring:

    def __init__(self, banks, full, free):
        self.banks, self.full, self.free = banks, full, free

    def end(self):
        return RingEnd(self)


class RingEnd:

    def __init__(self, ring):
        self.ring, self.base, self.even, self.k = ring, 0, 0, 0

    def at(self, before, each=0, i=0):
        assert each % 2 == 0
        self.base, self.even, self.k = before + each * i, before % 2, 0

    def _take(self):
        pos, bank = self.base + self.k, self.ring.banks[(self.even + self.k) % len(self.ring.banks)]
        self.k += 1
        return pos, bank

    def fill(self, pe):
        pos, bank = self._take()
        if not (isinstance(pos, int) and pos < len(self.ring.banks)):
            pe.wait_ge(self.ring.free, pos - len(self.ring.banks) + 1)
        return bank

    def read(self, eng):
        pos, bank = self._take()
        eng.wait_ge(self.ring.full, pos + 1)
        return bank

    def evacuated(self, eng, back=1):
        eng.wait_ge(self.ring.free, self.base + self.k - back + 1)

    def skip(self, n):
        self.k += n


class Chain:

    def __init__(self, eng, sem):
        self.eng, self.sem, self.base, self.k = eng, sem, 0, 0

    def at(self, base):
        self.base, self.k = base, 0

    def add(self, ins):
        ins.then_inc(self.sem, 1)
        self.k += 1
        return self.k

    def wait(self, k=None):
        self.eng.wait_ge(self.sem, self.base + (self.k if k is None else k))


def flamingo(nc, a, out, stages=4):
    with ExitStack() as ctx:
        def sb(name, shape, dt=F32, scope=ctx):
            return scope.enter_context(nc.sbuf_tensor(name, shape, dt))

        def sem(name):
            return ctx.enter_context(nc.semaphore(name))

        bank = [ctx.enter_context(nc.psum_tensor(f"bank{n}", [P, 512], F32)) for n in range(8)]
        q_ring = Ring([bank[0], bank[1]], sem("q_full"), sem("q_free"))
        s_ring = Ring([bank[2], bank[3]], sem("s_full"), sem("s_free"))
        t_ring = Ring([bank[4], bank[5]], sem("t_full"), sem("t_free"))
        o_banks = [bank[6], bank[7]]
        n_bank = bank[7]

        x = sb("x", [P, NT, DIM])
        ident = sb("ident", [P, P])
        ones = sb("ones", [P, P])
        neghalf = sb("neghalf", [P, 64])
        gates = sb("gates", [P, 4])
        xn = sb("xn", [P, G, DIM])
        xnT = sb("xnT", [P, C, G * P])
        stats = sb("stats", [P, G, 6])
        mv = sb("mv", [P, G, 2])
        var = sb("var", [P, G])
        rstd = sb("rstd", [P, G])
        soft = sb("soft", [P, G, 1024])
        attnT = sb("attnT", [P, 2, 8, P])
        small = sb("small", [P, G, 2, 32])

        rwT = sb("rwT", [P, C, E0])
        e_bias = sb("e_bias", [P, E0])
        sh_gu = sb("sh_gu", [P, C, 2 * I0])
        sh_dn = sb("sh_dn", [I0, DIM])
        xw = sb("xw", [P, G, ROW])
        before = sb("before", [P, 8, 8])
        key_base = sb("key_base", [P, NT])
        keyT = sb("keyT", [P, T])
        zeros = keyT
        slots = sb("slots", [E0, CAP])
        slotsT = sb("slotsT", [P, E0])
        spare = sb("spare", [P, E0])
        src_idx = sb("src_idx", [P, E0], I32)
        dst_idx = sb("dst_idx", [P, E0], I32)
        part = [soft[:, n // 4, (n % 4) * 256:(n % 4 + 1) * 256] for n in range(16)]

        ctx_rows = sb("ctx_rows", [P, CDIM])
        ctxT = sb("ctxT", [P, 3 * SKV])

        gqk = sb("gqk", [P, 2])
        gscale = sb("gscale", [P, 1])
        first = ExitStack()
        wq = sb("wq", [P, C, H0 * D0], scope=first)
        wk = sb("wk", [P, H0 * D0], scope=first)
        wv = sb("wv", [P, H0 * D0], scope=first)
        wo = sb("wo", [P, H0, DIM], scope=first)
        
        qT = sb("qT", [P, 2, G * P], scope=first)
        q2 = sb("q2", [P, 2, G * P], scope=first)
        ksb = sb("ksb", [P, H0, D0], scope=first)
        ksq = sb("ksq", [P, H0, D0], scope=first)
        kstat = sb("kstat", [P, 2, H0], scope=first)
        kT = sb("kT", [P, H0, P], scope=first)
        vT = sb("vT", [P, H0, P], scope=first)
        vw = sb("vw", [P, 2, 2, 8, DIM], scope=first)
        qvar = sb("qvar", [P, G * H0], scope=first)
        rq = sb("rq", [P, G * H0], scope=first)


        first.close()

        y2_rows = sb("y2_rows", [P, 2, K0 * DIM])
        y2_sum = sb("y2_sum", [P, 2, DIM])
        second = ExitStack()
        w_gu = sb("w_gu", [P, 4, 2, C, 2 * I0], scope=second)
        w_dn = sb("w_dn", [I0, 4, 2, DIM], scope=second)
        xg = sb("xg", [P, 4, 2, ROW], scope=second)
        xgT = sb("xgT", [P, 2, 2, C, P], scope=second)
        act_g = sb("act_g", [I0, 2, 2 * P], scope=second)
        act_h = sb("act_h", [I0, 2, 2 * P], scope=second)
        sh_g = sb("sh_g", [I0, G * P], scope=second)
        sh_h = sb("sh_h", [I0, G * P], scope=second)
        y = sb("y", [P, 4, 2, DIM], scope=second)
        src_now = sb("src_now", [P, 4, 2], I32, scope=second)
        dst_now = sb("dst_now", [P, 4, 2], I32, scope=second)
        second.close()

        gu1 = sb("gu1", [P, C, 5, 2, 2 * F1])
        dn1 = sb("dn1", [P, FC, DIM])
        gate1 = sb("gate1", [P, C, E1])
        sg = sb("sg", [P, 2, 2 * F1])
        combine_w = sb("combine_w", [P, G, E1 + 2])
        act_v = soft[:].rearrange("p j n -> p (j n)")[:, 0:2 * FC * P].rearrange("p (b n) -> p b n", b=2)
        logits = sb("logits", [P, G * E1])
        rank_t = sb("rank_t", [P, 2, G * E1 * E1])
        gate_s = sb("gate_s", [P, 3, G * E1])

        is_main = sb("is_main", [P, 2])
        head_mask = sb("head_mask", [P, 8])
        kv_raw = sb("kv_raw", [P, 2, 2 * DIM])
        k1 = sb("k1", [P, 3, H1, D1])
        v1 = sb("v1", [P, 2, H1, D1])
        k1_stat = sb("k1_stat", [P, 2, H1])
        k1T = sb("k1T", [P, C, P])
        k_blocks = sb("k_blocks", [P, 2, C, 8, SKV])
        v_blocks = sb("v_blocks", [P, 2, 8, 2, D1])
        q1 = sb("q1", [P, G * H1, D1])
        q1_sq = sb("q1_sq", [P, G * H1, D1])
        q1_stat = sb("q1_stat", [P, 2, G * H1])
        q1T = sb("q1T", [P, C, G * P])
        c1 = sb("c1", [P, 2, DIM])
        c1T = sb("c1T", [P, 2, C, P])
        o1 = sb("o1", [P, 2, DIM])
        wq1 = sb("wq1", [P, C, DIM])
        wkv1 = sb("wkv1", [P, 2, 2 * DIM])
        wo1 = sb("wo1", [P, C, DIM])
        bq1 = sb("bq1", [P, DIM])
        bkv1 = sb("bkv1", [P, 2, 2 * DIM])
        bo1 = sb("bo1", [P, DIM])
        qn = sb("qn", [P, 2, D1])
        kn = sb("kn", [P, 2, D1])

        table = nc.dram_tensor("table", (T + 1, ROW), F32, kind="Internal").ap()
        y2 = nc.dram_tensor("y2", (K0 * T + E0 * CAP, DIM), F32, kind="Internal").ap()

        const_ready = sem("const_ready")
        ident_zero = sem("ident_zero")
        x_loaded = sem("x_loaded")
        x_rest_loaded = sem("x_rest_loaded")
        gates_loaded = sem("gates_loaded")
        gates_ready = sem("gates_ready")
        w1_loaded = sem("w1_loaded")
        gqk_loaded = sem("gqk_loaded")
        gqk_ready = sem("gqk_ready")
        ctx_loaded = sem("ctx_loaded")
        dve_chain = sem("dve_chain")
        wait_done, pe_wait_done, pool_wait_done = sem("wait_done"), sem("pe_wait_done"), sem("pool_wait_done")
        ln_var = sem("ln_var")
        ln_rstd = sem("ln_rstd")
        xn_ready = sem("xn_ready")
        k_var = sem("k_var")
        k_rstd = sem("k_rstd")
        kn_ready = sem("kn_ready")
        q2_ready = sem("q2_ready")
        q_norm = sem("q_norm")
        q_var = sem("q_var")
        q_rstd = sem("q_rstd")
        shifted = sem("shifted")
        exp_done = sem("exp_done")
        attn_ready = sem("attn_ready")
        o_full = sem("o_full")
        o_read = sem("o_read")
        x_done = sem("x_done")
        stored = sem("stored")
        done1 = {e: sem(f"done1_{e}") for e in ("pe", "act", "dve", "pool")}
        r_loaded = sem("r_loaded")
        r_const = sem("r_const")
        zero_ready = sem("zero_ready")
        zeroed = sem("zeroed")
        table_stored = sem("table_stored")
        key_ready = sem("key_ready")
        rows_ready = sem("rows_ready")
        slot_chain = sem("slot_chain")
        slots_ready = sem("slots_ready")
        idx_ready = sem("idx_ready")
        idx_now = sem("idx_now")
        w_loaded = [sem(f"w_loaded{q}") for q in range(4)]
        xg_loaded = [sem(f"xg_loaded{q}") for q in range(4)]
        y_stored = [sem(f"y_stored{q}") for q in range(4)]
        y_full = sem("y_full")
        y_ready = sem("y_ready")
        y2_loaded = [sem(f"y2_loaded{q}") for q in range(2)]
        y2_used = sem("y2_used")
        w3_loaded = sem("w3_loaded")
        w4_loaded = sem("w4_loaded")
        mask_step = sem("mask_step")
        masks_ready = sem("masks_ready")
        k1_var = sem("k1_var")
        k1_rstd = sem("k1_rstd")
        k1_ready = sem("k1_ready")
        v1_ready = sem("v1_ready")
        k_blocks_ready = sem("k_blocks_ready")
        q1_var = sem("q1_var")
        q1_rstd = sem("q1_rstd")
        q1_ready = sem("q1_ready")
        c1_full = sem("c1_full")
        c1_ready = sem("c1_ready")
        gate_shifted = sem("gate_shifted")
        gate_exp = sem("gate_exp")
        act_ready = sem("act_ready")

        x_d = a["x"].rearrange("b t d -> (b t) d").rearrange("(n p) d -> p n d", p=P)
        out_d = out.rearrange("b t d -> (b t) d").rearrange("(n p) d -> p n d", p=P)
        ctx_d = a["ctx_1024"].rearrange("b s c -> (b s) c")

        Q_PREP, Q_STEP = 8, 24
        S_PREP, S_STEP = 8, 16
        T_PREP, T_STEP = 6, 16
        Q2, S2, T2 = Q_PREP + Q_STEP * NG - 8, S_PREP + S_STEP * NG - 8, T_PREP + T_STEP * NG - 6
        QR, SR, TR = 2, 2, 4
        Q3, S3, T3 = Q2 + QR * NG, S2 + SR * NG, T2 + TR * NG + 1
        NQ = E0 // 8
        Q4, S4, T4 = Q3 + 4 * NQ, S3 + 4 * NQ, T3 + 4 * NQ
        QA, SA, TA = 6, 8, 20
        Q5, S5, T5 = Q4 + QA * NG, S4 + SA * NG, T4 + TA * NG
        QM, SM, TM = 20, 20, 20

        block = ctx.enter_context(nc.Block())

        @block.sync
        def _(sp):
            sp.dma_start(x[:, 0:G, :], x_d[:, 0:G, :]).then_inc(x_loaded, 16)
            sp.dma_start(ctx_rows[:], ctx_d[0:P, :]).then_inc(ctx_loaded, 16)
            sp.dma_start(wk[:], a["L0_xattn_Wk"]).then_inc(w1_loaded, 16)
            sp.dma_start(wv[:], a["L0_xattn_Wv"]).then_inc(w1_loaded, 16)
            sp.dma_start(wq[:], a["L0_xattn_Wq"].rearrange("(c p) n -> p c n", p=P)).then_inc(w1_loaded, 16)
            sp.dma_start(wo[:], a["L0_xattn_Wo"].rearrange("(h p) n -> p h n", p=P)).then_inc(w1_loaded, 16)
            sp.dma_start(x[:, G:NT, :], x_d[:, G:NT, :]).then_inc(x_rest_loaded, 16)
            for m in range(1, NG):
                sp.wait_ge(t_ring.full, 2 if m == 1 else T_PREP + T_STEP * (m - 2) + 4)
                sp.dma_start(ctx_rows[:], ctx_d[m * P:(m + 1) * P, :]).then_inc(ctx_loaded, 16)
            sp.wait_ge(zero_ready, 1)
            for n in range(NT):
                sp.dma_start(y2[n * P * K0:(n + 1) * P * K0, :].rearrange("(p k) d -> p (k d)", p=P),
                             zeros[:]).then_inc(zeroed, 16)
            sp.dma_start(table[T:T + 1, :], zeros[0:1, 0:ROW]).then_inc(table_stored, 16)
            table_d = table[0:T, :].rearrange("(n p) r -> p n r", p=P)
            with sp.Fori(0, NG) as i:
                sp.wait_ge(rows_ready, i + 1)
                sp.dma_start(table_d[:, bass.ds(G * i, G), :], xw[:]).then_inc(table_stored, 16)

            def load_experts(i, q):
                sp.dma_start(w_gu[:, q], gu_d[:, bass.ds(8 * i + 2 * q, 2)]).then_inc(w_loaded[q], 16)
                sp.dma_start(w_dn[:, q], dn_d[:, bass.ds(8 * i + 2 * q, 2)]).then_inc(w_loaded[q], 16)

            gu_d = a["L0_ffn_w_gu"].rearrange("e (c p) n -> p e c n", p=P)
            dn_d = a["L0_ffn_w_down"].rearrange("e p n -> p e n")
            for e in done1.values():
                sp.wait_ge(e, 1)
            for q in range(4):
                load_experts(0, q)
            for dst, src in ((wq1[:], a["L1_xattn_Wq"].rearrange("(c p) n -> p c n", p=P)),
                             (wo1[:], a["L1_xattn_Wo"].rearrange("(c p) n -> p c n", p=P)),
                             (wkv1[:, 0, 0:DIM], a["L1_xattn_Wk"]), (wkv1[:, 0, DIM:2 * DIM], a["L1_xattn_Wv"]),
                             (wkv1[:, 1, :], a["L1_xattn_Wkv_dca"]),
                             (bq1[:], a["L1_xattn_bq"].partition_broadcast(P)),
                             (bo1[:], a["L1_xattn_bo"].partition_broadcast(P)),
                             (bkv1[:, 0, 0:DIM], a["L1_xattn_bk"].partition_broadcast(P)),
                             (bkv1[:, 0, DIM:2 * DIM], a["L1_xattn_bv"].partition_broadcast(P)),
                             (bkv1[:, 1, :], a["L1_xattn_bkv_dca"].partition_broadcast(P)),
                             (qn[:, 0, :], a["L1_xattn_qn_w"].partition_broadcast(P)),
                             (qn[:, 1, :], a["L1_xattn_qn_b"].partition_broadcast(P))):
                sp.dma_start(dst, src).then_inc(w3_loaded, 16)
            for b0 in (0, SKV):
                for n, name in enumerate(("w", "b")):
                    sp.dma_start(kn[b0:b0 + MAIN, n, :], a["L1_xattn_kn_" + name].partition_broadcast(MAIN)).then_inc(
                        w3_loaded, 16)
                    sp.dma_start(kn[b0 + MAIN:b0 + SKV, n, :], a["L1_xattn_kn_dca_" + name].partition_broadcast(
                        SKV - MAIN)).then_inc(w3_loaded, 16)
            sp.dma_start(ctx_rows[:], ctx_d[0:P, :]).then_inc(ctx_loaded, 16)
            with sp.Fori(1, NQ) as i:
                for q in range(4):
                    sp.wait_ge(y_full, 4 * i + q - 3)
                    load_experts(i, q)
            for q in range(4):
                sp.wait_ge(y_stored[q], 32 * NQ)
            y2_d = y2[0:K0 * T, :].rearrange("(n p k) d -> n p (k d)", p=P, k=K0)

            def load_y2(n, q):
                sp.dma_start(y2_rows[:, q], y2_d[bass.ds(n, 1)].rearrange("n p k -> p (n k)")).then_inc(
                    y2_loaded[q], 16)

            load_y2(0, 0)
            load_y2(1, 1)
            sp.dma_start(gu1[:], a["L1_gu"].rearrange("(c p) e g n -> p c e g n", p=P)).then_inc(w4_loaded, 16)
            full = (FC - 1) * P
            sp.dma_start(dn1[:, 0:FC - 1, :], a["L1_down"][0:full, :].rearrange("(f p) n -> p f n", p=P)).then_inc(
                w4_loaded, 16)
            sp.dma_start(dn1[0:W1 - full, FC - 1, :], a["L1_down"][full:W1, :]).then_inc(w4_loaded, 16)
            sp.dma_start(gate1[:], a["L1_gateT"].rearrange("(c p) e -> p c e", p=P)).then_inc(w4_loaded, 16)
            def more_y2(i, tiles):
                for k in range(tiles):
                    sp.wait_ge(y2_used, G * i + k + 1)
                    load_y2(G * i + k + 2, k % 2)

            with sp.Fori(0, NG - 1) as i:
                more_y2(i, G)
                sp.wait_ge(t_ring.full, T4 + TA * i + 2)
                sp.dma_start(ctx_rows[:], ctx_d[bass.ds((i + 1) * P, P), :]).then_inc(ctx_loaded, 16)
            more_y2(NG - 1, G - 2)
            sp.wait_ge(x_done, 1)
            sp.dma_start(out_d, x[:]).then_inc(stored, 16)
            sp.wait_ge(stored, 16)

        @block.gpsimd
        def _(pool):
            pool.memset(ident[:], 0.0).then_inc(ident_zero, 1)
            pool.memset(neghalf[:], -0.5).then_inc(ident_zero, 1)
            pool.wait_ge(ident_zero, 2)
            pool.memset(zeros[:], 0.0).then_inc(zero_ready, 1)
            pool.memset(before[:], 1.0).then_inc(ident_zero, 1)
            pool.iota(key_base[:], pattern=[[-K0 * P * G, NG], [K0 - K0 * P, G]], base=K0 * T + 1,
                      channel_multiplier=-K0, allow_small_or_imprecise_dtypes=True).then_inc(r_const, 1)
            pool.iota(spare[:], pattern=[[CAP, E0]], base=0, channel_multiplier=1,
                      allow_small_or_imprecise_dtypes=True).then_inc(r_const, 1)
            pool.wait_ge(ident_zero, 3)
            pool.affine_select(out=before[:], in_=before[:], compare_op=ALU.is_gt, fill=0.0,
                               base=0, pattern=[[1, 8], [-1, 8]], channel_multiplier=0).then_inc(r_const, 1)
            pool.affine_select(out=ident[:], in_=ident[:], compare_op=ALU.not_equal, fill=1.0,
                               base=0, pattern=[[-1, P]], channel_multiplier=1).then_inc(const_ready, 1)

            def inverse_root(dst, src, n, wanted, done, value):
                pool.wait_ge(wanted, value)
                pool.tensor_tensor(dst, src, neghalf[:, 0:n], ALU.pow).then_inc(done, 1)

            inverse_root(rstd[:], var[:], G, ln_var, ln_rstd, 1)
            inverse_root(kstat[:, 1, :], kstat[:, 0, :], H0, k_var, k_rstd, 1)

            def step(i, last):
                if not last:
                    inverse_root(kstat[:, 1, :], kstat[:, 0, :], H0, k_var, k_rstd, i + 2)
                inverse_root(rq[:], qvar[:], G * H0, q_var, q_rstd, i + 1)
                if not last:
                    inverse_root(rstd[:], var[:], G, ln_var, ln_rstd, i + 2)

            with pool.Fori(0, NG - 1) as i:
                step(i, False)
            step(NG - 1, True)
            pool.drain().then_inc(done1["pool"], 1)

            with pool.Fori(0, NG) as i:
                inverse_root(rstd[:], var[:], G, ln_var, ln_rstd, NG + i + 1)

            def gather(i, q):
                pool.sem_inc(pool_wait_done, 1)
                for e in range(2):
                    pool.indirect_dma_start(xg[:, q, e, :], None, table, bass.IndirectOffsetOnAxis(
                        ap=src_now[:, q, e:e + 1], axis=0)).then_inc(xg_loaded[q], 16)

            def scatter(i, q):
                pool.wait_ge(y_ready, 4 * i + q + 1)
                pool.sem_inc(pool_wait_done, 1)
                for e in range(2):
                    pool.indirect_dma_start(y2, bass.IndirectOffsetOnAxis(ap=dst_now[:, q, e:e + 1], axis=0),
                                            y[:, q, e, :], None).then_inc(y_stored[q], 16)

            pool.wait_ge(table_stored, 16 * (NG + 1))
            pool.wait_ge(zeroed, 16 * NT)
            for q in range(3):
                pool.wait_ge(idx_now, q + 1)
                gather(0, q)

            def experts(i, last):
                for q in range(4):
                    if not (last and q):
                        pool.wait_ge(idx_now, 4 * i + q + 4)
                        gather(i, (q + 3) % 4)
                    scatter(i, q)

            with pool.Fori(0, NQ - 1) as i:
                experts(i, False)
            experts(NQ - 1, True)

            def attention(i):
                inverse_root(rstd[:], var[:], G, ln_var, ln_rstd, 2 * NG + i + 1)
                inverse_root(k1_stat[:, 1, :], k1_stat[:, 0, :], H1, k1_var, k1_rstd, i + 1)
                inverse_root(q1_stat[:, 1, :], q1_stat[:, 0, :], G * H1, q1_var, q1_rstd, i + 1)
                pool.wait_ge(t_ring.free, T4 + TA * i + 6)
                for b in range(2):
                    for c in range(C):
                        pool.tensor_tensor(
                            k_blocks[:, b, c], k1T[:, c, b * SKV:(b + 1) * SKV].unsqueeze(1).to_broadcast([P, 8, SKV]),
                            head_mask[:].unsqueeze(2).to_broadcast([P, 8, SKV]), ALU.mult).then_inc(k_blocks_ready, 1)

            for q in range(4):
                pool.wait_ge(y_stored[q], 32 * NQ)
            pool.memset(head_mask[:], 1.0).then_inc(mask_step, 1)
            pool.wait_ge(mask_step, 1)
            pool.affine_select(out=head_mask[:], in_=head_mask[:], compare_op=ALU.is_ge, fill=0.0, base=0,
                               pattern=[[-D1, 8]], channel_multiplier=1).then_inc(mask_step, 1)
            pool.wait_ge(mask_step, 2)
            pool.affine_select(out=head_mask[:], in_=head_mask[:], compare_op=ALU.is_ge, fill=0.0, base=D1 - 1,
                               pattern=[[D1, 8]], channel_multiplier=-1).then_inc(mask_step, 1)
            pool.wait_ge(mask_step, 3)
            with pool.Fori(0, NG) as i:
                attention(i)
            with pool.Fori(0, NG) as i:
                inverse_root(rstd[:], var[:], G, ln_var, ln_rstd, 3 * NG + i + 1)

        @block.vector
        def _(dve):
            qr = q_ring.end()
            ch = Chain(dve, dve_chain)
            dve.memset(ones[:], 1.0).then_inc(const_ready, 1)
            dve.sem_inc(o_read, 2)
            dve.wait_ge(gqk_loaded, 32)
            dve.scalar_tensor_tensor(out=gscale[:], in0=gqk[:, 0:1], scalar=float(D0) ** -0.5,
                                     in1=gqk[:, 1:2], op0=ALU.mult, op1=ALU.mult).then_inc(gqk_ready, 1)

            def layer_norm(m, eps, i=None, dst=xn):
                i = m if i is None else i
                dve.sem_inc(wait_done, 1)
                for j in range(G):
                    ch.add(dve.bn_stats(stats[:, j, :], x[:, G * i + j, :]))
                ch.wait()
                dve.sem_inc(wait_done, 1)
                for j in range(G):
                    ch.add(dve.bn_aggr(mv[:, j, :], stats[:, j, :]))
                ch.wait()
                dve.tensor_scalar(var[:], mv[:, :, 1], eps, None, ALU.add).then_inc(ln_var, 1)
                dve.wait_ge(ln_rstd, m + 1)
                for j in range(G):
                    dve.tensor_scalar(dst[:, j, 0:DIM], x[:, G * i + j, :], mv[:, j, 0:1], rstd[:, j:j + 1],
                                      ALU.subtract, ALU.mult).then_inc(xn_ready, 1)

            def kv_evacuate():
                for g in range(4):
                    dve.tensor_copy(ksb[:, 4 * g:4 * g + 4, :], qr.read(dve)[:].rearrange(
                        "p (h d) -> p h d", h=4)).then_inc(q_ring.free, 1)
                for g in range(4):
                    dve.tensor_copy(vT[:, 4 * g:4 * g + 4, :], qr.read(dve)[:].rearrange(
                        "p (h d) -> p h d", h=4)).then_inc(q_ring.free, 1)

            def k_norm(m):
                qr.evacuated(dve, 5)
                ch.add(dve.tensor_tensor(ksq[:], ksb[:], ksb[:], ALU.mult))
                ch.wait()
                ch.add(dve.tensor_reduce(kstat[:, 0, :], ksq[:], AX.X, ALU.add))
                ch.wait()
                dve.tensor_scalar(kstat[:, 0, :], kstat[:, 0, :], 1.0 / D0, EPS0, ALU.mult,
                                  ALU.add).then_inc(k_var, 1)

            def k_scale(m):
                dve.wait_ge(k_rstd, m + 1)
                dve.tensor_tensor(ksb[:], ksb[:], kstat[:, 1, :].unsqueeze(2).to_broadcast([P, H0, D0]),
                                  ALU.mult).then_inc(kn_ready, 1)

            def scores(j):
                return soft[:, j, :].rearrange("p (h k) -> p h k", h=H0)

            def over(v):
                return v.unsqueeze(2).to_broadcast([P, H0, SKV])

            def soft_front(i, j):
                s, mx = scores(j), small[:, j, 0, 0:H0]
                ch.add(dve.tensor_tensor(s, s, over(rq[:, j * H0:(j + 1) * H0]), ALU.mult))
                ch.wait()
                ch.add(dve.tensor_reduce(mx, s, AX.X, ALU.max))
                ch.wait()
                dve.tensor_tensor(s, s, over(mx), ALU.subtract).then_inc(shifted, 1)

            def soft_back(i, j):
                s, sm = scores(j), small[:, j, 1, 0:H0]
                dve.wait_ge(exp_done, G * i + j + 1)
                ch.add(dve.tensor_reduce(sm, s, AX.X, ALU.add))
                ch.wait()
                ch.add(dve.reciprocal(sm, sm))
                ch.wait()
                dve.tensor_tensor(s, s, over(sm), ALU.mult).then_inc(attn_ready, 1)

            def residual(m, j, i=None, gate=0):
                dve.wait_ge(o_full, G * m + j + 1)
                i = m if i is None else i
                xj = x[:, G * i + j, :]
                dve.scalar_tensor_tensor(out=xj, in0=o_banks[j % 2][:, 0:DIM],
                                         scalar=gates[:, gate:gate + 1], in1=xj, op0=ALU.mult,
                                         op1=ALU.add).then_inc(o_read, 1)

            LN_CHAIN, K_CHAIN, SOFT_CHAIN = 2 * G, 2, 4 * G
            PREP_CHAIN = LN_CHAIN + K_CHAIN
            STEP_CHAIN = LN_CHAIN + K_CHAIN + SOFT_CHAIN
            dve.wait_ge(x_loaded, 16)
            layer_norm(0, EPS0)
            kv_evacuate()
            k_norm(0)
            k_scale(0)
            assert ch.k == PREP_CHAIN

            def step(i, last):
                qr.at(Q_PREP, Q_STEP, i)
                ch.at(PREP_CHAIN + STEP_CHAIN * i)
                for h in range(H0):
                    dve.tensor_copy(qT[:, h % 2, :], qr.read(dve)[:]).then_inc(q_ring.free, 1)
                dve.wait_ge(q_norm, i + 1)
                dve.tensor_scalar(qvar[:], n_bank[:, 0:G * H0], 1.0 / D0, EPS0, ALU.mult,
                                  ALU.add).then_inc(q_var, 1)
                if not last:
                    kv_evacuate()
                    k_norm(i + 1)
                    k_scale(i + 1)
                dve.wait_ge(q_rstd, i + 1)
                dve.wait_ge(s_ring.free, S_PREP + S_STEP * i + 8)
                soft_front(i, 0)
                soft_front(i, 1)
                soft_back(i, 0)
                soft_front(i, 2)
                soft_back(i, 1)
                soft_front(i, 3)
                residual(i, 0)
                soft_back(i, 2)
                residual(i, 1)
                soft_back(i, 3)
                if not last:
                    dve.wait_ge(t_ring.full, T_PREP + T_STEP * i + 2)
                    layer_norm(i + 1, EPS0)
                residual(i, 2)
                residual(i, 3)
                assert last or ch.k == STEP_CHAIN

            dve.wait_ge(gates_ready, 1)
            dve.wait_ge(x_rest_loaded, 16)
            with dve.Fori(0, NG - 1) as i:
                step(i, False)
            step(NG - 1, True)
            dve.wait_ge(o_read, 2 + NT)
            dve.drain().then_inc(done1["dve"], 1)

            def tiles(v, n=E0):
                return v.rearrange("p (j e) -> p j e", j=G)

            def group_max(dst, v):
                return dve.tensor_reduce(dst, v.rearrange("p (g e) -> p g e", e=8), AX.X, ALU.max)

            def wide(v, n=8):
                return v.unsqueeze(2).to_broadcast([P, v.shape[1], n])

            def by8(v):
                return v.rearrange("p (g e) -> p g e", e=8)

            def rank_below(dst, v, count, t0, t1):
                a0 = v.unsqueeze(2).to_broadcast([P, G, 8, 8])
                a1 = v.unsqueeze(3).to_broadcast([P, G, 8, 8])
                r0, r1 = (t.rearrange("p (j g k) -> p j g k", j=G, g=8) for t in (t0, t1))
                ch.add(dve.tensor_tensor(r0, a0, a1, ALU.is_gt))
                ch.add(dve.tensor_tensor(r1, a0, a1, ALU.is_ge))
                ch.wait()
                ch.add(dve.tensor_tensor(r1, r1, before[:].unsqueeze(1).to_broadcast([P, G, 8, 8]), ALU.mult))
                ch.wait()
                ch.add(dve.tensor_tensor(t0, t0, t1, ALU.max))
                ch.wait()
                ch.add(dve.tensor_reduce(t1[:, 0:8 * G], by8(t0), AX.X, ALU.add))
                ch.wait()
                ch.add(dve.tensor_scalar(dst, t1[:, 0:8 * G], count - 0.5, None, ALU.is_lt))
                ch.wait()

            dve.wait_ge(r_const, 3)
            dve.wait_ge(r_loaded, 64)
            dve.wait_ge(zeroed, 16 * NT)
            for e in done1.values():
                dve.wait_ge(e, 1)
            ROUTE_CHAIN = LN_CHAIN + 24 + 2 * G
            ROUTE_BASE = PREP_CHAIN + STEP_CHAIN * (NG - 1) + SOFT_CHAIN

            def route(i):
                ch.at(ROUTE_BASE + ROUTE_CHAIN * i)
                qr.at(Q2, QR, i)
                dve.wait_ge(table_stored, 16 * (i + 1))
                layer_norm(NG + i, EPS0, i, xw)
                sig, sc, eq, oth, msk, rep, t0, t1, sel, key = part[0:10]
                m = part[10]
                m1, cnt, m2, dup, gs, gm = (m[:, 32 * n:32 * n + 32] for n in range(6))
                top, sums = part[11][:, 0:32], part[11][:, 32:32 + G]
                dve.wait_ge(t_ring.free, T2 + TR * i + 3)
                ch.add(dve.tensor_tensor(tiles(sc), tiles(sig), e_bias[:].unsqueeze(1).to_broadcast([P, G, E0]),
                                         ALU.add))
                ch.wait()
                ch.add(group_max(m1, sc))
                ch.wait()
                ch.add(dve.tensor_tensor(by8(eq), by8(sc), wide(m1), ALU.is_equal))
                ch.wait()
                ch.add(dve.tensor_reduce(cnt, by8(eq), AX.X, ALU.add))
                ch.add(dve.scalar_tensor_tensor(out=oth, in0=eq, scalar=-FAR, in1=sc, op0=ALU.mult, op1=ALU.add))
                ch.wait()
                ch.add(group_max(m2, oth))
                ch.add(dve.tensor_scalar(dup, cnt, 1.5, 1.0, ALU.is_ge, ALU.subtract))
                ch.wait()
                ch.add(dve.scalar_tensor_tensor(out=dup, in0=dup, scalar=FAR, in1=m1, op0=ALU.mult, op1=ALU.add))
                ch.wait()
                ch.add(dve.tensor_tensor(m2, m2, dup, ALU.max))
                ch.wait()
                ch.add(dve.tensor_tensor(gs, m1, m2, ALU.add))
                ch.wait()
                rank_below(gm, gs.rearrange("p (j g) -> p j g", j=G), 4, t0, t1)
                ch.add(dve.tensor_tensor(by8(msk), by8(sc), wide(gm), ALU.mult))
                ch.wait()
                dve.sem_inc(wait_done, 1)
                for j in range(G):
                    ch.add(dve.max(top[:, 8 * j:8 * j + 8], tiles(msk)[:, j, :]))
                ch.wait()
                dve.sem_inc(wait_done, 1)
                for j in range(G):
                    ch.add(dve.match_replace(tiles(rep)[:, j, :], top[:, 8 * j:8 * j + 8], tiles(msk)[:, j, :],
                                             -FAR))
                ch.wait()
                ch.add(dve.tensor_tensor(sel, rep, msk, ALU.not_equal))
                ch.wait()
                ch.add(dve.tensor_tensor(t0, sel, sig, ALU.mult))
                ch.add(dve.tensor_tensor_scan(t1, sel, none[:], 0.0, ALU.add, ALU.add))
                ch.wait()
                ch.add(dve.tensor_reduce(sums, tiles(t0), AX.X, ALU.add))
                ch.add(dve.scalar_tensor_tensor(
                    out=tiles(t1), in0=tiles(t1), scalar=-1.0,
                    in1=key_base[:, bass.ds(G * i, G)].unsqueeze(2).to_broadcast([P, G, E0]),
                    op0=ALU.mult, op1=ALU.add))
                ch.wait()
                dve.tensor_tensor(key, t1, sel, ALU.mult).then_inc(key_ready, 1)
                ch.add(dve.tensor_scalar(sums, sums, 1e-20, None, ALU.add))
                ch.wait()
                ch.add(dve.reciprocal(sums, sums))
                ch.wait()
                dve.scalar_tensor_tensor(out=xw[:, :, DIM:ROW], in0=tiles(t0), scalar=2.5,
                                         in1=sums.unsqueeze(2).to_broadcast([P, G, E0]), op0=ALU.mult,
                                         op1=ALU.mult).then_inc(rows_ready, 1)
                for half in range(2):
                    dve.wait_ge(s_ring.free, S2 + SR * i + half + 1)
                    h = slice(half * 2 * P, (half + 1) * 2 * P)
                    dve.tensor_tensor(sh_h[:, h], sh_g[:, h], qr.read(dve)[0:I0, 0:2 * P],
                                      ALU.mult).then_inc(q_ring.free, 1)
                for j in range(G):
                    residual(NG + i, j, i, 2)
                assert ch.k == ROUTE_CHAIN

            ch.at(ROUTE_BASE)
            none = part[12]
            ch.add(dve.memset(none, 0.0))
            ch.wait()
            ROUTE_BASE += 1
            with dve.Fori(0, NG) as i:
                route(i)

            sl = Chain(dve, slot_chain)
            dve.wait_ge(t_ring.free, T2 + TR * NG)
            for r in range(CAP // 8):
                sl.add(dve.max(slots[:, 8 * r:8 * r + 8], keyT[0:E0, :]))
                sl.wait()
                if r < CAP // 8 - 1:
                    sl.add(dve.match_replace(keyT[0:E0, :], slots[:, 8 * r:8 * r + 8], keyT[0:E0, :], 0.0))
                    sl.wait()
            dve.drain().then_inc(slots_ready, 1)
            dve.wait_ge(t_ring.free, T3)
            sl.add(dve.tensor_scalar(part[0][:, 0:E0], slotsT[:], -1.0, float(K0 * T), ALU.mult, ALU.add))
            sl.add(dve.tensor_scalar(part[1][:, 0:E0], slotsT[:], 0.0, None, ALU.is_equal))
            sl.wait()
            sl.add(dve.tensor_copy(src_idx[:], part[0][:, 0:E0]))
            sl.add(dve.tensor_tensor(part[1][:, 0:E0], part[1][:, 0:E0], spare[:], ALU.mult))
            sl.wait()
            sl.add(dve.tensor_tensor(dst_idx[:], part[0][:, 0:E0], part[1][:, 0:E0], ALU.add))
            sl.add(dve.tensor_scalar(src_idx[:], src_idx[:], 3, None, ALU.logical_shift_right))
            sl.wait()

            def stage_source(i, q):
                dve.tensor_copy(src_now[:, q, :], src_idx[:, bass.ds(8 * i + 2 * q, 2)]).then_inc(idx_now, 1)

            for q in range(3):
                stage_source(0, q)

            def experts(i, last):
                qr.at(Q3, 4, i)
                for q in range(4):
                    if not (last and q):
                        stage_source(i + (q + 3) // 4, (q + 3) % 4)
                    dve.wait_ge(s_ring.free, S3 + 4 * i + q + 1)
                    b = qr.read(dve)
                    dve.tensor_tensor(act_h[:, q % 2, :], act_g[:, q % 2, :], b[0:I0, 0:2 * P],
                                      ALU.mult).then_inc(q_ring.free, 1)
                    if i is not first_step:
                        dve.wait_ge(y_stored[q], 32 * i)
                    dve.tensor_copy(dst_now[:, q, :], dst_idx[:, bass.ds(8 * i + 2 * q, 2)]).then_inc(idx_ready, 1)
                    dve.wait_ge(y_full, 4 * i + q + 1)
                    for e in range(2):
                        dve.tensor_scalar(y[:, q, e, :], o_banks[q % 2][:, e * DIM:(e + 1) * DIM],
                                          xg[:, q, e, bass.ds(DIM + 8 * i + 2 * q + e, 1)], None,
                                          ALU.mult).then_inc(y_ready if e else idx_ready, 1)

            first_step = 0
            experts(0, False)
            with dve.Fori(1, NQ - 1) as i:
                experts(i, False)
            experts(NQ - 1, True)

            def combine(i):
                for j in range(G):
                    dve.wait_ge(y2_loaded[j % 2], 16 * (2 * i + j // 2 + 1))
                    s_ = y2_sum[:, j % 2, :]
                    ch.add(dve.tensor_reduce(s_, y2_rows[:, j % 2].rearrange("p (k d) -> p d k", k=K0), AX.X,
                                             ALU.add))
                    ch.wait()
                    xj = x[:, G * i + j, :]
                    dve.scalar_tensor_tensor(out=xj, in0=s_, scalar=gates[:, 2:3], in1=xj, op0=ALU.mult,
                                             op1=ALU.add).then_inc(y2_used, 1)
                dve.wait_ge(y2_used, G * (i + 1))

            def norm_of(v, sq, stat, wanted):
                n = v.shape[1]
                wide_stat = stat[:, 0, :].unsqueeze(2).to_broadcast([P, n, D1])
                ch.add(dve.tensor_reduce(stat[:, 0, :], v, AX.X, ALU.add))
                ch.wait()
                ch.add(dve.scalar_tensor_tensor(out=v, in0=wide_stat, scalar=-1.0 / D1, in1=v, op0=ALU.mult,
                                                op1=ALU.add))
                ch.wait()
                ch.add(dve.tensor_tensor(sq, v, v, ALU.mult))
                ch.wait()
                ch.add(dve.tensor_reduce(stat[:, 0, :], sq, AX.X, ALU.add))
                ch.wait()
                dve.tensor_scalar(stat[:, 0, :], stat[:, 0, :], 1.0 / D1, EPS1, ALU.mult,
                                  ALU.add).then_inc(wanted, 1)

            def affine_of(v, stat, weights, ready):
                n = v.shape[1]
                ch.add(dve.tensor_tensor(v, v, stat[:, 1, :].unsqueeze(2).to_broadcast([P, n, D1]), ALU.mult))
                ch.wait()
                ch.add(dve.tensor_tensor(v, v, weights[:, 0, :].unsqueeze(1).to_broadcast([P, n, D1]), ALU.mult))
                ch.wait()
                dve.tensor_tensor(v, v, weights[:, 1, :].unsqueeze(1).to_broadcast([P, n, D1]),
                                  ALU.add).then_inc(ready, 1)

            SPANS = ((0, MAIN), (MAIN, SKV))

            def kv_attention(i):
                for swapped in range(2):
                    for n in range(2):
                        dve.tensor_tensor(kv_raw[:, n, :], qr.read(dve)[:], bkv1[:, n, :],
                                          ALU.add).then_inc(q_ring.free, 1)
                    qr.evacuated(dve)
                    main = kv_raw[:, 0, :].rearrange("p (h s d) -> p h s d", h=H1, s=2)
                    last = kv_raw[:, 1, :].rearrange("p (s h d) -> p h s d", h=H1, s=2)
                    parts = ((v1[:, swapped], 1),) if swapped else ((k1[:, 0], 0), (v1[:, 0], 1))
                    for dst, s_ in parts:
                        ch.add(dve.tensor_scalar(k1[:, 1 + s_], main[:, :, s_, :], is_main[:, 0:1], None, ALU.mult))
                    ch.wait()
                    for dst, s_ in parts:
                        ch.add(dve.scalar_tensor_tensor(out=dst, in0=last[:, :, s_, :], scalar=is_main[:, 1:2],
                                                        in1=k1[:, 1 + s_], op0=ALU.mult, op1=ALU.add))
                    ch.wait()
                    if not swapped:
                        norm_of(k1[:, 0], k1[:, 1], k1_stat, k1_var)
                for b in range(2):
                    for o in range(2):
                        rows = slice(o * SKV, (o + 1) * SKV)
                        v_ = v1[rows, b ^ o].rearrange("p (q o) d -> p q o d", o=2)[:, :, o, :]
                        dve.tensor_copy(v_blocks[rows, b, :, o, :], v_).then_inc(v1_ready, 1)
                dve.wait_ge(k1_rstd, i + 1)
                affine_of(k1[:, 0], k1_stat, kn, k1_ready)

            def soft_spans(j):
                s_ = soft[:, j, :].rearrange("p (h k) -> p h k", h=H1)
                return [(s_[:, :, lo:hi], hi - lo, slice(n * H1, (n + 1) * H1)) for n, (lo, hi) in enumerate(SPANS)]

            def soft2_front(i, j):
                for v, n, at in soft_spans(j):
                    ch.add(dve.tensor_reduce(small[:, j, 0, at], v, AX.X, ALU.max))
                ch.wait()
                for v, n, at in soft_spans(j):
                    mx = small[:, j, 0, at].unsqueeze(2).to_broadcast([P, H1, n])
                    dve.tensor_tensor(v, v, mx, ALU.subtract).then_inc(shifted, 1)

            def soft2_back(i, j):
                dve.wait_ge(exp_done, NT + G * i + j + 1)
                for v, n, at in soft_spans(j):
                    ch.add(dve.tensor_reduce(small[:, j, 1, at], v, AX.X, ALU.add))
                ch.wait()
                ch.add(dve.reciprocal(small[:, j, 1, :], small[:, j, 1, :]))
                ch.wait()
                for v, n, at in soft_spans(j):
                    sm = small[:, j, 1, at].unsqueeze(2).to_broadcast([P, H1, n])
                    dve.tensor_tensor(v, v, sm, ALU.mult).then_inc(attn_ready, 1)

            def context_out(i, j):
                dve.wait_ge(c1_full, G * i + j + 1)
                dve.tensor_copy(c1[:, j % 2, :], o_banks[j % 2][:, 0:DIM]).then_inc(c1_ready, 1)

            def attention_out(i, j):
                dve.wait_ge(o_full, G * (2 * NG + i) + j + 1)
                ch.add(dve.tensor_tensor(o1[:, j % 2, :], o_banks[j % 2][:, DIM:2 * DIM], bo1[:], ALU.add))
                ch.wait()
                xj = x[:, G * i + j, :]
                dve.scalar_tensor_tensor(out=xj, in0=o1[:, j % 2, :], scalar=gates[:, 1:2], in1=xj,
                                         op0=ALU.mult, op1=ALU.add).then_inc(o_read, 1)

            def attention(i):
                ch.at(ATT_BASE + ATT_CHAIN * i)
                qr.at(Q4, QA, i)
                combine(i)
                layer_norm(2 * NG + i, EPS0, i)
                kv_attention(i)
                for half in range(2):
                    dve.tensor_tensor(
                        q1[:, 2 * half * H1:2 * (half + 1) * H1, :].rearrange("p (j h) d -> p j (h d)", j=2),
                        qr.read(dve)[:].rearrange("p (j n) -> p j n", j=2),
                        bq1[:].unsqueeze(1).to_broadcast([P, 2, DIM]), ALU.add).then_inc(q_ring.free, 1)
                qr.evacuated(dve)
                norm_of(q1[:], q1_sq[:], q1_stat, q1_var)
                dve.wait_ge(q1_rstd, i + 1)
                affine_of(q1[:], q1_stat, qn, q1_ready)
                for j in range(G):
                    dve.wait_ge(s_ring.free, S4 + SA * i + 2 * j + 2)
                    soft2_front(i, j)
                    if j:
                        soft2_back(i, j - 1)
                    if j == 2:
                        context_out(i, 0)
                    if j == 3:
                        context_out(i, 1)
                soft2_back(i, G - 1)
                attention_out(i, 0)
                context_out(i, 2)
                attention_out(i, 1)
                context_out(i, 3)
                attention_out(i, 2)
                attention_out(i, 3)
                assert ch.k == ATT_CHAIN, ch.k

            ATT_BASE = ROUTE_BASE + ROUTE_CHAIN * NG + 4
            ATT_CHAIN = 54
            ch.at(ATT_BASE - 4)
            for q in range(4):
                dve.wait_ge(y_stored[q], 32 * NQ)
            dve.wait_ge(w3_loaded, 16 * 20)
            ch.add(dve.tensor_scalar(is_main[:, 0:1], spare[:, 0:1], float(SKV), float(SKV), ALU.is_ge, ALU.mult))
            ch.add(dve.memset(v_blocks[:], 0.0))
            ch.wait()
            ch.add(dve.tensor_tensor(is_main[:, 1:2], spare[:, 0:1], is_main[:, 0:1], ALU.subtract))
            ch.wait()
            ch.add(dve.tensor_scalar(is_main[:, 0:1], is_main[:, 1:2], float(MAIN), None, ALU.is_lt))
            dve.wait_ge(slot_chain, 1)
            dve.tensor_scalar(is_main[:, 1:2], is_main[:, 1:2], float(MAIN), None, ALU.is_ge).then_inc(masks_ready, 1)
            ch.wait()
            dve.wait_ge(masks_ready, 1)
            with dve.Fori(0, NG) as i:
                attention(i)

            def gating(i):
                t0, t1 = rank_t[:, 0, :], rank_t[:, 1, :]
                lg, mx, sm = gate_s[:, 0, :], gate_s[:, 1, 0:G], gate_s[:, 2, 0:G]

                def wide_(v):
                    return v.unsqueeze(2).to_broadcast([P, G, E1])

                dve.wait_ge(t_ring.free, T5 + TM * i + 4)
                ch.add(dve.tensor_reduce(mx, by8(logits[:]), AX.X, ALU.max))
                ch.wait()
                dve.tensor_tensor(by8(lg), by8(logits[:]), wide_(mx), ALU.subtract).then_inc(gate_shifted, 1)
                dve.wait_ge(gate_exp, i + 1)
                ch.add(dve.tensor_reduce(sm, by8(lg), AX.X, ALU.add))
                ch.wait()
                ch.add(dve.reciprocal(sm, sm))
                ch.wait()
                ch.add(dve.tensor_tensor(by8(lg), by8(lg), wide_(sm), ALU.mult))
                ch.wait()
                rank_below(gate_s[:, 1, :], by8(lg), 2, t0, t1)
                ch.add(dve.tensor_tensor(combine_w[:, :, 0:E1], by8(lg), by8(gate_s[:, 1, :]), ALU.mult))
                ch.wait()

            def products(i, j):
                for p in range(5):
                    dve.wait_ge(s_ring.free, S5 + SM * i + 5 * j + p + 1)
                    b = qr.read(dve)
                    for e in range(2):
                        at = (2 * p + e) * F1
                        ins = dve.scalar_tensor_tensor(
                            out=act_v[:, j % 2, at:at + F1], in0=sg[:, (j + p) % 2, e * F1:(e + 1) * F1],
                            scalar=combine_w[:, j, 2 * p + e:2 * p + e + 1], in1=b[:, e * F1:(e + 1) * F1],
                            op0=ALU.mult, op1=ALU.mult)
                    ins.then_inc(q_ring.free, 1)

            def mixture(i, last):
                ch.at(MIX_BASE + MIX_CHAIN * i)
                qr.at(Q5, QM, i)
                gating(i)
                products(i, 0)
                products(i, 1)
                for j in range(G):
                    if j == 2 and not last:
                        dve.wait_ge(t_ring.full, T5 + TM * i + 2)
                        layer_norm(3 * NG + i + 1, EPS0, i + 1)
                    residual(3 * NG + i, j, i, 3)
                    if j + 2 < G:
                        products(i, j + 2)
                assert last or ch.k == MIX_CHAIN, ch.k

            MIX_BASE = ATT_BASE + ATT_CHAIN * NG + LN_CHAIN + 1
            MIX_CHAIN = 5 + 6 + LN_CHAIN
            ch.at(MIX_BASE - LN_CHAIN - 1)
            ch.add(dve.memset(combine_w[:, :, E1:E1 + 2], 1.0))
            ch.wait()
            dve.wait_ge(o_read, 2 + 3 * NT)
            layer_norm(3 * NG, EPS0, 0)
            with dve.Fori(0, NG - 1) as i:
                mixture(i, False)
            mixture(NG - 1, True)
            dve.drain().then_inc(x_done, 1)

        @block.scalar
        def _(act):
            sr, tr, qr = s_ring.end(), t_ring.end(), q_ring.end()
            act.dma_start(gates[:, 0:2], a["g_xattn"].partition_broadcast(P)).then_inc(gates_loaded, 16)
            act.dma_start(gates[:, 2:4], a["g_ffn"].partition_broadcast(P)).then_inc(gates_loaded, 16)
            act.dma_start(gqk[:, 0:1], a["L0_xattn_gq"].unsqueeze(1)).then_inc(gqk_loaded, 16)
            act.dma_start(gqk[:, 1:2], a["L0_xattn_gk"].unsqueeze(1)).then_inc(gqk_loaded, 16)
            act.dma_start(rwT[:], a["L0_ffn_router_weightT"].rearrange("(c p) e -> p c e", p=P)).then_inc(r_loaded, 16)
            act.dma_start(e_bias[:], a["L0_ffn_e_bias"].partition_broadcast(P)).then_inc(r_loaded, 16)
            act.dma_start(sh_gu[:], a["L0_ffn_sh_gu"].rearrange("(c p) e -> p c e", p=P)).then_inc(r_loaded, 16)
            act.dma_start(sh_dn[:], a["L0_ffn_sh_down"]).then_inc(r_loaded, 16)
            act.wait_ge(gates_loaded, 32)
            act.activation(gates[:], gates[:], ACT.Tanh).then_inc(gates_ready, 1)
            act.wait_ge(gqk_ready, 1)

            def kv_evacuate(m):
                act.activation(ctxT[:, 0:P], tr.read(act)[:, 0:P], ACT.Copy).then_inc(t_ring.free, 1)
                act.activation(ctxT[:, P:P + SKV], tr.read(act)[:, 0:SKV], ACT.Copy).then_inc(t_ring.free, 1)
                for p in range(8):
                    b = sr.read(act)
                    w = vw[:, m % 2]
                    lo = w[0:SKV, :, p, :]
                    act.activation(lo, b[0:SKV, :].rearrange("p (b n) -> p b n", b=2), ACT.Copy)
                    act.activation(w[SKV:P, 0, p, :], b[SKV:P, DIM:2 * DIM], ACT.Copy)
                    act.activation(w[SKV:P, 1, p, :], b[SKV:P, 0:DIM], ACT.Copy).then_inc(s_ring.free, 1)
                for g in range(4):
                    act.activation(kT[:, 4 * g:4 * g + 4, :], tr.read(act)[:].rearrange(
                        "p (h k) -> p h k", h=4), ACT.Copy, scale=gscale[:]).then_inc(t_ring.free, 1)

            kv_evacuate(0)

            def step(i, last):
                qr.at(Q_PREP, Q_STEP, i)
                sr.at(S_PREP, S_STEP, i)
                tr.at(T_PREP, T_STEP, i)
                for c in range(C):
                    act.activation(xnT[:, c, :], tr.read(act)[:], ACT.Copy).then_inc(t_ring.free, 1)

                def scores_out(pair):
                    b = sr.read(act)
                    act.activation(soft[:, :, 2 * pair * SKV:2 * (pair + 1) * SKV],
                                   b[:].rearrange("p (j n) -> p j n", j=G), ACT.Copy).then_inc(s_ring.free, 1)

                for h in range(H0):
                    qr.skip(1)
                    qr.evacuated(act)
                    act.activation(q2[:, h % 2, :], qT[:, h % 2, :], ACT.Square).then_inc(q2_ready, 1)
                    if h >= 2 and h % 2 == 0:
                        scores_out(h // 2 - 1)
                scores_out(H0 // 2 - 1)
                if not last:
                    kv_evacuate(i + 1)

                def exponential(j):
                    act.wait_ge(shifted, G * i + j + 1)
                    act.activation(soft[:, j, :], soft[:, j, :], ACT.Exp).then_inc(exp_done, 1)

                def attn_out(j):
                    for g in range(2):
                        act.activation(attnT[:, j % 2, 4 * g:4 * g + 4, :], tr.read(act)[:].rearrange(
                            "p (h t) -> p h t", h=4), ACT.Copy).then_inc(t_ring.free, 1)

                exponential(0)
                exponential(1)
                if last:
                    tr.at(T_PREP + 2, T_STEP, i)
                for j in range(G):
                    attn_out(j)
                    if j + 2 < G:
                        exponential(j + 2)

            with act.Fori(0, NG - 1) as i:
                step(i, False)
            step(NG - 1, True)
            act.drain().then_inc(done1["act"], 1)
            for e in done1.values():
                act.wait_ge(e, 1)

            def route(i):
                sr.at(S2, SR, i)
                tr.at(T2, TR, i)
                for c in range(C):
                    act.activation(xnT[:, c, :], tr.read(act)[:], ACT.Copy).then_inc(t_ring.free, 1)
                act.activation(part[0], tr.read(act)[:, 0:G * E0], ACT.Sigmoid).then_inc(t_ring.free, 1)
                for half in range(2):
                    act.activation(sh_g[:, half * 2 * P:(half + 1) * 2 * P], sr.read(act)[0:I0, 0:2 * P],
                                   ACT.Silu).then_inc(s_ring.free, 1)
                act.activation(keyT[0:E0, bass.ds(G * P * i, G * P)], tr.read(act)[0:E0, :],
                               ACT.Copy).then_inc(t_ring.free, 1)

            with act.Fori(0, NG) as i:
                route(i)
            tr.at(T2 + TR * NG)
            act.activation(slotsT[:], tr.read(act)[:, 0:E0], ACT.Copy).then_inc(t_ring.free, 1)

            def transposed(q):
                act.activation(xgT[:, q % 2], tr.read(act)[:].rearrange(
                    "p (e c t) -> p e c t", e=2, c=C), ACT.Copy).then_inc(t_ring.free, 1)

            def experts(i, last):
                tr.at(T3 + 1, 4, i)
                sr.at(S3, 4, i)
                for q in range(4):
                    act.activation(act_g[:, q % 2, :], sr.read(act)[0:I0, 0:2 * P],
                                   ACT.Silu).then_inc(s_ring.free, 1)
                    if not (last and q == 3):
                        transposed(q + 1)

            tr.at(T3)
            transposed(0)
            with act.Fori(0, NQ - 1) as i:
                experts(i, False)
            experts(NQ - 1, True)

            def attention(i):
                sr.at(S4, SA, i)
                tr.at(T4, TA, i)
                act.activation(ctxT[:, 0:P], tr.read(act)[:, 0:P], ACT.Copy).then_inc(t_ring.free, 1)
                act.activation(ctxT[:, P:P + SKV], tr.read(act)[:, 0:SKV], ACT.Copy).then_inc(t_ring.free, 1)
                for c in range(C):
                    act.activation(xnT[:, c, :], tr.read(act)[:], ACT.Copy).then_inc(t_ring.free, 1)
                for c in range(C):
                    act.activation(k1T[:, c, :], tr.read(act)[:, 0:P], ACT.Copy).then_inc(t_ring.free, 1)
                for c in range(C):
                    act.activation(q1T[:, c, :], tr.read(act)[:], ACT.Copy).then_inc(t_ring.free, 1)
                for j in range(G):
                    for c in range(C):
                        act.activation(soft[:, j, c * 512:(c + 1) * 512], sr.read(act)[:], ACT.Copy,
                                       scale=float(D1) ** -0.5).then_inc(s_ring.free, 1)

                def exponential(j):
                    act.wait_ge(shifted, NT + 2 * (G * i + j) + 2)
                    act.activation(soft[:, j, :], soft[:, j, :], ACT.Exp).then_inc(exp_done, 1)

                def attn_out(j):
                    for g in range(2):
                        act.activation(attnT[:, j % 2, 4 * g:4 * g + 4, :], tr.read(act)[:].rearrange(
                            "p (h t) -> p h t", h=4), ACT.Copy).then_inc(t_ring.free, 1)

                def context_out(j):
                    act.activation(c1T[:, j % 2], tr.read(act)[:, 0:DIM].rearrange("p (c t) -> p c t", c=C),
                                   ACT.Copy).then_inc(t_ring.free, 1)

                exponential(0)
                exponential(1)
                attn_out(0)
                exponential(2)
                attn_out(1)
                exponential(3)
                attn_out(2)
                context_out(0)
                attn_out(3)
                context_out(1)
                context_out(2)
                context_out(3)

            with act.Fori(0, NG) as i:
                attention(i)

            def mixture(i):
                sr.at(S5, SM, i)
                tr.at(T5, TM, i)
                for c in range(C):
                    act.activation(xnT[:, c, :], tr.read(act)[:], ACT.Copy).then_inc(t_ring.free, 1)
                for half in range(2):
                    act.activation(logits[:, half * 2 * E1:(half + 1) * 2 * E1], tr.read(act)[:, 0:2 * E1],
                                   ACT.Copy).then_inc(t_ring.free, 1)
                act.wait_ge(gate_shifted, i + 1)
                act.activation(gate_s[:, 0, :], gate_s[:, 0, :], ACT.Exp).then_inc(gate_exp, 1)

                def silu(j):
                    for p in range(5):
                        b = sr.read(act)
                        act.wait_ge(q_ring.free, Q5 + QM * i + 5 * j + p - 1)
                        act.activation(sg[:, (j + p) % 2, :], b[:, 0:2 * F1], ACT.Silu).then_inc(s_ring.free, 1)

                def act_out(j):
                    for g in range(4):
                        n = min(4, FC - 4 * g)
                        act.activation(attn_flat[:, 4 * g:4 * g + n, :], tr.read(act)[:, 0:n * P].rearrange(
                            "p (f t) -> p f t", f=n), ACT.Copy).then_inc(t_ring.free, 1)

                silu(0)
                silu(1)
                for j in range(G):
                    act_out(j)
                    if j + 2 < G:
                        silu(j + 2)

            attn_flat = attnT[:].rearrange("p b f t -> p (b f) t")
            with act.Fori(0, NG) as i:
                mixture(i)

        @block.tensor
        def _(pe):
            qr, sr, tr = q_ring.end(), s_ring.end(), t_ring.end()

            def kv_prepare(m):
                pe.wait_ge(ctx_loaded, 16 * (m + 1))
                for _ in range(2):
                    pe.transpose(tr.fill(pe)[:, 0:P], ctx_rows[:], ident[:]).then_inc(t_ring.full, 1)
                tr.evacuated(pe)
                for g in range(4):
                    pe.matmul(qr.fill(pe)[:], ctxT[:, 0:P], wk[:, 512 * g:512 * (g + 1)],
                              start=True, stop=True).then_inc(q_ring.full, 1)
                for g in range(4):
                    b = qr.fill(pe)
                    for k in range(4):
                        h = 4 * g + k
                        first = SKV * (h % 2)
                        mm = pe.matmul(b[:, k * P:(k + 1) * P], wv[:, h * D0:(h + 1) * D0],
                                       ctxT[:, first:first + P], start=True, stop=True)
                    mm.then_inc(q_ring.full, 1)
                for p in range(8):
                    if p % 2 == 0:
                        qr.evacuated(pe, 4 - p // 2)
                    b = sr.fill(pe)
                    for o in range(2):
                        mm = pe.matmul(b[:, o * DIM:(o + 1) * DIM], vT[:, 2 * p + o, :], wo[:, 2 * p + o, :],
                                       start=True, stop=True)
                    mm.then_inc(s_ring.full, 1)
                pe.wait_ge(kn_ready, m + 1)
                for g in range(4):
                    b = tr.fill(pe)
                    for k in range(4):
                        mm = pe.transpose(b[:, k * P:(k + 1) * P], ksb[:, 4 * g + k, :], ident[:])
                    mm.then_inc(t_ring.full, 1)

            pe.wait_ge(const_ready, 2)
            pe.wait_ge(w1_loaded, 64)
            kv_prepare(0)

            def transpose_xn(m, src=xn):
                pe.wait_ge(xn_ready, G * (m + 1))
                for c in range(C):
                    b = tr.fill(pe)
                    for j in range(G):
                        mm = pe.transpose(b[:, j * P:(j + 1) * P], src[:, j, c * P:(c + 1) * P], ident[:])
                    mm.then_inc(t_ring.full, 1)
                tr.evacuated(pe)

            def step(i, last):
                qr.at(Q_PREP, Q_STEP, i)
                sr.at(S_PREP, S_STEP, i)
                tr.at(T_PREP, T_STEP, i)
                transpose_xn(i)
                pe.wait_ge(o_read, G * i + 2)
                s_bank = [None]

                def scores(h):
                    qr.evacuated(pe, 1 if h == H0 - 1 else 2)
                    pe.wait_ge(q2_ready, H0 * i + h + 1)
                    place = [(h ^ 1) if j >= 2 else h for j in range(G)]
                    for j in range(G):
                        mm = pe.matmul(n_bank[:, j * H0 + place[j]:j * H0 + place[j] + 1],
                                       q2[:, h % 2, j * P:(j + 1) * P], ones[:, 0:1], start=True, stop=True)
                    if h == H0 - 1:
                        mm.then_inc(q_norm, 1)
                    if h % 2 == 0:
                        s_bank[0] = sr.fill(pe)
                    for j in range(G):
                        at = (2 * j + place[j] % 2) * SKV
                        mm = pe.matmul(s_bank[0][:, at:at + SKV], qT[:, h % 2, j * P:(j + 1) * P],
                                       kT[:, h, (j // 2) * SKV:(j // 2 + 1) * SKV], start=True, stop=True)
                    if h % 2:
                        mm.then_inc(s_ring.full, 1)

                for h in range(H0):
                    b = qr.fill(pe)
                    for c in range(C):
                        mm = pe.matmul(b[:], wq[:, c, h * D0:(h + 1) * D0], xnT[:, c, :],
                                       start=(c == 0), stop=(c == C - 1))
                    mm.then_inc(q_ring.full, 1)
                    if h >= 1:
                        scores(h - 1)
                scores(H0 - 1)
                if not last:
                    kv_prepare(i + 1)

                def transpose_attn(j):
                    pe.wait_ge(attn_ready, G * i + j + 1)
                    for g in range(2):
                        b = tr.fill(pe)
                        for k in range(4):
                            at = (4 * g + k) * P
                            mm = pe.transpose(b[:, k * P:(k + 1) * P], soft[:, j, at:at + P], ident[:])
                        mm.then_inc(t_ring.full, 1)

                def output(j, back):
                    tr.evacuated(pe, back)
                    pe.wait_ge(o_read, G * i + j + 1)
                    for p in range(8):
                        mm = pe.matmul(o_banks[j % 2][:, 0:DIM], attnT[:, j % 2, p, :],
                                       vw[:, i % 2, j // 2, p, :], start=(p == 0), stop=(p == 7))
                    mm.then_inc(o_full, 1)

                transpose_attn(0)
                for j in range(G):
                    if j + 1 < G:
                        transpose_attn(j + 1)
                    output(j, 3 if j + 1 < G else 1)

            with pe.Fori(0, NG - 1) as i:
                step(i, False)
            step(NG - 1, True)
            pe.drain().then_inc(done1["pe"], 1)

            def route(i):
                qr.at(Q2, QR, i)
                sr.at(S2, SR, i)
                tr.at(T2, TR, i)
                transpose_xn(NG + i, xw)
                b = tr.fill(pe)
                for j in range(G):
                    for c in range(C):
                        mm = pe.matmul(b[:, j * E0:(j + 1) * E0], xnT[:, c, j * P:(j + 1) * P], rwT[:, c, :],
                                       start=(c == 0), stop=(c == C - 1))
                mm.then_inc(t_ring.full, 1)
                for half in range(2):
                    for ring, end, o in ((s_ring, sr, 0), (q_ring, qr, I0)):
                        b = end.fill(pe)
                        for c in range(C):
                            mm = pe.matmul(b[0:I0, 0:2 * P], sh_gu[:, c, o:o + I0],
                                           xnT[:, c, half * 2 * P:(half + 1) * 2 * P], start=(c == 0),
                                           stop=(c == C - 1))
                        mm.then_inc(ring.full, 1)
                for j in range(G):
                    if j % 2 == 0:
                        qr.evacuated(pe, 2 - j // 2)
                    pe.wait_ge(o_read, G * (NG + i) + j + 1)
                    pe.matmul(o_banks[j % 2][:, 0:DIM], sh_h[:, j * P:(j + 1) * P], sh_dn[:], start=True,
                              stop=True).then_inc(o_full, 1)
                pe.wait_ge(key_ready, i + 1)
                b = tr.fill(pe)
                pe.sem_inc(pe_wait_done, 1)
                for j in range(G):
                    mm = pe.transpose(b[0:E0, j * P:(j + 1) * P], part[9][:, j * E0:(j + 1) * E0], ident[:])
                mm.then_inc(t_ring.full, 1)

            pe.wait_ge(r_loaded, 64)
            with pe.Fori(0, NG) as i:
                route(i)
            tr.at(T2 + TR * NG)
            pe.wait_ge(slots_ready, 1)
            pe.transpose(tr.fill(pe)[:, 0:E0], slots[:], ident[0:E0, 0:E0]).then_inc(t_ring.full, 1)

            def transpose_rows(i, q):
                pe.wait_ge(xg_loaded[q], 32 * (i + 1))
                b = tr.fill(pe)
                for e in range(2):
                    for c in range(C):
                        at = (2 * e + c) * P
                        mm = pe.transpose(b[:, at:at + P], xg[:, q, e, c * P:(c + 1) * P], ident[:])
                mm.then_inc(t_ring.full, 1)

            def experts(i, last):
                qr.at(Q3, 4, i)
                sr.at(S3, 4, i)
                tr.at(T3 + 1, 4, i)
                for q in range(4):
                    pe.wait_ge(w_loaded[q], 32 * (i + 1))
                    tr.evacuated(pe)
                    for ring, end, o in ((s_ring, sr, 0), (q_ring, qr, I0)):
                        b = end.fill(pe)
                        for e in range(2):
                            for c in range(C):
                                mm = pe.matmul(b[0:I0, e * P:(e + 1) * P], w_gu[:, q, e, c, o:o + I0],
                                               xgT[:, q % 2, e, c, :], start=(c == 0), stop=(c == C - 1))
                        mm.then_inc(ring.full, 1)
                    if not (last and q == 3):
                        transpose_rows(i + (q + 1) // 4, (q + 1) % 4)
                    qr.evacuated(pe)
                    if q < 2:
                        pe.wait_ge(y_ready if i is not first_step else o_read,
                                   4 * i + q - 1 if i is not first_step else 2 + 2 * NT)
                    else:
                        pe.wait_ge(y_ready, 4 * i + q - 1)
                    for e in range(2):
                        mm = pe.matmul(o_banks[q % 2][:, e * DIM:(e + 1) * DIM], act_h[:, q % 2, e * P:(e + 1) * P],
                                       w_dn[:, q, e, :], start=True, stop=True)
                    mm.then_inc(y_full, 1)

            first_step = 0
            tr.at(T3)
            transpose_rows(0, 0)
            experts(0, False)
            with pe.Fori(1, NQ - 1) as i:
                experts(i, False)
            experts(NQ - 1, True)

            def attention(i):
                qr.at(Q4, QA, i)
                sr.at(S4, SA, i)
                tr.at(T4, TA, i)
                pe.wait_ge(ctx_loaded, 16 * (NG + i + 1))
                for _ in range(2):
                    pe.transpose(tr.fill(pe)[:, 0:P], ctx_rows[:], ident[:]).then_inc(t_ring.full, 1)
                tr.evacuated(pe)
                for swapped in range(2):
                    for n in range(2):
                        pe.matmul(qr.fill(pe)[:], ctxT[:, swapped * SKV:swapped * SKV + P], wkv1[:, n, :],
                                  start=True, stop=True).then_inc(q_ring.full, 1)
                transpose_xn(2 * NG + i)
                for half in range(2):
                    b = qr.fill(pe)
                    for k in range(2):
                        j = 2 * half + k
                        for c in range(C):
                            mm = pe.matmul(b[:, k * DIM:(k + 1) * DIM], xnT[:, c, j * P:(j + 1) * P], wq1[:, c, :],
                                           start=(c == 0), stop=(c == C - 1))
                    mm.then_inc(q_ring.full, 1)
                pe.wait_ge(k1_ready, i + 1)
                for c in range(C):
                    pe.transpose(tr.fill(pe)[:, 0:P], k1[:, 0, 8 * c:8 * c + 8, :].rearrange("p h d -> p (h d)"),
                                 ident[:]).then_inc(t_ring.full, 1)
                pe.wait_ge(q1_ready, i + 1)
                for c in range(C):
                    b = tr.fill(pe)
                    for j in range(G):
                        at = j * H1 + 8 * c
                        mm = pe.transpose(b[:, j * P:(j + 1) * P],
                                          q1[:, at:at + 8, :].rearrange("p h d -> p (h d)"), ident[:])
                    mm.then_inc(t_ring.full, 1)
                tr.evacuated(pe)
                pe.wait_ge(k_blocks_ready, 4 * (i + 1))
                for j in range(G):
                    for c in range(C):
                        pe.matmul(sr.fill(pe)[:], q1T[:, c, j * P:(j + 1) * P],
                                  k_blocks[:, j // 2, c].rearrange("p h k -> p (h k)"), start=True,
                                  stop=True).then_inc(s_ring.full, 1)

                place = {}

                def transpose_attn(j):
                    pe.wait_ge(attn_ready, NT + 2 * (G * i + j) + 2)
                    for g in range(2):
                        b = tr.fill(pe)
                        for k in range(4):
                            at = (4 * g + k) * P
                            mm = pe.transpose(b[:, k * P:(k + 1) * P], soft[:, j, at:at + P], ident[:])
                        mm.then_inc(t_ring.full, 1)
                    place["a", j] = tr.k

                def contexts(j):
                    tr.evacuated(pe, tr.k - place["a", j] + 1)
                    if j == 0:
                        pe.wait_ge(v1_ready, 4 * (i + 1))
                    pe.wait_ge(o_read, G * (2 * NG + i) + j + 1)
                    for p in range(8):
                        mm = pe.matmul(o_banks[j % 2][:, 32 * p:32 * (p + 1)], attnT[:, j % 2, p, :],
                                       v_blocks[:, j // 2, p].rearrange("p o d -> p (o d)"), start=True, stop=True)
                    mm.then_inc(c1_full, 1)

                def transpose_context(j):
                    pe.wait_ge(c1_ready, G * i + j + 1)
                    b = tr.fill(pe)
                    for c in range(C):
                        mm = pe.transpose(b[:, c * P:(c + 1) * P], c1[:, j % 2, c * P:(c + 1) * P], ident[:])
                    mm.then_inc(t_ring.full, 1)
                    place["c", j] = tr.k

                def output(j):
                    tr.evacuated(pe, tr.k - place["c", j] + 1)
                    for c in range(C):
                        mm = pe.matmul(o_banks[j % 2][:, DIM:2 * DIM], c1T[:, j % 2, c, :], wo1[:, c, :],
                                       start=(c == 0), stop=(c == C - 1))
                    mm.then_inc(o_full, 1)

                transpose_attn(0)
                transpose_attn(1)
                contexts(0)
                transpose_attn(2)
                contexts(1)
                transpose_context(0)
                transpose_attn(3)
                output(0)
                transpose_context(1)
                contexts(2)
                output(1)
                transpose_context(2)
                contexts(3)
                output(2)
                transpose_context(3)
                output(3)

            pe.wait_ge(w3_loaded, 16 * 20)
            with pe.Fori(0, NG) as i:
                attention(i)

            def mixture(i):
                qr.at(Q5, QM, i)
                sr.at(S5, SM, i)
                tr.at(T5, TM, i)
                transpose_xn(3 * NG + i)
                for half in range(2):
                    b = tr.fill(pe)
                    for k in range(2):
                        j = 2 * half + k
                        for c in range(C):
                            mm = pe.matmul(b[:, k * E1:(k + 1) * E1], xnT[:, c, j * P:(j + 1) * P], gate1[:, c, :],
                                           start=(c == 0), stop=(c == C - 1))
                    mm.then_inc(t_ring.full, 1)

                def gates_ups(j):
                    for p in range(5):
                        for o, (ring, end) in enumerate(((s_ring, sr), (q_ring, qr))):
                            b = end.fill(pe)
                            for c in range(C):
                                mm = pe.matmul(b[:, 0:2 * F1], xnT[:, c, j * P:(j + 1) * P], gu1[:, c, p, o, :],
                                               start=(c == 0), stop=(c == C - 1))
                            mm.then_inc(ring.full, 1)

                def down(j):
                    pe.wait_ge(q_ring.free, Q5 + QM * i + 5 * (j + 1))
                    for g in range(4):
                        b = tr.fill(pe)
                        for f in range(4 * g, min(4 * g + 4, FC)):
                            n = min(P, W1 - f * P)
                            mm = pe.transpose(b[0:n, (f % 4) * P:(f % 4 + 1) * P],
                                              act_v[:, j % 2, f * P:f * P + n], ident[:])
                        mm.then_inc(t_ring.full, 1)
                    pe.wait_ge(o_read, G * (3 * NG + i) + j + 1)
                    for f in range(FC):
                        n = min(P, W1 - f * P)
                        if f % 4 == 0:
                            tr.evacuated(pe, 4 - f // 4)
                        mm = pe.matmul(o_banks[j % 2][:, 0:DIM], attn_flat[0:n, f, :], dn1[0:n, f, :],
                                       start=(f == 0), stop=(f == FC - 1))
                    mm.then_inc(o_full, 1)

                gates_ups(0)
                gates_ups(1)
                for j in range(G):
                    down(j)
                    if j + 2 < G:
                        gates_ups(j + 2)

            attn_flat = attnT[:].rearrange("p b f t -> p (b f) t")
            pe.wait_ge(w4_loaded, 64)
            with pe.Fori(0, NG) as i:
                mixture(i)


_INS = ["x", "ctx_1024", "g_xattn", "g_ffn", "L0_xattn_Wq", "L0_xattn_Wk", "L0_xattn_Wv", "L0_xattn_Wo",
        "L0_xattn_gq", "L0_xattn_gk", "L0_ffn_e_bias", "L0_ffn_w_down", "L0_ffn_sh_down",
        "L1_xattn_Wq", "L1_xattn_bq", "L1_xattn_Wk", "L1_xattn_bk", "L1_xattn_Wv", "L1_xattn_bv",
        "L1_xattn_Wkv_dca", "L1_xattn_bkv_dca", "L1_xattn_qn_w", "L1_xattn_qn_b", "L1_xattn_kn_w",
        "L1_xattn_kn_b", "L1_xattn_kn_dca_w", "L1_xattn_kn_dca_b", "L1_xattn_Wo", "L1_xattn_bo"]


def kernel(**inputs):
    import numpy as np
    import concourse.bacc as bacc
    from concourse.bass_utils import run_bass_kernel_spmd as run

    nc = bacc.Bacc("TRN2", target_bir_lowering=False, num_devices=1)
    arrays, args = {}, {}
    laid_out = {name: inputs[name] for name in _INS}
    laid_out["L0_ffn_router_weightT"] = np.asarray(inputs["L0_ffn_router_weight"]).T
    laid_out["L0_ffn_w_gu"] = np.concatenate([inputs["L0_ffn_w_gate"], inputs["L0_ffn_w_up"]], axis=2)
    laid_out["L0_ffn_sh_gu"] = np.concatenate([inputs["L0_ffn_sh_gate"], inputs["L0_ffn_sh_up"]], axis=1)
    gu = np.asarray(inputs["L1_ffn_gate_up_weights"]).reshape(E1, 2, F1, DIM)
    shared = np.asarray(inputs["L1_ffn_shared_gate_up"]).reshape(2, 2, F1, DIM).transpose(1, 0, 2, 3)
    gu = np.concatenate([gu, shared], axis=0).reshape(5, 2, 2, F1, DIM)
    laid_out["L1_gu"] = gu.transpose(4, 0, 2, 1, 3).reshape(DIM, 5, 2, 2 * F1)
    down = np.asarray(inputs["L1_ffn_down_weights"]).transpose(0, 2, 1).reshape(E1 * F1, DIM)
    laid_out["L1_down"] = np.concatenate([down, np.asarray(inputs["L1_ffn_shared_down"]).T], axis=0)
    laid_out["L1_gateT"] = np.asarray(inputs["L1_ffn_gate_weight"]).T
    for name, v in laid_out.items():
        v = np.ascontiguousarray(v)
        arrays[f"in_{name}"] = v
        args[name] = nc.dram_tensor(f"in_{name}", v.shape, mybir.dt.from_np(v.dtype), kind="ExternalInput").ap()
    out = nc.dram_tensor("out_0", (B, SQ, DIM), F32, kind="ExternalOutput").ap()
    flamingo(nc, args, out)
    r = run(nc, [arrays], core_ids=[0])
    return r.results[0]["out_0"]
```

```python
from contextlib import ExitStack

import concourse.bass as bass
from concourse import mybir

F32 = mybir.dt.float32
I32 = mybir.dt.int32
ACT = mybir.ActivationFunctionType
ALU = mybir.AluOpType
AX = mybir.AxisListType

P = 128
B, SQ, DIM = 8, 256, 256
SKV, CDIM = 64, 128
T = B * SQ
NT = T // P
G = 4
NG = NT // G
C = DIM // P
H0, D0 = 16, 128
E0, I0, K0 = 64, 88, 8
CAP = 128
ROW = DIM + E0
H1, D1, MAIN = 16, 16, 48
QK = G * H1 + H1
E1, F1 = 8, 176
W1 = (E1 + 2) * F1
FC = -(-W1 // P)
FAR = 1e30
EPS0 = 1e-5
EPS1 = 1e-6


class Ring:

    def __init__(self, banks, full, free):
        self.banks, self.full, self.free = banks, full, free

    def end(self):
        return RingEnd(self)


class RingEnd:

    def __init__(self, ring):
        self.ring, self.base, self.even, self.k = ring, 0, 0, 0

    def at(self, before, each=0, i=0):
        assert each % 2 == 0
        self.base, self.even, self.k = before + each * i, before % 2, 0

    def _take(self):
        pos, bank = self.base + self.k, self.ring.banks[(self.even + self.k) % len(self.ring.banks)]
        self.k += 1
        return pos, bank

    def fill(self, pe):
        pos, bank = self._take()
        if not (isinstance(pos, int) and pos < len(self.ring.banks)):
            pe.wait_ge(self.ring.free, pos - len(self.ring.banks) + 1)
        return bank

    def read(self, eng):
        pos, bank = self._take()
        eng.wait_ge(self.ring.full, pos + 1)
        return bank

    def evacuated(self, eng, back=1):
        eng.wait_ge(self.ring.free, self.base + self.k - back + 1)

    def skip(self, n):
        self.k += n


class Chain:

    def __init__(self, eng, sem):
        self.eng, self.sem, self.base, self.k = eng, sem, 0, 0

    def at(self, base):
        self.base, self.k = base, 0

    def add(self, ins):
        ins.then_inc(self.sem, 1)
        self.k += 1
        return self.k

    def wait(self, k=None):
        self.eng.wait_ge(self.sem, self.base + (self.k if k is None else k))


def flamingo(nc, a, out, stages=4):
    with ExitStack() as ctx:
        def sb(name, shape, dt=F32, scope=ctx):
            return scope.enter_context(nc.sbuf_tensor(name, shape, dt))

        def sem(name):
            return ctx.enter_context(nc.semaphore(name))

        bank = [ctx.enter_context(nc.psum_tensor(f"bank{n}", [P, 512], F32)) for n in range(8)]
        q_ring = Ring([bank[0], bank[1]], sem("q_full"), sem("q_free"))
        s_ring = Ring([bank[2], bank[3]], sem("s_full"), sem("s_free"))
        t_ring = Ring([bank[4], bank[5]], sem("t_full"), sem("t_free"))
        o_banks = [bank[6], bank[7]]
        n_bank = bank[7]

        x = sb("x", [P, NT, DIM])
        ident = sb("ident", [P, P])
        ones = sb("ones", [P, P])
        newton = sb("newton", [P, 80])
        gates = sb("gates", [P, 4])
        xn = sb("xn", [P, G, DIM])
        xnT = sb("xnT", [P, C, G * P])
        stats = sb("stats", [P, G, 6])
        mv = sb("mv", [P, G, 2])
        var = sb("var", [P, G])
        rstd = sb("rstd", [P, G])
        soft = sb("soft", [P, G, 1024])
        attnT = sb("attnT", [P, 2, 8, P])
        small = sb("small", [P, G, 2, 32])

        rwT = sb("rwT", [P, C, E0])
        e_bias = sb("e_bias", [P, E0])
        sh_gu = sb("sh_gu", [P, C, 2 * I0])
        sh_dn = sb("sh_dn", [I0, DIM])
        before = sb("before", [P, 8, 8])
        key_base = sb("key_base", [P, NT])
        keyT = sb("keyT", [P, T])
        zeros = keyT
        cand = sb("cand", [P, 2 * CAP])
        slots = sb("slots", [E0, CAP])
        slotsT = sb("slotsT", [P, E0])
        spare = sb("spare", [P, E0])
        src_idx = sb("src_idx", [P, E0], I32)
        dst_idx = sb("dst_idx", [P, E0], I32)
        sigs = soft[:, 3, 512:1024].rearrange("p (b n) -> p b n", b=2)
        keys2 = soft[:, 2, 0:512].rearrange("p (j h e) -> p j h e", j=G, h=2)
        part = [soft[:, n // 4, (n % 4) * 256:(n % 4 + 1) * 256] for n in range(16)]

        ctx_rows = sb("ctx_rows", [P, CDIM])

        gqk = sb("gqk", [P, 2])
        gscale = sb("gscale", [P, 1])
        first = ExitStack()
        wq = sb("wq", [P, C, H0 * D0], scope=first)
        wk = sb("wk", [P, H0 * D0], scope=first)
        wv = sb("wv", [P, H0 * D0], scope=first)
        wo = sb("wo", [P, H0, DIM], scope=first)
        ctxK = sb("ctxK", [P, P], scope=first)
        ctxV = sb("ctxV", [P, 2, 3 * SKV], scope=first)
        raw = sb("raw", [P, 2, G, H0 * SKV], scope=first)
        qT = sb("qT", [P, 3, G * P], scope=first)
        q2_last = sb("q2_last", [P, G * P], scope=first)
        q2 = [soft[:, 3, 0:512], soft[:, 3, 512:1024], q2_last[:]]
        prob = soft[:, 0, :]
        ksb = soft[:, 1:3, :].rearrange("p j (h d) -> p (j h) d", d=D0)
        ksq = attnT[:].rearrange("p b h t -> p (b h) t")
        kstat = sb("kstat", [P, 2, H0], scope=first)
        kT = sb("kT", [P, H0, P], scope=first)
        vT = sb("vT", [P, H0, P], scope=first)
        vw = sb("vw", [P, 2, 8, DIM], scope=first)
        qvar = sb("qvar", [P, G * H0], scope=first)
        rq = sb("rq", [P, G * H0], scope=first)


        first.close()

        xw = sb("xw", [P, 2, G, ROW])
        y2_rows = sb("y2_rows", [P, 2, K0 * DIM])
        y2_sum = sb("y2_sum", [P, 2, DIM])
        second = ExitStack()
        sh_g = sb("sh_g", [I0, G * P], scope=second)
        sh_h = sb("sh_h", [I0, G * P], scope=second)
        w_gu = sb("w_gu", [P, 4, 2, C, 2 * I0], scope=second)
        w_dn = sb("w_dn", [I0, 4, 2, DIM], scope=second)
        xg = sb("xg", [P, 4, 2, ROW], scope=second)
        xgT = sb("xgT", [P, 2, 2, C, P], scope=second)
        act_g = sb("act_g", [I0, 2, 2 * P], scope=second)
        act_h = sb("act_h", [I0, 2, 2 * P], scope=second)
        y = sb("y", [P, 4, 2, DIM], scope=second)
        src_now = sb("src_now", [P, 4, 2], I32, scope=second)
        dst_now = sb("dst_now", [P, 4, 2], I32, scope=second)
        second.close()

        gu1 = sb("gu1", [P, C, 5, 2, 2 * F1])
        dn1 = sb("dn1", [P, FC, DIM])
        gate1 = sb("gate1", [P, C, E1])
        sg = sb("sg", [P, 2, 2 * F1])
        combine_w = sb("combine_w", [P, G, E1 + 2])
        act_v = soft[:].rearrange("p j n -> p (j n)")[:, 0:2 * FC * P].rearrange("p (b n) -> p b n", b=2)
        logits = sb("logits", [P, G * E1])
        rank_t = sb("rank_t", [P, 2, G * E1 * E1])
        gate_s = sb("gate_s", [P, 3, G * E1])

        head_mask = sb("head_mask", [P, 8])
        qk1 = sb("qk1", [P, QK, D1])
        qk1_sq = sb("qk1_sq", [P, QK, D1])
        qk1_stat = sb("qk1_stat", [P, 2, QK])
        k1T = sb("k1T", [P, C, P])
        k_blocks = sb("k_blocks", [P, 2, C, 8, SKV])
        v_blocks = sb("v_blocks", [P, 2, 2, 8, 2, D1])
        q1T = sb("q1T", [P, C, G * P])
        c1 = sb("c1", [P, 2, DIM])
        c1T = sb("c1T", [P, 2, C, P])
        ctx1T = sb("ctx1T", [P, 2, 3 * SKV])
        wq1 = sb("wq1", [P, C, DIM])
        wkv1 = sb("wkv1", [P, 2, 2 * DIM])
        wo1 = sb("wo1", [P, C, DIM])
        bq1 = sb("bq1", [P, DIM])
        bkv1 = sb("bkv1", [P, 2 * DIM])
        bo1 = sb("bo1", [1, DIM])
        qn = sb("qn", [P, 2, D1])
        kn = sb("kn", [P, 2, D1])

        table = nc.dram_tensor("table", (T + 1, ROW), F32, kind="Internal").ap()
        y2 = nc.dram_tensor("y2", (K0 * T + E0 * CAP, DIM), F32, kind="Internal").ap()

        const_ready = sem("const_ready")
        ident_zero = sem("ident_zero")
        x_loaded = sem("x_loaded")
        x_rest_loaded = sem("x_rest_loaded")
        gates_loaded = sem("gates_loaded")
        gates_ready = sem("gates_ready")
        wk_loaded, wq_loaded, wv_loaded, wo_loaded = (sem(f"{w}_loaded") for w in ("wk", "wq", "wv", "wo"))
        gqk_loaded = sem("gqk_loaded")
        gqk_ready = sem("gqk_ready")
        ctx_loaded = sem("ctx_loaded")
        dve_chain = sem("dve_chain")
        wait_done, pe_wait_done, pool_wait_done = sem("wait_done"), sem("pe_wait_done"), sem("pool_wait_done")
        xn_ready = sem("xn_ready")
        kn_ready = sem("kn_ready")
        q2_ready = sem("q2_ready")
        q_norm = sem("q_norm")
        shifted = sem("shifted")
        exp_done = sem("exp_done")
        attn_ready = sem("attn_ready")
        o_full = sem("o_full")
        o_read = sem("o_read")
        x_done = sem("x_done")
        stored = sem("stored")
        done1 = {e: sem(f"done1_{e}") for e in ("pe", "act", "dve", "pool")}
        r_loaded = sem("r_loaded")
        r_const = sem("r_const")
        zero_ready = sem("zero_ready")
        zeroed = sem("zeroed")
        table_stored = sem("table_stored")
        key_ready = sem("key_ready")
        rows_ready = sem("rows_ready")
        slot_chain = sem("slot_chain")
        slots_ready = sem("slots_ready")
        cand_ready = sem("cand_ready")
        cand_moved = sem("cand_moved")
        idx_ready = sem("idx_ready")
        idx_now = sem("idx_now")
        w_loaded = [sem(f"w_loaded{q}") for q in range(4)]
        xg_loaded = [sem(f"xg_loaded{q}") for q in range(4)]
        y_stored = [sem(f"y_stored{q}") for q in range(4)]
        y_full = sem("y_full")
        y_ready = sem("y_ready")
        y2_loaded = [sem(f"y2_loaded{q}") for q in range(2)]
        y2_used = sem("y2_used")
        w3_loaded = sem("w3_loaded")
        w4_loaded = sem("w4_loaded")
        mask_step = sem("mask_step")
        combined = sem("combined")
        combine_step = sem("combine_step")
        k1_ready = sem("k1_ready")
        v1_ready = sem("v1_ready")
        k_blocks_ready = sem("k_blocks_ready")
        q1_centred = sem("q1_centred")
        q1_squared = sem("q1_squared")
        q1_ready = sem("q1_ready")
        c1_full = sem("c1_full")
        c1_ready = sem("c1_ready")
        gate_shifted = sem("gate_shifted")
        gate_exp = sem("gate_exp")
        act_ready = sem("act_ready")

        x_d = a["x"].rearrange("b t d -> (b t) d").rearrange("(n p) d -> p n d", p=P)
        out_d = out.rearrange("b t d -> (b t) d").rearrange("(n p) d -> p n d", p=P)
        ctx_d = a["ctx_1024"].rearrange("b s c -> (b s) c")

        Q_PREP, Q_STEP = 4, 24
        S_PREP, S_STEP = 0, 16
        T_PREP, T_STEP = 6, 16
        T_HEADS = 8
        Q2, S2, T2 = Q_STEP * NG, S_STEP * NG, T_STEP * NG
        QR, SR, TR, TRF = 2, 2, 4, 3
        Q3, S3, T3 = Q2 + QR * NG, S2 + SR * NG, T2 + TR * NG + 1
        NQ = E0 // 8
        Q4, S4, T4 = Q3 + 4 * NQ, S3 + 4 * NQ, T3 + 4 * NQ
        QA, SA, TA = 4, 8, 18
        W3 = 8 + 2 * 6
        TF = 6
        Q5, S5, T5 = Q4 + QA * NG, S4 + SA * NG, T4 + TA * NG
        QM, SM, TM = 20, 20, 20

        block = ctx.enter_context(nc.Block())

        @block.sync
        def _(sp):
            sp.dma_start(x[:, 0:G, :], x_d[:, 0:G, :]).then_inc(x_loaded, 16)
            sp.dma_start(ctx_rows[:], ctx_d[0:P, :]).then_inc(ctx_loaded, 16)
            sp.dma_start(wk[:], a["L0_xattn_Wk"]).then_inc(wk_loaded, 16)
            sp.dma_start(wq[:], a["L0_xattn_Wq"].rearrange("(c p) n -> p c n", p=P)).then_inc(wq_loaded, 16)
            sp.dma_start(wv[:], a["L0_xattn_Wv"]).then_inc(wv_loaded, 16)
            sp.dma_start(wo[:], a["L0_xattn_Wo"].rearrange("(h p) n -> p h n", p=P)).then_inc(wo_loaded, 16)
            sp.dma_start(x[:, G:NT, :], x_d[:, G:NT, :]).then_inc(x_rest_loaded, 16)
            for m in range(1, NG):
                sp.wait_ge(t_ring.full, 2 if m == 1 else T_PREP + 4 if m == 2 else
                           T_PREP + T_STEP * (m - 2) - T_HEADS + 4)
                sp.dma_start(ctx_rows[:], ctx_d[m * P:(m + 1) * P, :]).then_inc(ctx_loaded, 16)
            sp.wait_ge(zero_ready, 1)
            for n in range(NT):
                sp.dma_start(y2[n * P * K0:(n + 1) * P * K0, :].rearrange("(p k) d -> p (k d)", p=P),
                             zeros[:]).then_inc(zeroed, 16)
            sp.dma_start(table[T:T + 1, :], zeros[0:1, 0:ROW]).then_inc(table_stored, 16)
            table_d = table[0:T, :].rearrange("(n p) r -> p n r", p=P)
            with sp.Fori(0, NG) as i:
                sp.wait_ge(rows_ready, i + 1)
                sp.dma_start(table_d[:, bass.ds(G * i, G), :], xw[:, i % 2]).then_inc(table_stored, 16)

            def load_experts(i, q):
                sp.dma_start(w_gu[:, q], gu_d[:, bass.ds(8 * i + 2 * q, 2)]).then_inc(w_loaded[q], 16)
                sp.dma_start(w_dn[:, q], dn_d[:, bass.ds(8 * i + 2 * q, 2)]).then_inc(w_loaded[q], 16)

            gu_d = a["L0_ffn_w_gu"].rearrange("e (c p) n -> p e c n", p=P)
            dn_d = a["L0_ffn_w_down"].rearrange("e p n -> p e n")
            for e in done1.values():
                sp.wait_ge(e, 1)
            for q in range(4):
                load_experts(0, q)
            for dst, src in ((wq1[:], a["L1_xattn_Wq"].rearrange("(c p) n -> p c n", p=P)),
                             (wo1[:], a["L1_xattn_Wo"].rearrange("(c p) n -> p c n", p=P)),
                             (wkv1[:, 0, :], a["L1_kv_main"]), (wkv1[:, 1, :], a["L1_xattn_Wkv_dca"]),
                             (bq1[:], a["L1_xattn_bq"].partition_broadcast(P)),
                             (bo1[:], a["L1_xattn_bo"].unsqueeze(0)),
                             (qn[:, 0, :], a["L1_xattn_qn_w"].partition_broadcast(P)),
                             (qn[:, 1, :], a["L1_xattn_qn_b"].partition_broadcast(P))):
                sp.dma_start(dst, src).then_inc(w3_loaded, 16)
            for b0 in (0, SKV):
                sp.dma_start(bkv1[b0:b0 + MAIN, :], a["L1_bkv_main"].partition_broadcast(MAIN)).then_inc(w3_loaded, 16)
                sp.dma_start(bkv1[b0 + MAIN:b0 + SKV, :], a["L1_xattn_bkv_dca"].partition_broadcast(
                    SKV - MAIN)).then_inc(w3_loaded, 16)
                for n, name in enumerate(("w", "b")):
                    sp.dma_start(kn[b0:b0 + MAIN, n, :], a["L1_xattn_kn_" + name].partition_broadcast(MAIN)).then_inc(
                        w3_loaded, 16)
                    sp.dma_start(kn[b0 + MAIN:b0 + SKV, n, :], a["L1_xattn_kn_dca_" + name].partition_broadcast(
                        SKV - MAIN)).then_inc(w3_loaded, 16)
            sp.dma_start(ctx_rows[:], ctx_d[0:P, :]).then_inc(ctx_loaded, 16)
            sp.wait_ge(cand_ready, 1)
            sp.dma_start(cand[0:E0, CAP:2 * CAP], cand[E0:P, 0:CAP]).then_inc(cand_moved, 16)
            with sp.Fori(1, NQ) as i:
                for q in range(4):
                    sp.wait_ge(y_full, 4 * i + q - 3)
                    load_experts(i, q)
            for q in range(4):
                sp.wait_ge(y_stored[q], 32 * NQ)
            y2_d = y2[0:K0 * T, :].rearrange("(n p k) d -> n p (k d)", p=P, k=K0)

            def load_y2(n, q):
                sp.dma_start(y2_rows[:, q], y2_d[bass.ds(n, 1)].rearrange("n p k -> p (n k)")).then_inc(
                    y2_loaded[q], 16)

            load_y2(0, 0)
            load_y2(1, 1)

            def more_y2(i, tiles):
                for k in range(tiles):
                    sp.wait_ge(y2_used, G * i + k + 1)
                    load_y2(G * i + k + 2, k % 2)

            def next_context(i):
                sp.wait_ge(t_ring.full, T4 + 1 if i is first_group else T4 + TF + TA * (i - 1) + 1)
                sp.dma_start(ctx_rows[:], ctx_d[(i + 1) * P:(i + 2) * P, :] if i is first_group else
                             ctx_d[bass.ds((i + 1) * P, P), :]).then_inc(ctx_loaded, 16)

            first_group = 0
            more_y2(0, G)
            next_context(0)
            sp.dma_start(gu1[:], a["L1_gu"].rearrange("(c p) e g n -> p c e g n", p=P)).then_inc(w4_loaded, 16)
            full = (FC - 1) * P
            sp.dma_start(dn1[:, 0:FC - 1, :], a["L1_down"][0:full, :].rearrange("(f p) n -> p f n", p=P)).then_inc(
                w4_loaded, 16)
            sp.dma_start(dn1[0:W1 - full, FC - 1, :], a["L1_down"][full:W1, :]).then_inc(w4_loaded, 16)
            sp.dma_start(gate1[:], a["L1_gateT"].rearrange("(c p) e -> p c e", p=P)).then_inc(w4_loaded, 16)
            with sp.Fori(1, NG - 1) as i:
                more_y2(i, G)
                next_context(i)
            more_y2(NG - 1, G - 2)
            sp.wait_ge(x_done, 1)
            sp.dma_start(out_d, x[:]).then_inc(stored, 16)
            sp.wait_ge(stored, 16)

        @block.gpsimd
        def _(pool):
            pool.memset(ident[:], 0.0).then_inc(ident_zero, 1)
            pool.wait_ge(ident_zero, 1)
            pool.memset(zeros[:], 0.0).then_inc(zero_ready, 1)
            pool.memset(before[:], 1.0).then_inc(ident_zero, 1)
            pool.iota(key_base[:], pattern=[[-K0 * P * G, NG], [K0 - K0 * P, G]], base=K0 * T + 1,
                      channel_multiplier=-K0, allow_small_or_imprecise_dtypes=True).then_inc(r_const, 1)
            pool.iota(spare[:], pattern=[[CAP, E0]], base=0, channel_multiplier=1,
                      allow_small_or_imprecise_dtypes=True).then_inc(r_const, 1)
            pool.wait_ge(ident_zero, 2)
            pool.affine_select(out=before[:], in_=before[:], compare_op=ALU.is_gt, fill=0.0,
                               base=0, pattern=[[1, 8], [-1, 8]], channel_multiplier=0).then_inc(r_const, 1)
            pool.affine_select(out=ident[:], in_=ident[:], compare_op=ALU.not_equal, fill=1.0,
                               base=0, pattern=[[-1, P]], channel_multiplier=1).then_inc(const_ready, 1)

            pool.drain().then_inc(done1["pool"], 1)

            def gather(i, q):
                pool.sem_inc(pool_wait_done, 1)
                for e in range(2):
                    pool.indirect_dma_start(xg[:, q, e, :], None, table, bass.IndirectOffsetOnAxis(
                        ap=src_now[:, q, e:e + 1], axis=0)).then_inc(xg_loaded[q], 16)

            def scatter(i, q):
                pool.wait_ge(y_ready, 4 * i + q + 1)
                pool.sem_inc(pool_wait_done, 1)
                for e in range(2):
                    pool.indirect_dma_start(y2, bass.IndirectOffsetOnAxis(ap=dst_now[:, q, e:e + 1], axis=0),
                                            y[:, q, e, :], None).then_inc(y_stored[q], 16)

            pool.wait_ge(table_stored, 16 * (NG + 1))
            pool.wait_ge(zeroed, 16 * NT)
            for q in range(3):
                pool.wait_ge(idx_now, q + 1)
                gather(0, q)

            def experts(i, last):
                for q in range(4):
                    if not (last and q):
                        pool.wait_ge(idx_now, 4 * i + q + 4)
                        gather(i, (q + 3) % 4)
                    scatter(i, q)

            with pool.Fori(0, NQ - 1) as i:
                experts(i, False)
            experts(NQ - 1, True)

            def combine(i):
                for j in range(G):
                    r, base = y2_rows[:, j % 2], 4 * (G * (i - 1) + j)
                    pool.wait_ge(y2_loaded[j % 2], 16 * (2 * i + j // 2 + 1))
                    for n, half in enumerate((4 * DIM, 2 * DIM, DIM)):
                        pool.tensor_tensor(r[:, 0:half], r[:, 0:half], r[:, half:2 * half],
                                           ALU.add).then_inc(combine_step, 1)
                        pool.wait_ge(combine_step, base + n + 1)
                    pool.sem_inc(pool_wait_done, 1)
                    pool.tensor_scalar(r[:, 0:DIM], r[:, 0:DIM], gates[:, 2:3], None, ALU.mult).then_inc(combine_step, 1)
                    pool.wait_ge(combine_step, base + 4)
                    xj = x[:, G * i + j, :]
                    pool.tensor_tensor(xj, xj, r[:, 0:DIM], ALU.add).then_inc(y2_used, 1)

            def key_blocks(i):
                pool.wait_ge(t_ring.free, T4 + TF - 2 + TA * i)
                for b in range(2):
                    for c in range(C):
                        pool.tensor_tensor(
                            k_blocks[:, b, c], k1T[:, c, b * SKV:(b + 1) * SKV].unsqueeze(1).to_broadcast([P, 8, SKV]),
                            head_mask[:].unsqueeze(2).to_broadcast([P, 8, SKV]), ALU.mult).then_inc(k_blocks_ready, 1)

            for q in range(4):
                pool.wait_ge(y_stored[q], 32 * NQ)
            pool.memset(head_mask[:], 1.0).then_inc(mask_step, 1)
            pool.wait_ge(mask_step, 1)
            pool.affine_select(out=head_mask[:], in_=head_mask[:], compare_op=ALU.is_ge, fill=0.0, base=0,
                               pattern=[[-D1, 8]], channel_multiplier=1).then_inc(mask_step, 1)
            pool.wait_ge(mask_step, 2)
            pool.affine_select(out=head_mask[:], in_=head_mask[:], compare_op=ALU.is_ge, fill=0.0, base=D1 - 1,
                               pattern=[[D1, 8]], channel_multiplier=-1).then_inc(mask_step, 1)
            pool.wait_ge(mask_step, 3)
            pool.memset(ctx1T[:], 0.0).then_inc(mask_step, 1)
            pool.wait_ge(y2_used, G)
            with pool.Fori(0, NG - 1) as i:
                combine(i + 1)
                key_blocks(i)
            key_blocks(NG - 1)

        @block.vector
        def _(dve):
            qr = q_ring.end()
            ch = Chain(dve, dve_chain)
            dve.memset(ones[:], 1.0).then_inc(const_ready, 1)
            dve.sem_inc(o_read, 2)
            dve.wait_ge(gqk_loaded, 32)
            dve.scalar_tensor_tensor(out=gscale[:], in0=gqk[:, 0:1], scalar=float(D0) ** -0.5,
                                     in1=gqk[:, 1:2], op0=ALU.mult, op1=ALU.mult).then_inc(gqk_ready, 1)

            def inverse_root(y_, v, n):
                t = newton[:, 0:n]
                ch.add(dve.tensor_scalar(y_.bitcast(I32), v.bitcast(I32), 1, None, ALU.logical_shift_right))
                ch.wait()
                ch.add(dve.tensor_scalar(y_.bitcast(I32), y_.bitcast(I32), -1.0, float(0x5F3759DF), ALU.mult,
                                         ALU.add))
                ch.wait()
                for _ in range(3):
                    ch.add(dve.tensor_tensor(t, y_, y_, ALU.mult))
                    ch.wait()
                    ch.add(dve.scalar_tensor_tensor(out=t, in0=t, scalar=-0.5, in1=v, op0=ALU.mult, op1=ALU.mult))
                    ch.wait()
                    ch.add(dve.scalar_tensor_tensor(out=y_, in0=t, scalar=1.5, in1=y_, op0=ALU.add, op1=ALU.mult))
                    ch.wait()

            ROOT_CHAIN = 11

            def over_head(v, n=D1):
                return v.unsqueeze(2).to_broadcast([P, v.shape[1], n])

            def row_stats(i):
                dve.sem_inc(wait_done, 1)
                for j in range(G):
                    ch.add(dve.bn_stats(stats[:, j, :], x[:, G * i + j, :]))
                ch.wait()
                dve.sem_inc(wait_done, 1)
                for j in range(G):
                    ch.add(dve.bn_aggr(mv[:, j, :], stats[:, j, :]))
                ch.wait()

            def row_roots(eps):
                ch.add(dve.tensor_scalar(var[:], mv[:, :, 1], eps, None, ALU.add))
                ch.wait()
                inverse_root(rstd[:], var[:], G)

            def row_apply(i):
                for j in range(G):
                    dve.tensor_scalar(xn[:, j, :], x[:, G * i + j, :], mv[:, j, 0:1], rstd[:, j:j + 1],
                                      ALU.subtract, ALU.mult).then_inc(xn_ready, 1)

            def normed(i, eps):
                row_stats(i)
                row_roots(eps)
                row_apply(i)

            NORMED_CHAIN = 2 * G + 1 + ROOT_CHAIN

            def keys_in():
                for g in range(4):
                    dve.tensor_copy(ksb[:, 4 * g:4 * g + 4, :], qr.read(dve)[:].rearrange(
                        "p (h d) -> p h d", h=4)).then_inc(q_ring.free, 1)

            def values_in():
                for g in range(4):
                    dve.tensor_copy(vT[:, 4 * g:4 * g + 4, :], qr.read(dve)[:].rearrange(
                        "p (h d) -> p h d", h=4)).then_inc(q_ring.free, 1)

            def key_norm(back):
                qr.evacuated(dve, back)
                ch.add(dve.tensor_tensor(ksq[:], ksb[:], ksb[:], ALU.mult))
                ch.wait()
                ch.add(dve.tensor_reduce(kstat[:, 0, :], ksq[:], AX.X, ALU.add))
                ch.wait()
                ch.add(dve.tensor_scalar(kstat[:, 0, :], kstat[:, 0, :], 1.0 / D0, EPS0, ALU.mult, ALU.add))
                ch.wait()
                inverse_root(kstat[:, 1, :], kstat[:, 0, :], H0)
                dve.tensor_tensor(ksb[:], ksb[:], over_head(kstat[:, 1, :], D0), ALU.mult).then_inc(kn_ready, 1)

            def over(v):
                return v.unsqueeze(2).to_broadcast([P, H0, SKV])

            def residual(m, j, i=None, gate=0, one_bank=False):
                dve.wait_ge(o_full, G * m + j + 1)
                i = m if i is None else i
                xj = x[:, G * i + j, :]
                dve.scalar_tensor_tensor(out=xj, in0=o_banks[0 if one_bank else j % 2][:, 0:DIM],
                                         scalar=gates[:, gate:gate + 1], in1=xj, op0=ALU.mult,
                                         op1=ALU.add).then_inc(o_read, 1)

            KEY_CHAIN, ROOTS_CHAIN, SOFT_CHAIN = 3 + ROOT_CHAIN, 1 + ROOT_CHAIN, 4 * G
            PREP_CHAIN = NORMED_CHAIN + KEY_CHAIN
            STEP_CHAIN = NORMED_CHAIN + KEY_CHAIN + ROOTS_CHAIN + SOFT_CHAIN

            def softmax_pieces(i, par):
                def tile(j):
                    return raw[:, par, j, :].rearrange("p (h k) -> p h k", h=H0)

                def by_norm(j):
                    ch.add(dve.tensor_tensor(tile(j), tile(j), over(rq[:, j * H0:(j + 1) * H0]), ALU.mult))
                    ch.wait()

                def maximum(j):
                    dve.sem_inc(wait_done, 1)
                    ch.add(dve.tensor_reduce(small[:, j, 0, 0:H0], tile(j), AX.X, ALU.max))
                    ch.wait()

                def shift(j):
                    dve.tensor_tensor(tile(j), tile(j), over(small[:, j, 0, 0:H0]), ALU.subtract).then_inc(shifted, 1)

                def sums(j):
                    dve.wait_ge(exp_done, G * i + j + 1)
                    dve.sem_inc(wait_done, 1)
                    ch.add(dve.tensor_reduce(small[:, j, 1, 0:H0], tile(j), AX.X, ALU.add))
                    ch.wait()
                    ch.add(dve.reciprocal(small[:, j, 1, 0:H0], small[:, j, 1, 0:H0]))
                    ch.wait()

                def divide(j, before):
                    if before is not None:
                        dve.wait_ge(t_ring.full, before)
                    dve.tensor_tensor(prob.rearrange("p (h k) -> p h k", h=H0), tile(j),
                                      over(small[:, j, 1, 0:H0]), ALU.mult).then_inc(attn_ready, 1)

                return by_norm, maximum, shift, sums, divide

            dve.wait_ge(x_loaded, 16)
            normed(0, EPS0)
            keys_in()
            key_norm(1)
            assert ch.k == PREP_CHAIN

            def step(i, first_, last):
                qr.at(Q_PREP, Q_STEP, i)
                ch.at(PREP_CHAIN + STEP_CHAIN * i - (0 if first_ else SOFT_CHAIN))
                by_norm, maximum, shift, sums, divide = softmax_pieces(i - 1, (i + 1) % 2)
                t0 = T_PREP + T_STEP * i - T_HEADS + (2 if last else 4)

                def out(j):
                    residual(i - 1, j, one_bank=True)

                pieces = {0: (by_norm, 0, maximum, 0), 1: (shift, 0, by_norm, 1), 2: (maximum, 1, shift, 1),
                          3: (sums, 0), 4: (divide, 0), 5: (sums, 1), 6: (divide, 1, by_norm, 2),
                          7: (maximum, 2, shift, 2, out, 0), 8: (by_norm, 3, maximum, 3), 9: (sums, 2),
                          10: (divide, 2, out, 1), 11: (shift, 3), 13: (sums, 3), 14: (divide, 3, out, 2)}
                if not first_:
                    dve.wait_ge(s_ring.free, S_PREP + S_STEP * (i - 1) + 8)
                for h in range(H0):
                    dve.tensor_copy(qT[:, h % 3, :], qr.read(dve)[:]).then_inc(q_ring.free, 1)
                    if not first_:
                        run = pieces.get(h, ())
                        for piece, j in zip(run[0::2], run[1::2]):
                            if piece is divide:
                                divide(j, t0 + 2 * j if j else None)
                            else:
                                piece(j)
                    if h == 12 and not last:
                        row_stats(i + 1)
                    if h == 15 and not last:
                        row_roots(EPS0)
                if not last:
                    keys_in()
                if not first_:
                    out(3)
                values_in()
                dve.wait_ge(q_norm, i + 1)
                ch.add(dve.tensor_scalar(qvar[:], n_bank[:, 0:G * H0], 1.0 / D0, EPS0, ALU.mult, ALU.add))
                if not last:
                    row_apply(i + 1)
                    key_norm(5)
                ch.wait()
                inverse_root(rq[:], qvar[:], G * H0)
                assert first_ or last or ch.k == STEP_CHAIN, (ch.k, STEP_CHAIN)

            dve.wait_ge(gates_ready, 1)
            dve.wait_ge(x_rest_loaded, 16)
            step(0, True, False)
            with dve.Fori(1, NG - 1) as i:
                step(i, False, False)
            step(NG - 1, False, True)

            normed(0, EPS0)
            def shared_product(i):
                qr.at(Q2, QR, i)
                for half in range(2):
                    dve.wait_ge(s_ring.free, S2 + SR * i + half + 1)
                    h = slice(half * 2 * P, (half + 1) * 2 * P)
                    dve.tensor_tensor(sh_h[:, h], sh_g[:, h], qr.read(dve)[0:I0, 0:2 * P],
                                      ALU.mult).then_inc(q_ring.free, 1)

            dve.wait_ge(s_ring.free, S_PREP + S_STEP * (NG - 1) + 8)
            by_norm, maximum, shift, sums, divide = softmax_pieces(NG - 1, (NG - 1) % 2)
            T_LAST = T2 - T_HEADS + TRF
            for j in range(G):
                by_norm(j)
                maximum(j)
                shift(j)
                if j:
                    sums(j - 1)
                    divide(j - 1, T_LAST + 2 * (j - 1) if j > 1 else None)
                if j > 1:
                    residual(NG - 1, j - 2, one_bank=True)
                if j == 2:
                    shared_product(0)
            sums(G - 1)
            divide(G - 1, T_LAST + 2 * (G - 1))
            residual(NG - 1, G - 2, one_bank=True)
            residual(NG - 1, G - 1, one_bank=True)
            dve.wait_ge(o_read, 2 + NT)
            dve.drain().then_inc(done1["dve"], 1)

            def tiles(v, n=E0):
                return v.rearrange("p (j e) -> p j e", j=G)

            def group_max(dst, v):
                return dve.tensor_reduce(dst, v.rearrange("p (g e) -> p g e", e=8), AX.X, ALU.max)

            def wide(v, n=8):
                return v.unsqueeze(2).to_broadcast([P, v.shape[1], n])

            def by8(v):
                return v.rearrange("p (g e) -> p g e", e=8)

            def rank_below(dst, v, count, t0, t1):
                a0 = v.unsqueeze(2).to_broadcast([P, G, 8, 8])
                a1 = v.unsqueeze(3).to_broadcast([P, G, 8, 8])
                r0, r1 = (t.rearrange("p (j g k) -> p j g k", j=G, g=8) for t in (t0, t1))
                ch.add(dve.tensor_tensor(r0, a0, a1, ALU.is_gt))
                ch.add(dve.tensor_tensor(r1, a0, a1, ALU.is_ge))
                ch.wait()
                ch.add(dve.tensor_tensor(r1, r1, before[:].unsqueeze(1).to_broadcast([P, G, 8, 8]), ALU.mult))
                ch.wait()
                ch.add(dve.tensor_tensor(t0, t0, t1, ALU.max))
                ch.wait()
                ch.add(dve.tensor_reduce(t1[:, 0:8 * G], by8(t0), AX.X, ALU.add))
                ch.wait()
                ch.add(dve.tensor_scalar(dst, t1[:, 0:8 * G], count - 0.5, None, ALU.is_lt))
                ch.wait()

            dve.wait_ge(r_const, 3)
            dve.wait_ge(r_loaded, 64)
            dve.wait_ge(zeroed, 16 * NT)
            for e in done1.values():
                dve.wait_ge(e, 1)
            ROUTE_CHAIN = NORMED_CHAIN + 24 + 2 * G
            ROUTE_BASE = PREP_CHAIN + STEP_CHAIN * NG - KEY_CHAIN

            def route(i, last):
                ch.at(ROUTE_BASE + ROUTE_CHAIN * i)
                dve.wait_ge(t_ring.free, T2 + TRF + TR * i)
                if not last:
                    normed(i + 1, EPS0)
                dve.wait_ge(table_stored, 16 * (i + 1))
                sig, sc, eq, oth, msk, rep, t0, t1, sel = [sigs[:, i % 2, :]] + part[1:8] + part[0:1]
                m = part[10]
                m1, cnt, m2, dup, gs, gm = (m[:, 32 * n:32 * n + 32] for n in range(6))
                top, sums = part[11][:, 0:32], part[11][:, 32:32 + G]
                ch.add(dve.tensor_tensor(tiles(sc), tiles(sig), e_bias[:].unsqueeze(1).to_broadcast([P, G, E0]),
                                         ALU.add))
                ch.wait()
                ch.add(group_max(m1, sc))
                ch.wait()
                ch.add(dve.tensor_tensor(by8(eq), by8(sc), wide(m1), ALU.is_equal))
                ch.wait()
                ch.add(dve.tensor_reduce(cnt, by8(eq), AX.X, ALU.add))
                ch.add(dve.scalar_tensor_tensor(out=oth, in0=eq, scalar=-FAR, in1=sc, op0=ALU.mult, op1=ALU.add))
                ch.wait()
                ch.add(group_max(m2, oth))
                ch.add(dve.tensor_scalar(dup, cnt, 1.5, 1.0, ALU.is_ge, ALU.subtract))
                ch.wait()
                ch.add(dve.scalar_tensor_tensor(out=dup, in0=dup, scalar=FAR, in1=m1, op0=ALU.mult, op1=ALU.add))
                ch.wait()
                ch.add(dve.tensor_tensor(m2, m2, dup, ALU.max))
                ch.wait()
                ch.add(dve.tensor_tensor(gs, m1, m2, ALU.add))
                ch.wait()
                rank_below(gm, gs.rearrange("p (j g) -> p j g", j=G), 4, t0, t1)
                ch.add(dve.tensor_tensor(by8(msk), by8(sc), wide(gm), ALU.mult))
                ch.wait()
                dve.sem_inc(wait_done, 1)
                for j in range(G):
                    ch.add(dve.max(top[:, 8 * j:8 * j + 8], tiles(msk)[:, j, :]))
                ch.wait()
                dve.sem_inc(wait_done, 1)
                for j in range(G):
                    ch.add(dve.match_replace(tiles(rep)[:, j, :], top[:, 8 * j:8 * j + 8], tiles(msk)[:, j, :],
                                             -FAR))
                ch.wait()
                ch.add(dve.tensor_tensor(sel, rep, msk, ALU.not_equal))
                ch.wait()
                ch.add(dve.tensor_tensor(t0, sel, sig, ALU.mult))
                ch.add(dve.tensor_tensor_scan(t1, sel, none[:], 0.0, ALU.add, ALU.add))
                ch.wait()
                ch.add(dve.tensor_reduce(sums, tiles(t0), AX.X, ALU.add))
                ch.add(dve.scalar_tensor_tensor(
                    out=tiles(t1), in0=tiles(t1), scalar=-1.0,
                    in1=key_base[:, bass.ds(G * i, G)].unsqueeze(2).to_broadcast([P, G, E0]),
                    op0=ALU.mult, op1=ALU.add))
                ch.wait()
                for half in range(2):
                    dve.tensor_tensor(keys2[:, :, half, :], tiles(t1), tiles(sel), ALU.mult).then_inc(key_ready, 1)
                ch.add(dve.tensor_scalar(sums, sums, 1e-20, None, ALU.add))
                ch.wait()
                ch.add(dve.reciprocal(sums, sums))
                ch.wait()
                dve.scalar_tensor_tensor(out=xw[:, i % 2, :, DIM:ROW], in0=tiles(t0), scalar=2.5,
                                         in1=sums.unsqueeze(2).to_broadcast([P, G, E0]), op0=ALU.mult,
                                         op1=ALU.mult).then_inc(rows_ready, 1)
                for j in range(G):
                    residual(NG + i, j, i, 2)
                if not last:
                    shared_product(i + 1)
                assert last or ch.k == ROUTE_CHAIN

            ch.at(ROUTE_BASE)
            none = part[12]
            ch.add(dve.memset(none, 0.0))
            ch.wait()
            ROUTE_BASE += 1
            with dve.Fori(0, NG - 1) as i:
                route(i, False)
            route(NG - 1, True)

            sl = Chain(dve, slot_chain)
            dve.wait_ge(t_ring.free, T2 + TR * NG)

            def largest(dst, src):
                for r in range(CAP // 8):
                    sl.add(dve.max(dst[:, 8 * r:8 * r + 8], src))
                    sl.wait()
                    if r < CAP // 8 - 1:
                        sl.add(dve.match_replace(src, dst[:, 8 * r:8 * r + 8], src, 0.0))
                        sl.wait()

            largest(cand[:, 0:CAP], keyT[:, 0:T // 2])
            dve.drain().then_inc(cand_ready, 1)
            dve.wait_ge(cand_moved, 16)
            largest(slots[:], cand[0:E0, :])
            dve.drain().then_inc(slots_ready, 1)
            dve.wait_ge(t_ring.free, T3)
            sl.add(dve.tensor_scalar(part[0][:, 0:E0], slotsT[:], -1.0, float(K0 * T), ALU.mult, ALU.add))
            sl.add(dve.tensor_scalar(part[1][:, 0:E0], slotsT[:], 0.0, None, ALU.is_equal))
            sl.wait()
            sl.add(dve.tensor_copy(src_idx[:], part[0][:, 0:E0]))
            sl.add(dve.tensor_tensor(part[1][:, 0:E0], part[1][:, 0:E0], spare[:], ALU.mult))
            sl.wait()
            sl.add(dve.tensor_tensor(dst_idx[:], part[0][:, 0:E0], part[1][:, 0:E0], ALU.add))
            sl.add(dve.tensor_scalar(src_idx[:], src_idx[:], 3, None, ALU.logical_shift_right))
            sl.wait()

            def stage_source(i, q):
                dve.tensor_copy(src_now[:, q, :], src_idx[:, bass.ds(8 * i + 2 * q, 2)]).then_inc(idx_now, 1)

            for q in range(3):
                stage_source(0, q)

            def experts(i, last):
                qr.at(Q3, 4, i)
                for q in range(4):
                    if not (last and q):
                        stage_source(i + (q + 3) // 4, (q + 3) % 4)
                    dve.wait_ge(s_ring.free, S3 + 4 * i + q + 1)
                    b = qr.read(dve)
                    dve.tensor_tensor(act_h[:, q % 2, :], act_g[:, q % 2, :], b[0:I0, 0:2 * P],
                                      ALU.mult).then_inc(q_ring.free, 1)
                    if i is not first_step:
                        dve.wait_ge(y_stored[q], 32 * i)
                    dve.tensor_copy(dst_now[:, q, :], dst_idx[:, bass.ds(8 * i + 2 * q, 2)]).then_inc(idx_ready, 1)
                    dve.wait_ge(y_full, 4 * i + q + 1)
                    for e in range(2):
                        dve.tensor_scalar(y[:, q, e, :], o_banks[q % 2][:, e * DIM:(e + 1) * DIM],
                                          xg[:, q, e, bass.ds(DIM + 8 * i + 2 * q + e, 1)], None,
                                          ALU.mult).then_inc(y_ready if e else idx_ready, 1)

            first_step = 0
            experts(0, False)
            with dve.Fori(1, NQ - 1) as i:
                experts(i, False)
            experts(NQ - 1, True)


            def project(i, par):
                b = qr.read(dve)[:].rearrange("p (s h d) -> p s h d", s=2, h=H1)
                bias = bkv1[:].rearrange("p (s h d) -> p s h d", s=2, h=H1)

                def values(o, bt, v_):
                    rows = slice(o * SKV, (o + 1) * SKV)
                    return dve.tensor_tensor(
                        v_blocks[rows, par, bt, :, o, :], v_[rows].rearrange("p (q o) d -> p q o d", o=2)[:, :, o, :],
                        bias[rows, 1].rearrange("p (q o) d -> p q o d", o=2)[:, :, o, :], ALU.add)

                for o in range(2):
                    values(o, o, b[:, 1])
                dve.tensor_tensor(qk1[:, G * H1:QK, :], b[:, 0], bias[:, 0], ALU.add).then_inc(q_ring.free, 1)
                b = qr.read(dve)[:, 0:DIM].rearrange("p (h d) -> p h d", h=H1)
                values(0, 1, b)
                values(1, 0, b).then_inc(q_ring.free, 1)
                for half in range(2):
                    dve.tensor_tensor(
                        qk1[:, 2 * half * H1:2 * (half + 1) * H1, :].rearrange("p (j h) d -> p j (h d)", j=2),
                        qr.read(dve)[:].rearrange("p (j n) -> p j n", j=2),
                        bq1[:].unsqueeze(1).to_broadcast([P, 2, DIM]), ALU.add).then_inc(q_ring.free, 1)

            def centre(i):
                qr.evacuated(dve)
                ch.add(dve.tensor_reduce(qk1_stat[:, 0, :], qk1[:], AX.X, ALU.add))
                ch.wait()
                dve.scalar_tensor_tensor(out=qk1[:], in0=over_head(qk1_stat[:, 0, :]), scalar=-1.0 / D1, in1=qk1[:],
                                         op0=ALU.mult, op1=ALU.add).then_inc(q1_centred, 1)

            def deviation(i):
                dve.wait_ge(q1_squared, i + 1)
                ch.add(dve.tensor_reduce(qk1_stat[:, 0, :], qk1_sq[:], AX.X, ALU.add))
                ch.wait()
                ch.add(dve.tensor_scalar(qk1_stat[:, 0, :], qk1_stat[:, 0, :], 1.0 / D1, EPS1, ALU.mult, ALU.add))
                ch.wait()
                inverse_root(qk1_stat[:, 1, :], qk1_stat[:, 0, :], QK)

            def scale(lo, hi, w, ready):
                v, n = qk1[:, lo:hi, :], hi - lo
                ch.add(dve.tensor_tensor(v, v, over_head(qk1_stat[:, 1, lo:hi]), ALU.mult))
                ch.wait()
                ch.add(dve.tensor_tensor(v, v, w[:, 0, :].unsqueeze(1).to_broadcast([P, n, D1]), ALU.mult))
                ch.wait()
                dve.tensor_tensor(v, v, w[:, 1, :].unsqueeze(1).to_broadcast([P, n, D1]), ALU.add).then_inc(ready, 1)

            def scale_keys():
                scale(G * H1, QK, kn, k1_ready)

            def scale_queries():
                scale(0, G * H1, qn, q1_ready)

            FRONT_CHAIN = NORMED_CHAIN + 1 + 2 + ROOT_CHAIN + 4

            SPANS = ((0, MAIN), (MAIN, SKV))

            def soft_spans(j):
                s_ = soft[:, j, :].rearrange("p (h k) -> p h k", h=H1)
                return [(s_[:, :, lo:hi], hi - lo, slice(n * H1, (n + 1) * H1)) for n, (lo, hi) in enumerate(SPANS)]

            def soft2_front(i, j):
                dve.wait_ge(s_ring.free, S4 + SA * i + 2 * j + 2)
                for v, n, at in soft_spans(j):
                    ch.add(dve.tensor_reduce(small[:, j, 0, at], v, AX.X, ALU.max))
                ch.wait()
                for v, n, at in soft_spans(j):
                    dve.tensor_tensor(v, v, over_head(small[:, j, 0, at], n), ALU.subtract).then_inc(shifted, 1)

            def soft2_back(i, j):
                dve.wait_ge(exp_done, NT + G * i + j + 1)
                for v, n, at in soft_spans(j):
                    ch.add(dve.tensor_reduce(small[:, j, 1, at], v, AX.X, ALU.add))
                ch.wait()
                ch.add(dve.reciprocal(small[:, j, 1, :], small[:, j, 1, :]))
                ch.wait()
                for v, n, at in soft_spans(j):
                    dve.tensor_tensor(v, v, over_head(small[:, j, 1, at], n), ALU.mult).then_inc(attn_ready, 1)

            def context_out(i, j):
                dve.wait_ge(c1_full, G * i + j + 1)
                dve.tensor_copy(c1[:, j % 2, :], o_banks[j % 2][:, 0:DIM]).then_inc(c1_ready, 1)

            def attention_out(i, j):
                dve.wait_ge(o_full, G * (2 * NG + i) + j + 1)
                xj = x[:, G * i + j, :]
                dve.scalar_tensor_tensor(out=xj, in0=o_banks[j % 2][:, DIM:2 * DIM], scalar=gates[:, 1:2], in1=xj,
                                         op0=ALU.mult, op1=ALU.add).then_inc(o_read, 1)

            def attention(i, last):
                ch.at(ATT_BASE + FRONT_CHAIN + ATT_CHAIN * i)
                qr.at(Q4 + QA, QA, i)
                if not last:
                    dve.wait_ge(y2_used, G * (i + 2))
                    normed(i + 1, EPS0)
                soft2_front(i, 0)
                soft2_front(i, 1)
                soft2_back(i, 0)
                if not last:
                    project(i + 1, (i + 1) % 2)
                soft2_front(i, 2)
                soft2_back(i, 1)
                if not last:
                    centre(i + 1)
                soft2_front(i, 3)
                context_out(i, 0)
                soft2_back(i, 2)
                context_out(i, 1)
                if not last:
                    deviation(i + 1)
                attention_out(i, 0)
                soft2_back(i, 3)
                if not last:
                    scale_keys()
                context_out(i, 2)
                attention_out(i, 1)
                if not last:
                    scale_queries()
                context_out(i, 3)
                attention_out(i, 2)
                attention_out(i, 3)
                assert last or ch.k == ATT_CHAIN, ch.k

            ATT_BASE = ROUTE_BASE + ROUTE_CHAIN * NG - NORMED_CHAIN + 1 + G
            ATT_CHAIN = FRONT_CHAIN + 5 * G
            ch.at(ATT_BASE - 1 - G)
            for q in range(4):
                dve.wait_ge(y_stored[q], 32 * NQ)
            dve.wait_ge(w3_loaded, 16 * W3)
            ch.add(dve.memset(v_blocks[:], 0.0))
            ch.wait()
            for j in range(G):
                dve.wait_ge(y2_loaded[j % 2], 16 * (j // 2 + 1))
                ch.add(dve.tensor_reduce(y2_sum[:, j % 2, :], y2_rows[:, j % 2].rearrange(
                    "p (k d) -> p d k", k=K0), AX.X, ALU.add))
                ch.wait()
                dve.scalar_tensor_tensor(out=x[:, j, :], in0=y2_sum[:, j % 2, :], scalar=gates[:, 2:3],
                                         in1=x[:, j, :], op0=ALU.mult, op1=ALU.add).then_inc(y2_used, 1)
            dve.wait_ge(y2_used, G)
            normed(0, EPS0)
            qr.at(Q4)
            project(0, 0)
            centre(0)
            deviation(0)
            scale_keys()
            scale_queries()
            assert ch.k == 1 + G + FRONT_CHAIN
            with dve.Fori(0, NG - 1) as i:
                attention(i, False)
            attention(NG - 1, True)

            def gating(i):
                t0, t1 = rank_t[:, 0, :], rank_t[:, 1, :]
                lg, mx, sm = gate_s[:, 0, :], gate_s[:, 1, 0:G], gate_s[:, 2, 0:G]

                def wide_(v):
                    return v.unsqueeze(2).to_broadcast([P, G, E1])

                dve.wait_ge(t_ring.free, T5 + TM * i + 4)
                ch.add(dve.tensor_reduce(mx, by8(logits[:]), AX.X, ALU.max))
                ch.wait()
                dve.tensor_tensor(by8(lg), by8(logits[:]), wide_(mx), ALU.subtract).then_inc(gate_shifted, 1)
                dve.wait_ge(gate_exp, i + 1)
                ch.add(dve.tensor_reduce(sm, by8(lg), AX.X, ALU.add))
                ch.wait()
                ch.add(dve.reciprocal(sm, sm))
                ch.wait()
                ch.add(dve.tensor_tensor(by8(lg), by8(lg), wide_(sm), ALU.mult))
                ch.wait()
                rank_below(gate_s[:, 1, :], by8(lg), 2, t0, t1)
                ch.add(dve.tensor_tensor(combine_w[:, :, 0:E1], by8(lg), by8(gate_s[:, 1, :]), ALU.mult))
                ch.wait()

            def products(i, j):
                for p in range(5):
                    dve.wait_ge(s_ring.free, S5 + SM * i + 5 * j + p + 1)
                    b = qr.read(dve)
                    for e in range(2):
                        at = (2 * p + e) * F1
                        ins = dve.scalar_tensor_tensor(
                            out=act_v[:, j % 2, at:at + F1], in0=sg[:, (j + p) % 2, e * F1:(e + 1) * F1],
                            scalar=combine_w[:, j, 2 * p + e:2 * p + e + 1], in1=b[:, e * F1:(e + 1) * F1],
                            op0=ALU.mult, op1=ALU.mult)
                    ins.then_inc(q_ring.free, 1)

            def mixture(i, last):
                ch.at(MIX_BASE + MIX_CHAIN * i)
                qr.at(Q5, QM, i)
                gating(i)
                products(i, 0)
                products(i, 1)
                for j in range(G):
                    if j == 2 and not last:
                        dve.wait_ge(t_ring.full, T5 + TM * i + 2)
                        normed(i + 1, EPS0)
                    residual(3 * NG + i, j, i, 3)
                    if j + 2 < G:
                        products(i, j + 2)
                assert last or ch.k == MIX_CHAIN, ch.k

            MIX_BASE = ATT_BASE + ATT_CHAIN * NG + NORMED_CHAIN + 1
            MIX_CHAIN = 5 + 6 + NORMED_CHAIN
            ch.at(MIX_BASE - NORMED_CHAIN - 1)
            ch.add(dve.memset(combine_w[:, :, E1:E1 + 2], 1.0))
            ch.wait()
            dve.wait_ge(o_read, 2 + 3 * NT)
            normed(0, EPS0)
            with dve.Fori(0, NG - 1) as i:
                mixture(i, False)
            mixture(NG - 1, True)
            dve.drain().then_inc(x_done, 1)

        @block.scalar
        def _(act):
            sr, tr, qr = s_ring.end(), t_ring.end(), q_ring.end()
            act.dma_start(gates[:, 0:2], a["g_xattn"].partition_broadcast(P)).then_inc(gates_loaded, 16)
            act.dma_start(gates[:, 2:4], a["g_ffn"].partition_broadcast(P)).then_inc(gates_loaded, 16)
            act.dma_start(gqk[:, 0:1], a["L0_xattn_gq"].unsqueeze(1)).then_inc(gqk_loaded, 16)
            act.dma_start(gqk[:, 1:2], a["L0_xattn_gk"].unsqueeze(1)).then_inc(gqk_loaded, 16)
            act.dma_start(rwT[:], a["L0_ffn_router_weightT"].rearrange("(c p) e -> p c e", p=P)).then_inc(r_loaded, 16)
            act.dma_start(e_bias[:], a["L0_ffn_e_bias"].partition_broadcast(P)).then_inc(r_loaded, 16)
            act.dma_start(sh_gu[:], a["L0_ffn_sh_gu"].rearrange("(c p) e -> p c e", p=P)).then_inc(r_loaded, 16)
            act.dma_start(sh_dn[:], a["L0_ffn_sh_down"]).then_inc(r_loaded, 16)
            act.wait_ge(gates_loaded, 32)
            act.activation(gates[:], gates[:], ACT.Tanh).then_inc(gates_ready, 1)
            act.wait_ge(gqk_ready, 1)

            def context_in(par):
                act.activation(ctxK[:], tr.read(act)[:, 0:P], ACT.Copy).then_inc(t_ring.free, 1)
                b = tr.read(act)
                act.activation(ctxV[:, par, 0:P], b[:, 0:P], ACT.Copy)
                act.activation(ctxV[:, par, P:P + SKV], b[:, 0:SKV], ACT.Copy).then_inc(t_ring.free, 1)

            def keys_in():
                for g in range(4):
                    act.activation(kT[:, 4 * g:4 * g + 4, :], tr.read(act)[:].rearrange(
                        "p (h k) -> p h k", h=4), ACT.Copy, scale=gscale[:]).then_inc(t_ring.free, 1)

            def values_in():
                for p in range(8):
                    b = sr.read(act)
                    lo = vw[0:SKV, :, p, :]
                    act.activation(lo, b[0:SKV, :].rearrange("p (b n) -> p b n", b=2), ACT.Copy)
                    act.activation(vw[SKV:P, 0, p, :], b[SKV:P, DIM:2 * DIM], ACT.Copy)
                    act.activation(vw[SKV:P, 1, p, :], b[SKV:P, 0:DIM], ACT.Copy).then_inc(s_ring.free, 1)

            def exponential(i, j, par):
                act.wait_ge(shifted, G * i + j + 1)
                v = raw[:, par, j, :]
                act.activation(v, v, ACT.Exp).then_inc(exp_done, 1)

            def attn_out(j):
                for g in range(2):
                    act.activation(attnT[:, j % 2, 4 * g:4 * g + 4, :], tr.read(act)[:].rearrange(
                        "p (h t) -> p h t", h=4), ACT.Copy).then_inc(t_ring.free, 1)

            context_in(0)
            keys_in()

            def step(i, first_, last):
                qr.at(Q_PREP, Q_STEP, i)
                sr.at(S_PREP, S_STEP, i)
                tr.at(T_PREP - (0 if first_ else T_HEADS), T_STEP, i)
                for c in range(C):
                    act.activation(xnT[:, c, :], tr.read(act)[:], ACT.Copy).then_inc(t_ring.free, 1)
                if not last:
                    context_in((i + 1) % 2)

                def scores_out(pair):
                    b = sr.read(act)
                    act.activation(raw[:, i % 2, :, 2 * pair * SKV:2 * (pair + 1) * SKV],
                                   b[:].rearrange("p (j n) -> p j n", j=G), ACT.Copy).then_inc(s_ring.free, 1)

                exps, outs = {2: 0, 3: 1, 8: 2, 12: 3}, {5: 0, 8: 1, 12: 2, 15: 3}
                for h in range(H0):
                    qr.skip(1)
                    qr.evacuated(act)
                    act.activation(q2[h % 3], qT[:, h % 3, :], ACT.Square).then_inc(q2_ready, 1)
                    if not first_ and h in outs:
                        attn_out(outs[h])
                    if not first_ and h in exps:
                        exponential(i - 1, exps[h], (i + 1) % 2)
                    if h >= 3 and h % 2:
                        scores_out((h - 3) // 2)
                scores_out(H0 // 2 - 1)
                values_in()
                if not last:
                    keys_in()

            step(0, True, False)
            with act.Fori(1, NG - 1) as i:
                step(i, False, False)
            step(NG - 1, False, True)
            def route_front(i):
                sr.at(S2, SR, i)
                for c in range(C):
                    act.activation(xnT[:, c, :], tr.read(act)[:], ACT.Copy).then_inc(t_ring.free, 1)
                act.wait_ge(table_stored, 16 * i if i is not first_group else 16)
                act.activation(xw[:, i % 2, :, 0:DIM], xn[:], ACT.Copy)
                act.activation(sigs[:, i % 2, :], tr.read(act)[:, 0:G * E0], ACT.Sigmoid).then_inc(t_ring.free, 1)
                if i is not first_group:
                    act.wait_ge(q_ring.free, Q2 + QR * i)
                for half in range(2):
                    act.activation(sh_g[:, half * 2 * P:(half + 1) * 2 * P], sr.read(act)[0:I0, 0:2 * P],
                                   ACT.Silu).then_inc(s_ring.free, 1)

            first_group = 0
            exponential(NG - 1, 0, (NG - 1) % 2)
            tr.at(T2 - T_HEADS)
            route_front(first_group)
            for j in range(G):
                if j + 1 < G:
                    exponential(NG - 1, j + 1, (NG - 1) % 2)
                attn_out(j)
            act.drain().then_inc(done1["act"], 1)
            for e in done1.values():
                act.wait_ge(e, 1)

            def route(i, half, last):
                tr.at(T2 + TRF, TR, i)
                if not last:
                    route_front(i + 1)
                rows = slice(half * E0, (half + 1) * E0)
                act.activation(keyT[rows, bass.ds(G * P * (i - half * (NG // 2)), G * P)], tr.read(act)[rows, :],
                               ACT.Copy).then_inc(t_ring.free, 1)

            with act.Fori(0, NG // 2) as i:
                route(i, 0, False)
            with act.Fori(NG // 2, NG - 1) as i:
                route(i, 1, False)
            route(NG - 1, 1, True)
            tr.at(T2 + TR * NG)
            act.activation(slotsT[:], tr.read(act)[:, 0:E0], ACT.Copy).then_inc(t_ring.free, 1)

            def transposed(q):
                act.activation(xgT[:, q % 2], tr.read(act)[:].rearrange(
                    "p (e c t) -> p e c t", e=2, c=C), ACT.Copy).then_inc(t_ring.free, 1)

            def experts(i, last):
                tr.at(T3 + 1, 4, i)
                sr.at(S3, 4, i)
                for q in range(4):
                    act.activation(act_g[:, q % 2, :], sr.read(act)[0:I0, 0:2 * P],
                                   ACT.Silu).then_inc(s_ring.free, 1)
                    if not (last and q == 3):
                        transposed(q + 1)

            tr.at(T3)
            transposed(0)
            with act.Fori(0, NQ - 1) as i:
                experts(i, False)
            experts(NQ - 1, True)

            def front(i):
                b = tr.read(act)
                for kind, (lo, hi) in enumerate(((0, MAIN), (MAIN, SKV))):
                    dst = ctx1T[:, kind, :].rearrange("p (b k) -> p b k", b=3)
                    src = b[:, 0:P].rearrange("p (b k) -> p b k", b=2)
                    act.activation(dst[:, 0:2, lo:hi], src[:, :, lo:hi], ACT.Copy)
                    ins = act.activation(dst[:, 2, lo:hi], src[:, 0, lo:hi], ACT.Copy)
                ins.then_inc(t_ring.free, 1)
                for c in range(C):
                    act.activation(xnT[:, c, :], tr.read(act)[:], ACT.Copy).then_inc(t_ring.free, 1)

            def squares(i):
                act.wait_ge(q1_centred, i + 1)
                act.activation(qk1_sq[:], qk1[:], ACT.Square).then_inc(q1_squared, 1)

            def heads_in():
                act.activation(k1T[:], tr.read(act)[:, 0:C * P].rearrange("p (c t) -> p c t", c=C),
                               ACT.Copy).then_inc(t_ring.free, 1)
                for c in range(C):
                    act.activation(q1T[:, c, :], tr.read(act)[:], ACT.Copy).then_inc(t_ring.free, 1)

            def scores_in(i):
                for j in range(G):
                    for c in range(C):
                        act.activation(soft[:, j, c * 512:(c + 1) * 512], sr.read(act)[:], ACT.Copy,
                                       scale=float(D1) ** -0.5).then_inc(s_ring.free, 1)

            def attention(i, last):
                sr.at(S4 + SA, SA, i)
                tr.at(T4 + TF, TA, i)
                if not last:
                    front(i + 1)

                def exponential(j):
                    act.wait_ge(shifted, NT + 2 * (G * i + j) + 2)
                    act.activation(soft[:, j, :], soft[:, j, :], ACT.Exp).then_inc(exp_done, 1)

                def attn_out(j):
                    for g in range(2):
                        act.activation(attnT[:, j % 2, 4 * g:4 * g + 4, :], tr.read(act)[:].rearrange(
                            "p (h t) -> p h t", h=4), ACT.Copy).then_inc(t_ring.free, 1)

                def context_out(j):
                    act.activation(c1T[:, j % 2], tr.read(act)[:, 0:DIM].rearrange("p (c t) -> p c t", c=C),
                                   ACT.Copy).then_inc(t_ring.free, 1)

                exponential(0)
                exponential(1)
                attn_out(0)
                exponential(2)
                attn_out(1)
                if not last:
                    squares(i + 1)
                exponential(3)
                context_out(0)
                attn_out(2)
                context_out(1)
                attn_out(3)
                context_out(2)
                if not last:
                    heads_in()
                context_out(3)
                if not last:
                    scores_in(i + 1)

            act.wait_ge(mask_step, 4)
            sr.at(S4)
            tr.at(T4)
            front(0)
            squares(0)
            heads_in()
            scores_in(0)
            with act.Fori(0, NG - 1) as i:
                attention(i, False)
            attention(NG - 1, True)

            def mixture(i):
                sr.at(S5, SM, i)
                tr.at(T5, TM, i)
                for c in range(C):
                    act.activation(xnT[:, c, :], tr.read(act)[:], ACT.Copy).then_inc(t_ring.free, 1)
                for half in range(2):
                    act.activation(logits[:, half * 2 * E1:(half + 1) * 2 * E1], tr.read(act)[:, 0:2 * E1],
                                   ACT.Copy).then_inc(t_ring.free, 1)
                act.wait_ge(gate_shifted, i + 1)
                act.activation(gate_s[:, 0, :], gate_s[:, 0, :], ACT.Exp).then_inc(gate_exp, 1)

                def silu(j):
                    for p in range(5):
                        b = sr.read(act)
                        act.wait_ge(q_ring.free, Q5 + QM * i + 5 * j + p - 1)
                        act.activation(sg[:, (j + p) % 2, :], b[:, 0:2 * F1], ACT.Silu).then_inc(s_ring.free, 1)

                def act_out(j):
                    for g in range(4):
                        n = min(4, FC - 4 * g)
                        act.activation(attn_flat[:, 4 * g:4 * g + n, :], tr.read(act)[:, 0:n * P].rearrange(
                            "p (f t) -> p f t", f=n), ACT.Copy).then_inc(t_ring.free, 1)

                silu(0)
                silu(1)
                for j in range(G):
                    act_out(j)
                    if j + 2 < G:
                        silu(j + 2)

            attn_flat = attnT[:].rearrange("p b f t -> p (b f) t")
            with act.Fori(0, NG) as i:
                mixture(i)

        @block.tensor
        def _(pe):
            qr, sr, tr = q_ring.end(), s_ring.end(), t_ring.end()

            def context_in(m):
                pe.wait_ge(ctx_loaded, 16 * (m + 1))
                for _ in range(2):
                    pe.transpose(tr.fill(pe)[:, 0:P], ctx_rows[:], ident[:]).then_inc(t_ring.full, 1)

            def keys():
                for g in range(4):
                    pe.matmul(qr.fill(pe)[:], ctxK[:], wk[:, 512 * g:512 * (g + 1)],
                              start=True, stop=True).then_inc(q_ring.full, 1)

            def transpose_keys(m):
                pe.wait_ge(kn_ready, m + 1)
                for g in range(4):
                    b = tr.fill(pe)
                    for k in range(4):
                        mm = pe.transpose(b[:, k * P:(k + 1) * P], ksb[:, 4 * g + k, :], ident[:])
                    mm.then_inc(t_ring.full, 1)

            def values(par):
                for g in range(4):
                    b = qr.fill(pe)
                    for k in range(4):
                        h = 4 * g + k
                        at = SKV * (h % 2)
                        mm = pe.matmul(b[:, k * P:(k + 1) * P], wv[:, h * D0:(h + 1) * D0],
                                       ctxV[:, par, at:at + P], start=True, stop=True)
                    mm.then_inc(q_ring.full, 1)
                for p in range(8):
                    if p % 2 == 0:
                        qr.evacuated(pe, 4 - p // 2)
                    b = sr.fill(pe)
                    for o in range(2):
                        mm = pe.matmul(b[:, o * DIM:(o + 1) * DIM], vT[:, 2 * p + o, :], wo[:, 2 * p + o, :],
                                       start=True, stop=True)
                    mm.then_inc(s_ring.full, 1)

            pe.wait_ge(const_ready, 2)
            context_in(0)
            tr.evacuated(pe)
            pe.wait_ge(wk_loaded, 16)
            keys()
            transpose_keys(0)

            def transpose_xn(m, src=xn):
                pe.wait_ge(xn_ready, G * (m + 1))
                for c in range(C):
                    b = tr.fill(pe)
                    for j in range(G):
                        mm = pe.transpose(b[:, j * P:(j + 1) * P], src[:, j, c * P:(c + 1) * P], ident[:])
                    mm.then_inc(t_ring.full, 1)
                tr.evacuated(pe)

            def transpose_attn(i, j):
                pe.wait_ge(attn_ready, G * i + j + 1)
                for g in range(2):
                    b = tr.fill(pe)
                    for k in range(4):
                        at = (4 * g + k) * P
                        mm = pe.transpose(b[:, k * P:(k + 1) * P], prob[:, at:at + P], ident[:])
                    mm.then_inc(t_ring.full, 1)

            def output(i, j):
                tr.evacuated(pe)
                pe.wait_ge(o_read, G * i + j + 2)
                for p in range(8):
                    mm = pe.matmul(o_banks[0][:, 0:DIM], attnT[:, j % 2, p, :], vw[:, j // 2, p, :],
                                   start=(p == 0), stop=(p == 7))
                mm.then_inc(o_full, 1)

            def step(i, first_, last):
                qr.at(Q_PREP, Q_STEP, i)
                sr.at(S_PREP, S_STEP, i)
                tr.at(T_PREP - (0 if first_ else T_HEADS), T_STEP, i)
                transpose_xn(i)
                if not last:
                    context_in(i + 1)
                s_bank = [None]

                def scores(h, done):
                    qr.evacuated(pe, done - h)
                    pe.wait_ge(q2_ready, H0 * i + h + 1)
                    place = [(h ^ 1) if j >= 2 else h for j in range(G)]
                    for j in range(G):
                        mm = pe.matmul(n_bank[:, j * H0 + place[j]:j * H0 + place[j] + 1],
                                       q2[h % 3][:, j * P:(j + 1) * P], ones[:, 0:1], start=True, stop=True)
                    if h == H0 - 1:
                        mm.then_inc(q_norm, 1)
                    if h % 2 == 0:
                        s_bank[0] = sr.fill(pe)
                    for j in range(G):
                        at = (2 * j + place[j] % 2) * SKV
                        mm = pe.matmul(s_bank[0][:, at:at + SKV], qT[:, h % 3, j * P:(j + 1) * P],
                                       kT[:, h, (j // 2) * SKV:(j // 2 + 1) * SKV], start=True, stop=True)
                    if h % 2:
                        mm.then_inc(s_ring.full, 1)

                turns, outs = {5: 0, 8: 1, 12: 2, 15: 3}, {6: 0, 9: 1, 13: 2}
                for h in range(H0):
                    b = qr.fill(pe)
                    for c in range(C):
                        mm = pe.matmul(b[:], wq[:, c, h * D0:(h + 1) * D0], xnT[:, c, :],
                                       start=(c == 0), stop=(c == C - 1))
                    mm.then_inc(q_ring.full, 1)
                    if not first_ and h in turns:
                        transpose_attn(i - 1, turns[h])
                    if not first_ and h in outs:
                        output(i - 1, outs[h])
                    if h >= 2:
                        scores(h - 2, h + 1)
                scores(H0 - 2, H0)
                scores(H0 - 1, H0)
                if not first_:
                    output(i - 1, G - 1)
                if not last:
                    keys()
                values(i % 2)
                if not last:
                    transpose_keys(i + 1)

            pe.wait_ge(wq_loaded, 16)
            pe.wait_ge(wv_loaded, 16)
            pe.wait_ge(wo_loaded, 16)
            step(0, True, False)
            with pe.Fori(1, NG - 1) as i:
                step(i, False, False)
            step(NG - 1, False, True)
            def route_front(i):
                qr.at(Q2, QR, i)
                sr.at(S2, SR, i)
                transpose_xn(NG + i)
                b = tr.fill(pe)
                for j in range(G):
                    for c in range(C):
                        mm = pe.matmul(b[:, j * E0:(j + 1) * E0], xnT[:, c, j * P:(j + 1) * P], rwT[:, c, :],
                                       start=(c == 0), stop=(c == C - 1))
                mm.then_inc(t_ring.full, 1)
                for half in range(2):
                    for ring, end, o in ((s_ring, sr, 0), (q_ring, qr, I0)):
                        b = end.fill(pe)
                        for c in range(C):
                            mm = pe.matmul(b[0:I0, 0:2 * P], sh_gu[:, c, o:o + I0],
                                           xnT[:, c, half * 2 * P:(half + 1) * 2 * P], start=(c == 0),
                                           stop=(c == C - 1))
                        mm.then_inc(ring.full, 1)

            pe.wait_ge(r_loaded, 64)
            tr.at(T2 - T_HEADS)
            route_front(0)
            for j in range(G):
                transpose_attn(NG - 1, j)
                output(NG - 1, j)
            pe.drain().then_inc(done1["pe"], 1)

            def route(i, last):
                tr.at(T2 + TRF, TR, i)
                if not last:
                    route_front(i + 1)
                pe.wait_ge(q_ring.free, Q2 + QR * (i + 1))
                for j in range(G):
                    pe.wait_ge(o_read, G * (NG + i) + j + 1)
                    pe.matmul(o_banks[j % 2][:, 0:DIM], sh_h[:, j * P:(j + 1) * P], sh_dn[:], start=True,
                              stop=True).then_inc(o_full, 1)
                pe.wait_ge(key_ready, 2 * (i + 1))
                b = tr.fill(pe)
                pe.sem_inc(pe_wait_done, 1)
                for j in range(G):
                    mm = pe.transpose(b[:, j * P:(j + 1) * P], keys2[:, j].rearrange("p h e -> p (h e)"), ident[:])
                mm.then_inc(t_ring.full, 1)

            with pe.Fori(0, NG - 1) as i:
                route(i, False)
            route(NG - 1, True)
            tr.at(T2 + TR * NG)
            pe.wait_ge(slots_ready, 1)
            pe.transpose(tr.fill(pe)[:, 0:E0], slots[:], ident[0:E0, 0:E0]).then_inc(t_ring.full, 1)

            def transpose_rows(i, q):
                pe.wait_ge(xg_loaded[q], 32 * (i + 1))
                b = tr.fill(pe)
                for e in range(2):
                    for c in range(C):
                        at = (2 * e + c) * P
                        mm = pe.transpose(b[:, at:at + P], xg[:, q, e, c * P:(c + 1) * P], ident[:])
                mm.then_inc(t_ring.full, 1)

            def experts(i, last):
                qr.at(Q3, 4, i)
                sr.at(S3, 4, i)
                tr.at(T3 + 1, 4, i)
                for q in range(4):
                    pe.wait_ge(w_loaded[q], 32 * (i + 1))
                    tr.evacuated(pe)
                    for ring, end, o in ((s_ring, sr, 0), (q_ring, qr, I0)):
                        b = end.fill(pe)
                        for e in range(2):
                            for c in range(C):
                                mm = pe.matmul(b[0:I0, e * P:(e + 1) * P], w_gu[:, q, e, c, o:o + I0],
                                               xgT[:, q % 2, e, c, :], start=(c == 0), stop=(c == C - 1))
                        mm.then_inc(ring.full, 1)
                    if not (last and q == 3):
                        transpose_rows(i + (q + 1) // 4, (q + 1) % 4)
                    qr.evacuated(pe)
                    if q < 2:
                        pe.wait_ge(y_ready if i is not first_step else o_read,
                                   4 * i + q - 1 if i is not first_step else 2 + 2 * NT)
                    else:
                        pe.wait_ge(y_ready, 4 * i + q - 1)
                    for e in range(2):
                        mm = pe.matmul(o_banks[q % 2][:, e * DIM:(e + 1) * DIM], act_h[:, q % 2, e * P:(e + 1) * P],
                                       w_dn[:, q, e, :], start=True, stop=True)
                    mm.then_inc(y_full, 1)

            first_step = 0
            tr.at(T3)
            transpose_rows(0, 0)
            experts(0, False)
            with pe.Fori(1, NQ - 1) as i:
                experts(i, False)
            experts(NQ - 1, True)

            def front(i):
                pe.wait_ge(ctx_loaded, 16 * (NG + i + 1))
                pe.transpose(tr.fill(pe)[:, 0:P], ctx_rows[:], ident[:]).then_inc(t_ring.full, 1)
                tr.evacuated(pe)
                for swapped in range(2):
                    b = qr.fill(pe)[:, 0:DIM] if swapped else qr.fill(pe)[:]
                    for kind in range(2):
                        w = wkv1[:, kind, :]
                        mm = pe.matmul(b, ctx1T[:, kind, swapped * SKV:swapped * SKV + P],
                                       w[:, DIM:2 * DIM] if swapped else w, start=(kind == 0), stop=(kind == 1))
                    mm.then_inc(q_ring.full, 1)
                transpose_xn(2 * NG + i)
                for half in range(2):
                    b = qr.fill(pe)
                    for k in range(2):
                        j = 2 * half + k
                        for c in range(C):
                            mm = pe.matmul(b[:, k * DIM:(k + 1) * DIM], xnT[:, c, j * P:(j + 1) * P], wq1[:, c, :],
                                           start=(c == 0), stop=(c == C - 1))
                    mm.then_inc(q_ring.full, 1)

            def heads1(i):
                pe.wait_ge(k1_ready, i + 1)
                b = tr.fill(pe)
                for c in range(C):
                    at = G * H1 + 8 * c
                    mm = pe.transpose(b[:, c * P:(c + 1) * P], qk1[:, at:at + 8, :].rearrange("p h d -> p (h d)"),
                                      ident[:])
                mm.then_inc(t_ring.full, 1)
                pe.wait_ge(q1_ready, i + 1)
                for c in range(C):
                    b = tr.fill(pe)
                    for j in range(G):
                        at = j * H1 + 8 * c
                        mm = pe.transpose(b[:, j * P:(j + 1) * P],
                                          qk1[:, at:at + 8, :].rearrange("p h d -> p (h d)"), ident[:])
                    mm.then_inc(t_ring.full, 1)

            def scores1(i):
                pe.wait_ge(t_ring.free, T4 + TF + TA * i)
                pe.wait_ge(k_blocks_ready, 4 * (i + 1))
                for j in range(G):
                    for c in range(C):
                        pe.matmul(sr.fill(pe)[:], q1T[:, c, j * P:(j + 1) * P],
                                  k_blocks[:, j // 2, c].rearrange("p h k -> p (h k)"), start=True,
                                  stop=True).then_inc(s_ring.full, 1)

            def attention(i, last):
                qr.at(Q4 + QA, QA, i)
                sr.at(S4 + SA, SA, i)
                tr.at(T4 + TF, TA, i)
                if not last:
                    front(i + 1)
                place = {}

                def transpose_attn(j):
                    pe.wait_ge(attn_ready, NT + 2 * (G * i + j) + 2)
                    for g in range(2):
                        b = tr.fill(pe)
                        for k in range(4):
                            at = (4 * g + k) * P
                            mm = pe.transpose(b[:, k * P:(k + 1) * P], soft[:, j, at:at + P], ident[:])
                        mm.then_inc(t_ring.full, 1)
                    place["a", j] = tr.k

                def contexts(j):
                    tr.evacuated(pe, tr.k - place["a", j] + 1)
                    pe.wait_ge(o_read, G * (2 * NG + i) + j + 1)
                    for p in range(8):
                        mm = pe.matmul(o_banks[j % 2][:, 32 * p:32 * (p + 1)], attnT[:, j % 2, p, :],
                                       v_blocks[:, i % 2, j // 2, p].rearrange("p o d -> p (o d)"), start=True,
                                       stop=True)
                    mm.then_inc(c1_full, 1)

                def transpose_context(j):
                    pe.wait_ge(c1_ready, G * i + j + 1)
                    b = tr.fill(pe)
                    for c in range(C):
                        mm = pe.transpose(b[:, c * P:(c + 1) * P], c1[:, j % 2, c * P:(c + 1) * P], ident[:])
                    mm.then_inc(t_ring.full, 1)
                    place["c", j] = tr.k

                def output(j):
                    tr.evacuated(pe, tr.k - place["c", j] + 1)
                    b = o_banks[j % 2][:, DIM:2 * DIM]
                    for c in range(C):
                        pe.matmul(b, c1T[:, j % 2, c, :], wo1[:, c, :], start=(c == 0), stop=False)
                    pe.matmul(b, ones[0:1, 0:P], bo1[:], start=False, stop=True).then_inc(o_full, 1)

                transpose_attn(0)
                transpose_attn(1)
                contexts(0)
                transpose_context(0)
                contexts(1)
                transpose_attn(2)
                output(0)
                transpose_context(1)
                contexts(2)
                transpose_attn(3)
                output(1)
                transpose_context(2)
                contexts(3)
                output(2)
                if not last:
                    heads1(i + 1)
                transpose_context(3)
                output(3)
                if not last:
                    scores1(i + 1)

            pe.wait_ge(w3_loaded, 16 * W3)
            qr.at(Q4)
            sr.at(S4)
            tr.at(T4)
            front(0)
            heads1(0)
            scores1(0)
            with pe.Fori(0, NG - 1) as i:
                attention(i, False)
            attention(NG - 1, True)

            def mixture(i):
                qr.at(Q5, QM, i)
                sr.at(S5, SM, i)
                tr.at(T5, TM, i)
                transpose_xn(3 * NG + i)
                for half in range(2):
                    b = tr.fill(pe)
                    for k in range(2):
                        j = 2 * half + k
                        for c in range(C):
                            mm = pe.matmul(b[:, k * E1:(k + 1) * E1], xnT[:, c, j * P:(j + 1) * P], gate1[:, c, :],
                                           start=(c == 0), stop=(c == C - 1))
                    mm.then_inc(t_ring.full, 1)

                def gates_ups(j):
                    for p in range(5):
                        for o, (ring, end) in enumerate(((s_ring, sr), (q_ring, qr))):
                            b = end.fill(pe)
                            for c in range(C):
                                mm = pe.matmul(b[:, 0:2 * F1], xnT[:, c, j * P:(j + 1) * P], gu1[:, c, p, o, :],
                                               start=(c == 0), stop=(c == C - 1))
                            mm.then_inc(ring.full, 1)

                def down(j):
                    pe.wait_ge(q_ring.free, Q5 + QM * i + 5 * (j + 1))
                    for g in range(4):
                        b = tr.fill(pe)
                        for f in range(4 * g, min(4 * g + 4, FC)):
                            n = min(P, W1 - f * P)
                            mm = pe.transpose(b[0:n, (f % 4) * P:(f % 4 + 1) * P],
                                              act_v[:, j % 2, f * P:f * P + n], ident[:])
                        mm.then_inc(t_ring.full, 1)
                    pe.wait_ge(o_read, G * (3 * NG + i) + j + 1)
                    for f in range(FC):
                        n = min(P, W1 - f * P)
                        if f % 4 == 0:
                            tr.evacuated(pe, 4 - f // 4)
                        mm = pe.matmul(o_banks[j % 2][:, 0:DIM], attn_flat[0:n, f, :], dn1[0:n, f, :],
                                       start=(f == 0), stop=(f == FC - 1))
                    mm.then_inc(o_full, 1)

                gates_ups(0)
                gates_ups(1)
                for j in range(G):
                    down(j)
                    if j + 2 < G:
                        gates_ups(j + 2)

            attn_flat = attnT[:].rearrange("p b f t -> p (b f) t")
            pe.wait_ge(w4_loaded, 64)
            with pe.Fori(0, NG) as i:
                mixture(i)


_INS = ["x", "ctx_1024", "g_xattn", "g_ffn", "L0_xattn_Wq", "L0_xattn_Wk", "L0_xattn_Wv", "L0_xattn_Wo",
        "L0_xattn_gq", "L0_xattn_gk", "L0_ffn_e_bias", "L0_ffn_w_down", "L0_ffn_sh_down",
        "L1_xattn_Wq", "L1_xattn_bq",
        "L1_xattn_Wkv_dca", "L1_xattn_bkv_dca", "L1_xattn_qn_w", "L1_xattn_qn_b", "L1_xattn_kn_w",
        "L1_xattn_kn_b", "L1_xattn_kn_dca_w", "L1_xattn_kn_dca_b", "L1_xattn_Wo", "L1_xattn_bo"]


def kernel(**inputs):
    import numpy as np
    import concourse.bacc as bacc
    from concourse.bass_utils import run_bass_kernel_spmd as run

    nc = bacc.Bacc("TRN2", target_bir_lowering=False, num_devices=1)
    arrays, args = {}, {}
    laid_out = {name: inputs[name] for name in _INS}
    laid_out["L0_ffn_router_weightT"] = np.asarray(inputs["L0_ffn_router_weight"]).T
    laid_out["L0_ffn_w_gu"] = np.concatenate([inputs["L0_ffn_w_gate"], inputs["L0_ffn_w_up"]], axis=2)
    laid_out["L0_ffn_sh_gu"] = np.concatenate([inputs["L0_ffn_sh_gate"], inputs["L0_ffn_sh_up"]], axis=1)
    gu = np.asarray(inputs["L1_ffn_gate_up_weights"]).reshape(E1, 2, F1, DIM)
    shared = np.asarray(inputs["L1_ffn_shared_gate_up"]).reshape(2, 2, F1, DIM).transpose(1, 0, 2, 3)
    gu = np.concatenate([gu, shared], axis=0).reshape(5, 2, 2, F1, DIM)
    laid_out["L1_gu"] = gu.transpose(4, 0, 2, 1, 3).reshape(DIM, 5, 2, 2 * F1)
    down = np.asarray(inputs["L1_ffn_down_weights"]).transpose(0, 2, 1).reshape(E1 * F1, DIM)
    laid_out["L1_down"] = np.concatenate([down, np.asarray(inputs["L1_ffn_shared_down"]).T], axis=0)
    for name, parts in (("L1_kv_main", ("L1_xattn_Wk", "L1_xattn_Wv")), ("L1_bkv_main", ("L1_xattn_bk", "L1_xattn_bv"))):
        kv = np.concatenate([np.asarray(inputs[p]) for p in parts], axis=-1)
        laid_out[name] = kv.reshape(-1, H1, 2, D1).transpose(0, 2, 1, 3).reshape(kv.shape)
    laid_out["L1_gateT"] = np.asarray(inputs["L1_ffn_gate_weight"]).T
    for name, v in laid_out.items():
        v = np.ascontiguousarray(v)
        arrays[f"in_{name}"] = v
        args[name] = nc.dram_tensor(f"in_{name}", v.shape, mybir.dt.from_np(v.dtype), kind="ExternalInput").ap()
    out = nc.dram_tensor("out_0", (B, SQ, DIM), F32, kind="ExternalOutput").ap()
    flamingo(nc, args, out)
    r = run(nc, [arrays], core_ids=[0])
    return r.results[0]["out_0"]
```

```python
from contextlib import ExitStack

import concourse.bass as bass
from concourse import mybir

F32 = mybir.dt.float32
F32R = mybir.dt.float32r
I32 = mybir.dt.int32
ACT = mybir.ActivationFunctionType
ALU = mybir.AluOpType
AX = mybir.AxisListType

P = 128
B, SQ, DIM = 8, 256, 256
SKV, CDIM = 64, 128
T = B * SQ
NT = T // P
G = 4
NG = NT // G
C = DIM // P
H0, D0 = 16, 128
E0, I0, K0 = 64, 88, 8
CAP = 128
ROW = DIM + E0
H1, D1, MAIN = 16, 16, 48
QK = G * H1 + H1
E1, F1 = 8, 176
W1 = (E1 + 2) * F1
FC = -(-W1 // P)
FAR = 1e30
EPS0 = 1e-5
EPS1 = 1e-6


class Ring:

    def __init__(self, banks, full, free):
        self.banks, self.full, self.free = banks, full, free

    def end(self):
        return RingEnd(self)


class RingEnd:

    def __init__(self, ring):
        self.ring, self.base, self.even, self.k = ring, 0, 0, 0

    def at(self, before, each=0, i=0):
        assert each % 2 == 0
        self.base, self.even, self.k = before + each * i, before % 2, 0

    def _take(self):
        pos, bank = self.base + self.k, self.ring.banks[(self.even + self.k) % len(self.ring.banks)]
        self.k += 1
        return pos, bank

    def fill(self, pe):
        pos, bank = self._take()
        if not (isinstance(pos, int) and pos < len(self.ring.banks)):
            pe.wait_ge(self.ring.free, pos - len(self.ring.banks) + 1)
        return bank

    def read(self, eng):
        pos, bank = self._take()
        eng.wait_ge(self.ring.full, pos + 1)
        return bank

    def evacuated(self, eng, back=1):
        eng.wait_ge(self.ring.free, self.base + self.k - back + 1)

    def skip(self, n):
        self.k += n


class Chain:

    def __init__(self, eng, sem):
        self.eng, self.sem, self.base, self.k = eng, sem, 0, 0

    def at(self, base):
        self.base, self.k = base, 0

    def add(self, ins):
        ins.then_inc(self.sem, 1)
        self.k += 1
        return self.k

    def wait(self, k=None):
        self.eng.wait_ge(self.sem, self.base + (self.k if k is None else k))


def flamingo(nc, a, out, stages=4):
    with ExitStack() as ctx:
        def sb(name, shape, dt=F32, scope=ctx):
            return scope.enter_context(nc.sbuf_tensor(name, shape, dt))

        def sem(name):
            return ctx.enter_context(nc.semaphore(name))

        bank = [ctx.enter_context(nc.psum_tensor(f"bank{n}", [P, 512], F32)) for n in range(8)]
        q_ring = Ring([bank[0], bank[1]], sem("q_full"), sem("q_free"))
        s_ring = Ring([bank[2], bank[3]], sem("s_full"), sem("s_free"))
        t_ring = Ring([bank[4], bank[5]], sem("t_full"), sem("t_free"))
        o_banks = [bank[6], bank[7]]
        n_bank = bank[7]

        x = sb("x", [P, NT, DIM])
        ident = sb("ident", [P, P])
        ones = sb("ones", [P, P])
        band = sb("band", [P, 2 * H0])
        band_r = sb("band_r", [P, 2 * H0], F32R)
        n_rows = sb("n_rows", [H0, G * P])
        newton = sb("newton", [P, 80])
        gates = sb("gates", [P, 4])
        xn = sb("xn", [P, G, DIM])
        same = ExitStack()
        xnT = sb("xnT", [P, C, G * P], scope=same)
        same.close()
        xnT_rest = sb("xnT_rest", [P, C, G * P], F32R)
        stats = sb("stats", [P, G, 6])
        mv = sb("mv", [P, G, 2])
        var = sb("var", [P, G])
        rstd = sb("rstd", [P, G])
        soft = sb("soft", [P, G, 1024])
        attnT = sb("attnT", [P, 2, 8, P])
        small = sb("small", [P, G, 2, 32])

        rwT = sb("rwT", [P, C, E0])
        e_bias = sb("e_bias", [P, E0])
        sh_gu = sb("sh_gu", [P, C, 2 * I0])
        sh_dn = sb("sh_dn", [I0, DIM])
        before = sb("before", [P, 8, 8])
        key_base = sb("key_base", [P, NT])
        zeros = sb("zeros", [P, ROW])
        cand = sb("cand", [P, 2 * CAP])
        slots = sb("slots", [E0, CAP])
        slotsT = sb("slotsT", [P, E0])
        spare = sb("spare", [P, E0])
        src_idx = sb("src_idx", [P, E0], I32)
        dst_idx = sb("dst_idx", [P, E0], I32)
        sigs = soft[:, 3, 512:1024].rearrange("p (b n) -> p b n", b=2)
        keys2 = soft[:, 2, 0:512].rearrange("p (j h e) -> p j h e", j=G, h=2)
        part = [soft[:, n // 4, (n % 4) * 256:(n % 4 + 1) * 256] for n in range(16)]

        ctx_rows = sb("ctx_rows", [P, CDIM])

        gqk = sb("gqk", [P, 2])
        gscale = sb("gscale", [P, 1])
        first = ExitStack()
        loaded = ExitStack()
        wq = sb("wq", [P, C, H0 * D0], scope=loaded)
        loaded.close()
        wq_lo = sb("wq_lo", [P, C, H0 * D0], F32R, scope=first)
        wq_hi = sb("wq_hi", [P, C, H0 * D0], F32R, scope=first)
        wk = sb("wk", [P, H0 * D0], scope=first)
        wv = sb("wv", [P, H0 * D0], scope=first)
        wo = sb("wo", [P, H0, DIM], scope=first)
        ctxK = sb("ctxK", [P, P], scope=first)
        ctxV = sb("ctxV", [P, 2, 3 * SKV], scope=first)
        raw = sb("raw", [P, 2, G, H0 * SKV], scope=first)
        qT = sb("qT", [P, 3, G * P], scope=first)
        xnT_top = sb("xnT_top", [P, C, G * P], F32R, scope=first)
        values_space = ExitStack()
        vT = sb("vT", [P, H0, P], scope=values_space)
        values_space.close()
        q2_hi = sb("q2_hi", [P, 3, G * P], F32R, scope=first)
        q2_lo = sb("q2_lo", [P, 3, G * P], F32R, scope=first)
        q2 = [soft[:, 3, 0:512], soft[:, 3, 512:1024]]
        prob = soft[:, 0, :]
        ksb = soft[:, 1:3, :].rearrange("p j (h d) -> p (j h) d", d=D0)
        ksq = attnT[:].rearrange("p b h t -> p (b h) t")
        kstat = sb("kstat", [P, 2, H0], scope=first)
        kT = sb("kT", [P, H0, P], scope=first)
        vw = sb("vw", [P, 2, 8, DIM], scope=first)
        qvar = sb("qvar", [P, G * H0], scope=first)
        rq = sb("rq", [P, G * H0], scope=first)


        first.close()

        rows = ExitStack()
        xw = sb("xw", [P, 2, G, ROW], scope=rows)
        y2_rows = sb("y2_rows", [P, 2, K0 * DIM], scope=rows)
        y2_sum = sb("y2_sum", [P, 2, DIM], scope=rows)
        keyT = sb("keyT", [P, T // 2], scope=rows)
        rows.close()
        gu_hi = sb("gu_hi", [P, 2 * G * ROW + 2 * K0 * DIM + 2 * DIM + T // 2], F32R)[:, 0:C * 5 * 4 * F1].rearrange(
            "p (c e g n) -> p c e g n", c=C, e=5, g=2)
        second = ExitStack()
        sh_g = sb("sh_g", [I0, G * P], scope=second)
        sh_h = sb("sh_h", [I0, G * P], scope=second)
        w_gu = sb("w_gu", [P, 4, 2, C, 2 * I0], scope=second)
        w_dn = sb("w_dn", [I0, 4, 2, DIM], scope=second)
        xg = sb("xg", [P, 4, 2, ROW], scope=second)
        xgT = sb("xgT", [P, 2, 2, C, P], scope=second)
        act_g = sb("act_g", [I0, 2, 2 * P], scope=second)
        act_h = sb("act_h", [I0, 2, 2 * P], scope=second)
        y = sb("y", [P, 4, 2, DIM], scope=second)
        src_now = sb("src_now", [P, 4, 2], I32, scope=second)
        dst_now = sb("dst_now", [P, 4, 2], I32, scope=second)
        second.close()

        loaded = ExitStack()
        gu1 = sb("gu1", [P, C, 5, 2, 2 * F1], scope=loaded)
        loaded.close()
        gu_lo = sb("gu_lo", [P, C, 5, 2, 2 * F1], F32R)
        dn1 = sb("dn1", [P, FC, DIM])
        gate1 = sb("gate1", [P, C, E1])
        sg = sb("sg", [P, 2, 2 * F1])
        combine_w = sb("combine_w", [P, G, E1 + 2])
        act_v = soft[:].rearrange("p j n -> p (j n)")[:, 0:2 * FC * P].rearrange("p (b n) -> p b n", b=2)
        logits = sb("logits", [P, G * E1])
        rank_t = sb("rank_t", [P, 2, G * E1 * E1])
        gate_s = sb("gate_s", [P, 3, G * E1])

        head_mask = sb("head_mask", [P, 8])
        qk1 = sb("qk1", [P, QK, D1])
        heads = ExitStack()
        qk1_sq = sb("qk1_sq", [P, QK, D1], scope=heads)
        q1T = sb("q1T", [P, C, G * P], scope=heads)
        heads.close()
        xnT_split = sb("xnT_split", [P, QK * D1 + C * G * P], F32R)
        xnT_hi, xnT_lo = (xnT_split[:, n * C * G * P:(n + 1) * C * G * P].rearrange("p (c t) -> p c t", c=C)
                          for n in range(2))
        qk1_stat = sb("qk1_stat", [P, 2, QK])
        k1T = sb("k1T", [P, C, P])
        k_blocks = sb("k_blocks", [P, 2, C, 8, SKV])
        v_blocks = sb("v_blocks", [P, 2, 2, 8, 2, D1])
        c1 = sb("c1", [P, 2, DIM])
        c1T = sb("c1T", [P, 2, C, P])
        ctx1T = sb("ctx1T", [P, 2, 3 * SKV])
        wq1 = sb("wq1", [P, C, DIM])
        wkv1 = sb("wkv1", [P, 2, 2 * DIM])
        wo1 = sb("wo1", [P, C, DIM])
        bq1 = sb("bq1", [P, DIM])
        bkv1 = sb("bkv1", [P, 2 * DIM])
        bo1 = sb("bo1", [1, DIM])
        qn = sb("qn", [P, 2, D1])
        kn = sb("kn", [P, 2, D1])

        table = nc.dram_tensor("table", (T + 1, ROW), F32, kind="Internal").ap()
        y2 = nc.dram_tensor("y2", (K0 * T + E0 * CAP, DIM), F32, kind="Internal").ap()

        const_ready = sem("const_ready")
        ident_zero = sem("ident_zero")
        x_loaded = sem("x_loaded")
        x_rest_loaded = sem("x_rest_loaded")
        gates_loaded = sem("gates_loaded")
        gates_ready = sem("gates_ready")
        wk_loaded, wq_loaded, wv_loaded, wo_loaded = (sem(f"{w}_loaded") for w in ("wk", "wq", "wv", "wo"))
        gqk_loaded = sem("gqk_loaded")
        gqk_ready = sem("gqk_ready")
        ctx_loaded = sem("ctx_loaded")
        dve_chain = sem("dve_chain")
        wait_done, pe_wait_done, pool_wait_done = sem("wait_done"), sem("pe_wait_done"), sem("pool_wait_done")
        xn_ready = sem("xn_ready")
        kn_ready = sem("kn_ready")
        q2_ready = sem("q2_ready")
        q2_split = sem("q2_split")
        wq_rounded = sem("wq_rounded")
        wq_split = sem("wq_split")
        xnT_rounded = sem("xnT_rounded")
        xnT_ready = sem("xnT_ready")
        q_norm = sem("q_norm")
        n_copied = sem("n_copied")
        shifted = sem("shifted")
        exp_done = sem("exp_done")
        attn_ready = sem("attn_ready")
        o_full = sem("o_full")
        o_read = sem("o_read")
        x_done = sem("x_done")
        stored = sem("stored")
        done1 = {e: sem(f"done1_{e}") for e in ("pe", "act", "dve", "pool")}
        r_loaded = sem("r_loaded")
        r_const = sem("r_const")
        zero_ready = sem("zero_ready")
        zeroed = sem("zeroed")
        table_stored = sem("table_stored")
        key_ready = sem("key_ready")
        rows_ready = sem("rows_ready")
        slot_chain = sem("slot_chain")
        slots_ready = sem("slots_ready")
        cand_ready = sem("cand_ready")
        cand_moved = sem("cand_moved")
        idx_ready = sem("idx_ready")
        idx_now = sem("idx_now")
        w_loaded = [sem(f"w_loaded{q}") for q in range(4)]
        xg_loaded = [sem(f"xg_loaded{q}") for q in range(4)]
        y_stored = [sem(f"y_stored{q}") for q in range(4)]
        y_full = sem("y_full")
        y_ready = sem("y_ready")
        y2_loaded = [sem(f"y2_loaded{q}") for q in range(2)]
        y2_used = sem("y2_used")
        w3_loaded = sem("w3_loaded")
        w4_loaded = sem("w4_loaded")
        mask_step = sem("mask_step")
        combine_step = sem("combine_step")
        k1_ready = sem("k1_ready")
        k_blocks_ready = sem("k_blocks_ready")
        q1_centred = sem("q1_centred")
        q1_squared = sem("q1_squared")
        q1_scaled = sem("q1_scaled")
        affine_step = sem("affine_step")
        q1_ready = sem("q1_ready")
        c1_full = sem("c1_full")
        c1_ready = sem("c1_ready")
        w_rounded = sem("w_rounded")
        w_split = sem("w_split")
        xn_rounded = sem("xn_rounded")
        xn_split = sem("xn_split")
        gate_shifted = sem("gate_shifted")
        gate_exp = sem("gate_exp")

        x_d = a["x"].rearrange("b t d -> (b t) d").rearrange("(n p) d -> p n d", p=P)
        out_d = out.rearrange("b t d -> (b t) d").rearrange("(n p) d -> p n d", p=P)
        ctx_d = a["ctx_1024"].rearrange("b s c -> (b s) c")

        Q_PREP, Q_STEP = 4, 24
        S_PREP, S_STEP = 0, 16
        T_PREP, T_STEP = 8, 16
        T_HEADS = 8
        Q2, S2, T2 = Q_STEP * NG, S_STEP * NG, T_STEP * NG
        QR, SR, TR, TRF = 2, 2, 4, 3
        Q3, S3, T3 = Q2 + QR * NG, S2 + SR * NG, T2 + TR * NG + 1
        NQ = E0 // 8
        Q4, S4, T4 = Q3 + 4 * NQ, S3 + 4 * NQ, T3 + 4 * NQ
        QA, SA, TA = 4, 8, 18
        W3 = 8 + 2 * 6
        TF = 6
        Q5, S5, T5 = Q4 + QA * NG, S4 + SA * NG, T4 + TA * NG
        QM, SM, TM, TMF = 20, 20, 20, 4

        block = ctx.enter_context(nc.Block())

        @block.sync
        def _(sp):
            sp.dma_start(x[:, 0:G, :], x_d[:, 0:G, :]).then_inc(x_loaded, 16)
            sp.dma_start(ctx_rows[:], ctx_d[0:P, :]).then_inc(ctx_loaded, 16)
            sp.dma_start(wk[:], a["L0_xattn_Wk"]).then_inc(wk_loaded, 16)
            sp.dma_start(wq[:], a["L0_xattn_Wq"].rearrange("(c p) n -> p c n", p=P)).then_inc(wq_loaded, 16)
            sp.dma_start(wv[:], a["L0_xattn_Wv"]).then_inc(wv_loaded, 16)
            sp.dma_start(wo[:], a["L0_xattn_Wo"].rearrange("(h p) n -> p h n", p=P)).then_inc(wo_loaded, 16)
            sp.dma_start(x[:, G:NT, :], x_d[:, G:NT, :]).then_inc(x_rest_loaded, 16)
            for m in range(1, NG):
                sp.wait_ge(t_ring.full, 2 if m == 1 else T_PREP + 2 if m == 2 else
                           T_PREP + T_STEP * (m - 2) - T_HEADS + 2)
                sp.dma_start(ctx_rows[:], ctx_d[m * P:(m + 1) * P, :]).then_inc(ctx_loaded, 16)
            sp.wait_ge(zero_ready, 1)
            for n in range(NT):
                sp.dma_start(y2[n * P * K0:(n + 1) * P * K0, :].rearrange("(p k) d -> p k d", p=P),
                             zeros[:, 0:DIM].unsqueeze(1).to_broadcast([P, K0, DIM])).then_inc(zeroed, 16)
            sp.dma_start(table[T:T + 1, :], zeros[0:1, 0:ROW]).then_inc(table_stored, 16)
            table_d = table[0:T, :].rearrange("(n p) r -> p n r", p=P)
            with sp.Fori(0, NG) as i:
                sp.wait_ge(rows_ready, i + 1)
                sp.dma_start(table_d[:, bass.ds(G * i, G), :], xw[:, i % 2]).then_inc(table_stored, 16)

            def load_experts(i, q):
                sp.dma_start(w_gu[:, q], gu_d[:, bass.ds(8 * i + 2 * q, 2)]).then_inc(w_loaded[q], 16)
                sp.dma_start(w_dn[:, q], dn_d[:, bass.ds(8 * i + 2 * q, 2)]).then_inc(w_loaded[q], 16)

            gu_d = a["L0_ffn_w_gu"].rearrange("e (c p) n -> p e c n", p=P)
            dn_d = a["L0_ffn_w_down"].rearrange("e p n -> p e n")
            for e in done1.values():
                sp.wait_ge(e, 1)
            for q in range(4):
                load_experts(0, q)
            for dst, src in ((wq1[:], a["L1_xattn_Wq"].rearrange("(c p) n -> p c n", p=P)),
                             (wo1[:], a["L1_xattn_Wo"].rearrange("(c p) n -> p c n", p=P)),
                             (wkv1[:, 0, :], a["L1_kv_main"]), (wkv1[:, 1, :], a["L1_xattn_Wkv_dca"]),
                             (bq1[:], a["L1_xattn_bq"].partition_broadcast(P)),
                             (bo1[:], a["L1_xattn_bo"].unsqueeze(0)),
                             (qn[:, 0, :], a["L1_xattn_qn_w"].partition_broadcast(P)),
                             (qn[:, 1, :], a["L1_xattn_qn_b"].partition_broadcast(P))):
                sp.dma_start(dst, src).then_inc(w3_loaded, 16)
            for b0 in (0, SKV):
                sp.dma_start(bkv1[b0:b0 + MAIN, :], a["L1_bkv_main"].partition_broadcast(MAIN)).then_inc(w3_loaded, 16)
                sp.dma_start(bkv1[b0 + MAIN:b0 + SKV, :], a["L1_xattn_bkv_dca"].partition_broadcast(
                    SKV - MAIN)).then_inc(w3_loaded, 16)
                for n, name in enumerate(("w", "b")):
                    sp.dma_start(kn[b0:b0 + MAIN, n, :], a["L1_xattn_kn_" + name].partition_broadcast(MAIN)).then_inc(
                        w3_loaded, 16)
                    sp.dma_start(kn[b0 + MAIN:b0 + SKV, n, :], a["L1_xattn_kn_dca_" + name].partition_broadcast(
                        SKV - MAIN)).then_inc(w3_loaded, 16)
            sp.dma_start(ctx_rows[:], ctx_d[0:P, :]).then_inc(ctx_loaded, 16)
            sp.wait_ge(cand_ready, 1)
            sp.dma_start(cand[0:E0, CAP:2 * CAP], cand[E0:P, 0:CAP]).then_inc(cand_moved, 16)
            with sp.Fori(1, NQ) as i:
                for q in range(4):
                    sp.wait_ge(y_full, 4 * i + q - 3)
                    load_experts(i, q)
            for q in range(4):
                sp.wait_ge(y_stored[q], 32 * NQ)
            y2_d = y2[0:K0 * T, :].rearrange("(n p k) d -> n p (k d)", p=P, k=K0)

            def load_y2(n, q):
                sp.dma_start(y2_rows[:, q], y2_d[bass.ds(n, 1)].rearrange("n p k -> p (n k)")).then_inc(
                    y2_loaded[q], 16)

            load_y2(0, 0)
            load_y2(1, 1)

            def more_y2(i, tiles):
                for k in range(tiles):
                    sp.wait_ge(y2_used, G * i + k + 1)
                    load_y2(G * i + k + 2, k % 2)

            def next_context(i):
                sp.wait_ge(t_ring.full, T4 + 1 if i is first_group else T4 + TF + TA * (i - 1) + 1)
                sp.dma_start(ctx_rows[:], ctx_d[(i + 1) * P:(i + 2) * P, :] if i is first_group else
                             ctx_d[bass.ds((i + 1) * P, P), :]).then_inc(ctx_loaded, 16)

            first_group = 0
            next_context(0)
            more_y2(0, G)
            sp.dma_start(gu1[:], a["L1_gu"].rearrange("(c p) e g n -> p c e g n", p=P)).then_inc(w4_loaded, 16)
            full = (FC - 1) * P
            sp.dma_start(dn1[:, 0:FC - 1, :], a["L1_down"][0:full, :].rearrange("(f p) n -> p f n", p=P)).then_inc(
                w4_loaded, 16)
            sp.dma_start(dn1[0:W1 - full, FC - 1, :], a["L1_down"][full:W1, :]).then_inc(w4_loaded, 16)
            sp.dma_start(gate1[:], a["L1_gateT"].rearrange("(c p) e -> p c e", p=P)).then_inc(w4_loaded, 16)
            with sp.Fori(1, NG - 1) as i:
                more_y2(i, G)
                next_context(i)
            more_y2(NG - 1, G - 2)
            sp.wait_ge(x_done, 1)
            sp.dma_start(out_d, x[:]).then_inc(stored, 16)
            sp.wait_ge(stored, 16)

        @block.gpsimd
        def _(pool):
            pool.memset(ident[:], 0.0).then_inc(ident_zero, 1)
            pool.wait_ge(ident_zero, 1)
            pool.memset(zeros[:], 0.0).then_inc(zero_ready, 1)
            pool.memset(before[:], 1.0).then_inc(ident_zero, 1)
            pool.iota(key_base[:], pattern=[[-K0 * P * G, NG], [K0 - K0 * P, G]], base=K0 * T + 1,
                      channel_multiplier=-K0, allow_small_or_imprecise_dtypes=True).then_inc(r_const, 1)
            pool.iota(spare[:], pattern=[[CAP, E0]], base=0, channel_multiplier=1,
                      allow_small_or_imprecise_dtypes=True).then_inc(r_const, 1)
            pool.wait_ge(ident_zero, 2)
            pool.affine_select(out=before[:], in_=before[:], compare_op=ALU.is_gt, fill=0.0,
                               base=0, pattern=[[1, 8], [-1, 8]], channel_multiplier=0).then_inc(r_const, 1)
            pool.affine_select(out=ident[:], in_=ident[:], compare_op=ALU.not_equal, fill=1.0,
                               base=0, pattern=[[-1, P]], channel_multiplier=1).then_inc(const_ready, 1)

            def split_squares(i):
                for h in range(H0):
                    pool.wait_ge(q2_ready, H0 * i + h + 1)
                    pool.tensor_tensor(q2_lo[:, h % 3, :], q2[h % 2], q2_hi[:, h % 3, :],
                                       ALU.subtract).then_inc(q2_split, 1)

            with pool.Fori(0, NG) as i:
                split_squares(i)
            pool.drain().then_inc(done1["pool"], 1)

            def gather(i, q):
                pool.sem_inc(pool_wait_done, 1)
                for e in range(2):
                    pool.indirect_dma_start(xg[:, q, e, :], None, table, bass.IndirectOffsetOnAxis(
                        ap=src_now[:, q, e:e + 1], axis=0)).then_inc(xg_loaded[q], 16)

            def scatter(i, q):
                pool.wait_ge(y_ready, 4 * i + q + 1)
                pool.sem_inc(pool_wait_done, 1)
                for e in range(2):
                    pool.indirect_dma_start(y2, bass.IndirectOffsetOnAxis(ap=dst_now[:, q, e:e + 1], axis=0),
                                            y[:, q, e, :], None).then_inc(y_stored[q], 16)

            pool.wait_ge(table_stored, 16 * (NG + 1))
            pool.wait_ge(zeroed, 16 * NT)
            for q in range(3):
                pool.wait_ge(idx_now, q + 1)
                gather(0, q)

            def experts(i, last):
                for q in range(4):
                    if not (last and q):
                        pool.wait_ge(idx_now, 4 * i + q + 4)
                        gather(i, (q + 3) % 4)
                    scatter(i, q)

            with pool.Fori(0, NQ - 1) as i:
                experts(i, False)
            experts(NQ - 1, True)

            def combine(i):
                for j in range(G):
                    r, base = y2_rows[:, j % 2], 4 * (G * (i - 2) + j)
                    pool.wait_ge(y2_loaded[j % 2], 16 * (2 * i + j // 2 + 1))
                    for n, half in enumerate((4 * DIM, 2 * DIM, DIM)):
                        pool.tensor_tensor(r[:, 0:half], r[:, 0:half], r[:, half:2 * half],
                                           ALU.add).then_inc(combine_step, 1)
                        pool.wait_ge(combine_step, base + n + 1)
                    pool.sem_inc(pool_wait_done, 1)
                    pool.tensor_scalar(r[:, 0:DIM], r[:, 0:DIM], gates[:, 2:3], None, ALU.mult).then_inc(combine_step, 1)
                    pool.wait_ge(combine_step, base + 4)
                    xj = x[:, G * i + j, :]
                    pool.tensor_tensor(xj, xj, r[:, 0:DIM], ALU.add).then_inc(y2_used, 1)

            first_group = 0

            def affine_queries(i):
                v = qk1[:, 0:G * H1, :]
                pool.wait_ge(q1_scaled, i + 1)
                pool.tensor_tensor(v, v, qn[:, 0, :].unsqueeze(1).to_broadcast([P, G * H1, D1]),
                                   ALU.mult).then_inc(affine_step, 1)
                pool.wait_ge(affine_step, i + 1)
                pool.tensor_tensor(v, v, qn[:, 1, :].unsqueeze(1).to_broadcast([P, G * H1, D1]),
                                   ALU.add).then_inc(q1_ready, 1)

            def key_blocks(i):
                pool.wait_ge(t_ring.free, T4 + TA * i + (TF - 2 if i is first_group else 0))
                for b in range(2):
                    for c in range(C):
                        pool.tensor_tensor(
                            k_blocks[:, b, c], k1T[:, c, b * SKV:(b + 1) * SKV].unsqueeze(1).to_broadcast([P, 8, SKV]),
                            head_mask[:].unsqueeze(2).to_broadcast([P, 8, SKV]), ALU.mult).then_inc(k_blocks_ready, 1)

            for q in range(4):
                pool.wait_ge(y_stored[q], 32 * NQ)
            pool.memset(head_mask[:], 1.0).then_inc(mask_step, 1)
            pool.wait_ge(mask_step, 1)
            pool.affine_select(out=head_mask[:], in_=head_mask[:], compare_op=ALU.is_ge, fill=0.0, base=0,
                               pattern=[[-D1, 8]], channel_multiplier=1).then_inc(mask_step, 1)
            pool.wait_ge(mask_step, 2)
            pool.affine_select(out=head_mask[:], in_=head_mask[:], compare_op=ALU.is_ge, fill=0.0, base=D1 - 1,
                               pattern=[[D1, 8]], channel_multiplier=-1).then_inc(mask_step, 1)
            pool.wait_ge(mask_step, 3)
            pool.memset(ctx1T[:], 0.0).then_inc(mask_step, 1)
            affine_queries(0)
            key_blocks(0)
            pool.wait_ge(y2_used, 2 * G)
            with pool.Fori(1, NG - 1) as i:
                combine(i + 1)
                affine_queries(i)
                key_blocks(i)
            affine_queries(NG - 1)
            key_blocks(NG - 1)

        @block.vector
        def _(dve):
            qr = q_ring.end()
            ch = Chain(dve, dve_chain)
            ch.add(dve.memset(ones[:], 1.0))
            ch.wait()
            ch.add(dve.memset(band[:], 0.0))
            ch.wait()
            ch.add(dve.memset(band[:, H0 - 1:H0], 1.0))
            ch.wait()
            dve.tensor_copy(band_r[:], band[:]).then_inc(const_ready, 1)
            dve.sem_inc(o_read, 2)

            def inverse_root(y_, v, n):
                t = newton[:, 0:n]
                ch.add(dve.tensor_scalar(y_.bitcast(I32), v.bitcast(I32), 1, None, ALU.logical_shift_right))
                ch.wait()
                ch.add(dve.tensor_scalar(y_.bitcast(I32), y_.bitcast(I32), -1.0, float(0x5F3759DF), ALU.mult,
                                         ALU.add))
                ch.wait()
                for _ in range(3):
                    ch.add(dve.tensor_tensor(t, y_, y_, ALU.mult))
                    ch.wait()
                    ch.add(dve.scalar_tensor_tensor(out=t, in0=t, scalar=-0.5, in1=v, op0=ALU.mult, op1=ALU.mult))
                    ch.wait()
                    ch.add(dve.scalar_tensor_tensor(out=y_, in0=t, scalar=1.5, in1=y_, op0=ALU.add, op1=ALU.mult))
                    ch.wait()

            ROOT_CHAIN = 11

            def over_head(v, n=D1):
                return v.unsqueeze(2).to_broadcast([P, v.shape[1], n])

            def row_stats(i):
                dve.sem_inc(wait_done, 1)
                for j in range(G):
                    ch.add(dve.bn_stats(stats[:, j, :], x[:, G * i + j, :]))
                ch.wait()
                dve.sem_inc(wait_done, 1)
                for j in range(G):
                    ch.add(dve.bn_aggr(mv[:, j, :], stats[:, j, :]))
                ch.wait()

            def row_roots(eps):
                ch.add(dve.tensor_scalar(var[:], mv[:, :, 1], eps, None, ALU.add))
                ch.wait()
                inverse_root(rstd[:], var[:], G)

            def row_apply(i):
                for j in range(G):
                    dve.tensor_scalar(xn[:, j, :], x[:, G * i + j, :], mv[:, j, 0:1], rstd[:, j:j + 1],
                                      ALU.subtract, ALU.mult).then_inc(xn_ready, 1)

            def normed(i, eps):
                row_stats(i)
                row_roots(eps)
                row_apply(i)

            NORMED_CHAIN = 2 * G + 1 + ROOT_CHAIN

            def keys_in():
                for g in range(4):
                    dve.tensor_copy(ksb[:, 4 * g:4 * g + 4, :], qr.read(dve)[:].rearrange(
                        "p (h d) -> p h d", h=4)).then_inc(q_ring.free, 1)

            def values_in():
                for g in range(4):
                    dve.tensor_copy(vT[:, 4 * g:4 * g + 4, :], qr.read(dve)[:].rearrange(
                        "p (h d) -> p h d", h=4)).then_inc(q_ring.free, 1)

            def key_norm(back):
                qr.evacuated(dve, back)
                ch.add(dve.tensor_tensor(ksq[:], ksb[:], ksb[:], ALU.mult))
                ch.wait()
                ch.add(dve.tensor_reduce(kstat[:, 0, :], ksq[:], AX.X, ALU.add))
                ch.wait()
                ch.add(dve.tensor_scalar(kstat[:, 0, :], kstat[:, 0, :], 1.0 / D0, EPS0, ALU.mult, ALU.add))
                ch.wait()
                inverse_root(kstat[:, 1, :], kstat[:, 0, :], H0)
                dve.tensor_tensor(ksb[:], ksb[:], over_head(kstat[:, 1, :], D0), ALU.mult).then_inc(kn_ready, 1)

            def over(v):
                return v.unsqueeze(2).to_broadcast([P, H0, SKV])

            def residual(m, j, i=None, gate=0, one_bank=False):
                dve.wait_ge(o_full, G * m + j + 1)
                i = m if i is None else i
                xj = x[:, G * i + j, :]
                dve.scalar_tensor_tensor(out=xj, in0=o_banks[0 if one_bank else j % 2][:, 0:DIM],
                                         scalar=gates[:, gate:gate + 1], in1=xj, op0=ALU.mult,
                                         op1=ALU.add).then_inc(o_read, 1)

            KEY_CHAIN, ROOTS_CHAIN, SOFT_CHAIN = 3 + ROOT_CHAIN, 1 + ROOT_CHAIN, 4 * G
            PREP_CHAIN = 3 + NORMED_CHAIN + KEY_CHAIN
            STEP_CHAIN = NORMED_CHAIN + KEY_CHAIN + ROOTS_CHAIN + SOFT_CHAIN

            def softmax_pieces(i, par):
                def tile(j):
                    return raw[:, par, j, :].rearrange("p (h k) -> p h k", h=H0)

                def by_norm(j):
                    ch.add(dve.tensor_tensor(tile(j), tile(j), over(rq[:, j * H0:(j + 1) * H0]), ALU.mult))
                    ch.wait()

                def maximum(j):
                    dve.sem_inc(wait_done, 1)
                    ch.add(dve.tensor_reduce(small[:, j, 0, 0:H0], tile(j), AX.X, ALU.max))
                    ch.wait()

                def shift(j):
                    dve.tensor_tensor(tile(j), tile(j), over(small[:, j, 0, 0:H0]), ALU.subtract).then_inc(shifted, 1)

                def sums(j):
                    dve.wait_ge(exp_done, G * i + j + 1)
                    dve.sem_inc(wait_done, 1)
                    ch.add(dve.tensor_reduce(small[:, j, 1, 0:H0], tile(j), AX.X, ALU.add))
                    ch.wait()
                    ch.add(dve.reciprocal(small[:, j, 1, 0:H0], small[:, j, 1, 0:H0]))
                    ch.wait()

                def divide(j, before):
                    if before is not None:
                        dve.wait_ge(t_ring.full, before)
                    dve.tensor_tensor(prob.rearrange("p (h k) -> p h k", h=H0), tile(j),
                                      over(small[:, j, 1, 0:H0]), ALU.mult).then_inc(attn_ready, 1)

                return by_norm, maximum, shift, sums, divide

            dve.wait_ge(x_loaded, 16)
            normed(0, EPS0)
            keys_in()
            dve.wait_ge(gqk_loaded, 32)
            dve.scalar_tensor_tensor(out=gscale[:], in0=gqk[:, 0:1], scalar=float(D0) ** -0.5,
                                     in1=gqk[:, 1:2], op0=ALU.mult, op1=ALU.mult).then_inc(gqk_ready, 1)
            key_norm(1)
            assert ch.k == PREP_CHAIN

            def split_tokens(i):
                dve.wait_ge(xnT_rounded, i + 1)
                dve.tensor_tensor(xnT_rest[:], xnT[:], xnT_top[:], ALU.subtract).then_inc(xnT_ready, 1)

            split_tokens(0)
            for g in range(4):
                dve.wait_ge(wq_rounded, g + 1)
                w = slice(512 * g, 512 * (g + 1))
                dve.tensor_tensor(wq_lo[:, :, w], wq[:, :, w], wq_hi[:, :, w], ALU.subtract).then_inc(wq_split, 1)

            def step(i, first_, last):
                qr.at(Q_PREP, Q_STEP, i)
                ch.at(PREP_CHAIN + STEP_CHAIN * i - (0 if first_ else SOFT_CHAIN))
                by_norm, maximum, shift, sums, divide = softmax_pieces(i - 1, (i + 1) % 2)
                t0 = T_PREP + T_STEP * i - T_HEADS + (0 if last else 2)

                def out(j):
                    residual(i - 1, j, one_bank=True)

                pieces = {0: (by_norm, 0, maximum, 0), 1: (shift, 0, by_norm, 1), 2: (maximum, 1, shift, 1),
                          3: (sums, 0), 4: (divide, 0), 5: (sums, 1), 6: (divide, 1, by_norm, 2),
                          7: (maximum, 2, shift, 2, out, 0), 8: (by_norm, 3, maximum, 3), 9: (sums, 2),
                          10: (divide, 2, out, 1), 11: (shift, 3), 13: (sums, 3), 14: (divide, 3, out, 2)}
                if not first_:
                    dve.wait_ge(s_ring.free, S_PREP + S_STEP * (i - 1) + 8)
                for h in range(H0):
                    dve.tensor_copy(qT[:, h % 3, :], qr.read(dve)[:]).then_inc(q_ring.free, 1)
                    if not first_:
                        run = pieces.get(h, ())
                        for piece, j in zip(run[0::2], run[1::2]):
                            if piece is divide:
                                divide(j, t0 + 2 * j if j else None)
                            else:
                                piece(j)
                    if h == 12 and not last:
                        row_stats(i + 1)
                    if h == 15 and not last:
                        row_roots(EPS0)
                dve.wait_ge(q_norm, 2 * i + 1)
                dve.tensor_copy(n_rows[:], n_bank[0:H0, :]).then_inc(n_copied, 1)
                if not last:
                    keys_in()
                if not first_:
                    out(3)
                values_in()
                dve.wait_ge(q_norm, 2 * i + 2)
                ch.add(dve.tensor_scalar(qvar[:], n_bank[:, 0:G * H0], 1.0 / D0, EPS0, ALU.mult, ALU.add))
                if not last:
                    row_apply(i + 1)
                    key_norm(5)
                    split_tokens(i + 1)
                ch.wait()
                inverse_root(rq[:], qvar[:], G * H0)
                assert first_ or last or ch.k == STEP_CHAIN, (ch.k, STEP_CHAIN)

            dve.wait_ge(gates_ready, 1)
            dve.wait_ge(x_rest_loaded, 16)
            step(0, True, False)
            with dve.Fori(1, NG - 1) as i:
                step(i, False, False)
            step(NG - 1, False, True)

            normed(0, EPS0)
            def shared_product(i):
                qr.at(Q2, QR, i)
                for half in range(2):
                    dve.wait_ge(s_ring.free, S2 + SR * i + half + 1)
                    h = slice(half * 2 * P, (half + 1) * 2 * P)
                    dve.tensor_tensor(sh_h[:, h], sh_g[:, h], qr.read(dve)[0:I0, 0:2 * P],
                                      ALU.mult).then_inc(q_ring.free, 1)

            dve.wait_ge(s_ring.free, S_PREP + S_STEP * (NG - 1) + 8)
            by_norm, maximum, shift, sums, divide = softmax_pieces(NG - 1, (NG - 1) % 2)
            T_LAST = T2 - T_HEADS + TRF
            for j in range(G):
                by_norm(j)
                maximum(j)
                shift(j)
                if j:
                    sums(j - 1)
                    divide(j - 1, T_LAST + 2 * (j - 1) if j > 1 else None)
                if j > 1:
                    residual(NG - 1, j - 2, one_bank=True)
                if j == 2:
                    shared_product(0)
            sums(G - 1)
            divide(G - 1, T_LAST + 2 * (G - 1))
            residual(NG - 1, G - 2, one_bank=True)
            residual(NG - 1, G - 1, one_bank=True)
            dve.wait_ge(o_read, 2 + NT)
            dve.drain().then_inc(done1["dve"], 1)

            def tiles(v, n=E0):
                return v.rearrange("p (j e) -> p j e", j=G)

            def group_max(dst, v):
                return dve.tensor_reduce(dst, v.rearrange("p (g e) -> p g e", e=8), AX.X, ALU.max)

            def wide(v, n=8):
                return v.unsqueeze(2).to_broadcast([P, v.shape[1], n])

            def by8(v):
                return v.rearrange("p (g e) -> p g e", e=8)

            def rank_below(dst, v, count, t0, t1):
                a0 = v.unsqueeze(2).to_broadcast([P, G, 8, 8])
                a1 = v.unsqueeze(3).to_broadcast([P, G, 8, 8])
                r0, r1 = (t.rearrange("p (j g k) -> p j g k", j=G, g=8) for t in (t0, t1))
                ch.add(dve.tensor_tensor(r0, a0, a1, ALU.is_gt))
                ch.add(dve.tensor_tensor(r1, a0, a1, ALU.is_ge))
                ch.wait()
                ch.add(dve.tensor_tensor(r1, r1, before[:].unsqueeze(1).to_broadcast([P, G, 8, 8]), ALU.mult))
                ch.wait()
                ch.add(dve.tensor_tensor(t0, t0, t1, ALU.max))
                ch.wait()
                ch.add(dve.tensor_reduce(t1[:, 0:8 * G], by8(t0), AX.X, ALU.add))
                ch.wait()
                ch.add(dve.tensor_scalar(dst, t1[:, 0:8 * G], count - 0.5, None, ALU.is_lt))
                ch.wait()

            dve.wait_ge(r_const, 3)
            dve.wait_ge(r_loaded, 64)
            dve.wait_ge(zeroed, 16 * NT)
            for e in done1.values():
                dve.wait_ge(e, 1)
            ROUTE_CHAIN = NORMED_CHAIN + 24 + 2 * G
            ROUTE_BASE = PREP_CHAIN + STEP_CHAIN * NG - KEY_CHAIN

            def route(i, last):
                ch.at(ROUTE_BASE + ROUTE_CHAIN * i)
                dve.wait_ge(t_ring.free, T2 + TRF + TR * i)
                if not last:
                    normed(i + 1, EPS0)
                dve.wait_ge(table_stored, 16 * (i + 1))
                sig, sc, eq, oth, msk, rep, t0, t1, sel = [sigs[:, i % 2, :]] + part[1:8] + part[0:1]
                m = part[10]
                m1, cnt, m2, dup, gs, gm = (m[:, 32 * n:32 * n + 32] for n in range(6))
                top, sums = part[11][:, 0:32], part[11][:, 32:32 + G]
                ch.add(dve.tensor_tensor(tiles(sc), tiles(sig), e_bias[:].unsqueeze(1).to_broadcast([P, G, E0]),
                                         ALU.add))
                ch.wait()
                ch.add(group_max(m1, sc))
                ch.wait()
                ch.add(dve.tensor_tensor(by8(eq), by8(sc), wide(m1), ALU.is_equal))
                ch.wait()
                ch.add(dve.tensor_reduce(cnt, by8(eq), AX.X, ALU.add))
                ch.add(dve.scalar_tensor_tensor(out=oth, in0=eq, scalar=-FAR, in1=sc, op0=ALU.mult, op1=ALU.add))
                ch.wait()
                ch.add(group_max(m2, oth))
                ch.add(dve.tensor_scalar(dup, cnt, 1.5, 1.0, ALU.is_ge, ALU.subtract))
                ch.wait()
                ch.add(dve.scalar_tensor_tensor(out=dup, in0=dup, scalar=FAR, in1=m1, op0=ALU.mult, op1=ALU.add))
                ch.wait()
                ch.add(dve.tensor_tensor(m2, m2, dup, ALU.max))
                ch.wait()
                ch.add(dve.tensor_tensor(gs, m1, m2, ALU.add))
                ch.wait()
                rank_below(gm, gs.rearrange("p (j g) -> p j g", j=G), 4, t0, t1)
                ch.add(dve.tensor_tensor(by8(msk), by8(sc), wide(gm), ALU.mult))
                ch.wait()
                dve.sem_inc(wait_done, 1)
                for j in range(G):
                    ch.add(dve.max(top[:, 8 * j:8 * j + 8], tiles(msk)[:, j, :]))
                ch.wait()
                dve.sem_inc(wait_done, 1)
                for j in range(G):
                    ch.add(dve.match_replace(tiles(rep)[:, j, :], top[:, 8 * j:8 * j + 8], tiles(msk)[:, j, :],
                                             -FAR))
                ch.wait()
                ch.add(dve.tensor_tensor(sel, rep, msk, ALU.not_equal))
                ch.wait()
                ch.add(dve.tensor_tensor(t0, sel, sig, ALU.mult))
                ch.add(dve.tensor_tensor_scan(t1, sel, none[:], 0.0, ALU.add, ALU.add))
                ch.wait()
                ch.add(dve.tensor_reduce(sums, tiles(t0), AX.X, ALU.add))
                ch.add(dve.scalar_tensor_tensor(
                    out=tiles(t1), in0=tiles(t1), scalar=-1.0,
                    in1=key_base[:, bass.ds(G * i, G)].unsqueeze(2).to_broadcast([P, G, E0]),
                    op0=ALU.mult, op1=ALU.add))
                ch.wait()
                for half in range(2):
                    dve.tensor_tensor(keys2[:, :, half, :], tiles(t1), tiles(sel), ALU.mult).then_inc(key_ready, 1)
                ch.add(dve.tensor_scalar(sums, sums, 1e-20, None, ALU.add))
                ch.wait()
                ch.add(dve.reciprocal(sums, sums))
                ch.wait()
                dve.scalar_tensor_tensor(out=xw[:, i % 2, :, DIM:ROW], in0=tiles(t0), scalar=2.5,
                                         in1=sums.unsqueeze(2).to_broadcast([P, G, E0]), op0=ALU.mult,
                                         op1=ALU.mult).then_inc(rows_ready, 1)
                for j in range(G):
                    residual(NG + i, j, i, 2)
                if not last:
                    shared_product(i + 1)
                assert last or ch.k == ROUTE_CHAIN

            ch.at(ROUTE_BASE)
            none = part[12]
            ch.add(dve.memset(none, 0.0))
            ch.wait()
            ROUTE_BASE += 1
            with dve.Fori(0, NG - 1) as i:
                route(i, False)
            route(NG - 1, True)

            sl = Chain(dve, slot_chain)
            dve.wait_ge(t_ring.free, T2 + TR * NG)

            def largest(dst, src):
                for r in range(CAP // 8):
                    sl.add(dve.max(dst[:, 8 * r:8 * r + 8], src))
                    sl.wait()
                    if r < CAP // 8 - 1:
                        sl.add(dve.match_replace(src, dst[:, 8 * r:8 * r + 8], src, 0.0))
                        sl.wait()

            largest(cand[:, 0:CAP], keyT[:])
            dve.drain().then_inc(cand_ready, 1)
            dve.wait_ge(cand_moved, 16)
            largest(slots[:], cand[0:E0, :])
            dve.drain().then_inc(slots_ready, 1)
            dve.wait_ge(t_ring.free, T3)
            sl.add(dve.tensor_scalar(part[0][:, 0:E0], slotsT[:], -1.0, float(K0 * T), ALU.mult, ALU.add))
            sl.add(dve.tensor_scalar(part[1][:, 0:E0], slotsT[:], 0.0, None, ALU.is_equal))
            sl.wait()
            sl.add(dve.tensor_copy(src_idx[:], part[0][:, 0:E0]))
            sl.add(dve.tensor_tensor(part[1][:, 0:E0], part[1][:, 0:E0], spare[:], ALU.mult))
            sl.wait()
            sl.add(dve.tensor_tensor(dst_idx[:], part[0][:, 0:E0], part[1][:, 0:E0], ALU.add))
            sl.add(dve.tensor_scalar(src_idx[:], src_idx[:], 3, None, ALU.logical_shift_right))
            sl.wait()

            def stage_source(i, q):
                dve.tensor_copy(src_now[:, q, :], src_idx[:, bass.ds(8 * i + 2 * q, 2)]).then_inc(idx_now, 1)

            for q in range(3):
                stage_source(0, q)

            def experts(i, last):
                qr.at(Q3, 4, i)
                for q in range(4):
                    if not (last and q):
                        stage_source(i + (q + 3) // 4, (q + 3) % 4)
                    dve.wait_ge(s_ring.free, S3 + 4 * i + q + 1)
                    b = qr.read(dve)
                    dve.tensor_tensor(act_h[:, q % 2, :], act_g[:, q % 2, :], b[0:I0, 0:2 * P],
                                      ALU.mult).then_inc(q_ring.free, 1)
                    if i is not first_step:
                        dve.wait_ge(y_stored[q], 32 * i)
                    dve.tensor_copy(dst_now[:, q, :], dst_idx[:, bass.ds(8 * i + 2 * q, 2)]).then_inc(idx_ready, 1)
                    dve.wait_ge(y_full, 4 * i + q + 1)
                    for e in range(2):
                        dve.tensor_scalar(y[:, q, e, :], o_banks[q % 2][:, e * DIM:(e + 1) * DIM],
                                          xg[:, q, e, bass.ds(DIM + 8 * i + 2 * q + e, 1)], None,
                                          ALU.mult).then_inc(y_ready if e else idx_ready, 1)

            first_step = 0
            experts(0, False)
            with dve.Fori(1, NQ - 1) as i:
                experts(i, False)
            experts(NQ - 1, True)


            def project_keys(par):
                b = qr.read(dve)[:].rearrange("p (s h d) -> p s h d", s=2, h=H1)
                bias = bkv1[:].rearrange("p (s h d) -> p s h d", s=2, h=H1)

                def values(o, bt, v_):
                    rows = slice(o * SKV, (o + 1) * SKV)
                    return dve.tensor_tensor(
                        v_blocks[rows, par, bt, :, o, :], v_[rows].rearrange("p (q o) d -> p q o d", o=2)[:, :, o, :],
                        bias[rows, 1].rearrange("p (q o) d -> p q o d", o=2)[:, :, o, :], ALU.add)

                for o in range(2):
                    values(o, o, b[:, 1])
                dve.tensor_tensor(qk1[:, G * H1:QK, :], b[:, 0], bias[:, 0], ALU.add).then_inc(q_ring.free, 1)
                b = qr.read(dve)[:, 0:DIM].rearrange("p (h d) -> p h d", h=H1)
                values(0, 1, b)
                values(1, 0, b).then_inc(q_ring.free, 1)

            def project_queries():
                for half in range(2):
                    dve.tensor_tensor(
                        qk1[:, 2 * half * H1:2 * (half + 1) * H1, :].rearrange("p (j h) d -> p j (h d)", j=2),
                        qr.read(dve)[:].rearrange("p (j n) -> p j n", j=2),
                        bq1[:].unsqueeze(1).to_broadcast([P, 2, DIM]), ALU.add).then_inc(q_ring.free, 1)

            def centre(i):
                qr.evacuated(dve)
                ch.add(dve.tensor_reduce(qk1_stat[:, 0, :], qk1[:], AX.X, ALU.add))
                ch.wait()
                dve.scalar_tensor_tensor(out=qk1[:], in0=over_head(qk1_stat[:, 0, :]), scalar=-1.0 / D1, in1=qk1[:],
                                         op0=ALU.mult, op1=ALU.add).then_inc(q1_centred, 1)

            def deviation(i):
                dve.wait_ge(q1_squared, i + 1)
                ch.add(dve.tensor_reduce(qk1_stat[:, 0, :], qk1_sq[:], AX.X, ALU.add))
                ch.wait()
                ch.add(dve.tensor_scalar(qk1_stat[:, 0, :], qk1_stat[:, 0, :], 1.0 / D1, EPS1, ALU.mult, ALU.add))
                ch.wait()
                inverse_root(qk1_stat[:, 1, :], qk1_stat[:, 0, :], QK)

            def scale(lo, hi, w, ready):
                v, n = qk1[:, lo:hi, :], hi - lo
                ch.add(dve.tensor_tensor(v, v, over_head(qk1_stat[:, 1, lo:hi]), ALU.mult))
                ch.wait()
                ch.add(dve.tensor_tensor(v, v, w[:, 0, :].unsqueeze(1).to_broadcast([P, n, D1]), ALU.mult))
                ch.wait()
                dve.tensor_tensor(v, v, w[:, 1, :].unsqueeze(1).to_broadcast([P, n, D1]), ALU.add).then_inc(ready, 1)

            def scale_keys():
                scale(G * H1, QK, kn, k1_ready)

            def scale_queries():
                v = qk1[:, 0:G * H1, :]
                dve.tensor_tensor(v, v, over_head(qk1_stat[:, 1, 0:G * H1]), ALU.mult).then_inc(q1_scaled, 1)

            FRONT_CHAIN = NORMED_CHAIN + 1 + 2 + ROOT_CHAIN + 2

            SPANS = ((0, MAIN), (MAIN, SKV))

            def soft_spans(j):
                s_ = soft[:, j, :].rearrange("p (h k) -> p h k", h=H1)
                return [(s_[:, :, lo:hi], hi - lo, slice(n * H1, (n + 1) * H1)) for n, (lo, hi) in enumerate(SPANS)]

            def soft2_front(i, j):
                dve.wait_ge(s_ring.free, S4 + SA * i + 2 * j + 2)
                for v, n, at in soft_spans(j):
                    ch.add(dve.tensor_reduce(small[:, j, 0, at], v, AX.X, ALU.max))
                ch.wait()
                for v, n, at in soft_spans(j):
                    dve.tensor_tensor(v, v, over_head(small[:, j, 0, at], n), ALU.subtract).then_inc(shifted, 1)

            def soft2_back(i, j):
                dve.wait_ge(exp_done, NT + G * i + j + 1)
                for v, n, at in soft_spans(j):
                    ch.add(dve.tensor_reduce(small[:, j, 1, at], v, AX.X, ALU.add))
                ch.wait()
                ch.add(dve.reciprocal(small[:, j, 1, :], small[:, j, 1, :]))
                ch.wait()
                for v, n, at in soft_spans(j):
                    dve.tensor_tensor(v, v, over_head(small[:, j, 1, at], n), ALU.mult).then_inc(attn_ready, 1)

            def context_out(i, j):
                dve.wait_ge(c1_full, G * i + j + 1)
                dve.tensor_copy(c1[:, j % 2, :], o_banks[j % 2][:, 0:DIM]).then_inc(c1_ready, 1)

            def attention_out(i, j):
                dve.wait_ge(o_full, G * (2 * NG + i) + j + 1)
                xj = x[:, G * i + j, :]
                dve.scalar_tensor_tensor(out=xj, in0=o_banks[j % 2][:, DIM:2 * DIM], scalar=gates[:, 1:2], in1=xj,
                                         op0=ALU.mult, op1=ALU.add).then_inc(o_read, 1)

            def split_weights(p):
                dve.wait_ge(w_rounded, p + 1)
                dve.tensor_tensor(gu_lo[:, :, p], gu1[:, :, p], gu_hi[:, :, p], ALU.subtract).then_inc(w_split, 1)

            def split_xn(i):
                dve.wait_ge(xn_rounded, i + 1)
                dve.tensor_tensor(xnT_lo, xnT[:], xnT_hi, ALU.subtract).then_inc(xn_split, 1)

            def attention(i, norm, last):
                ch.at(ATT_BASE + FRONT_CHAIN + NORMED_CHAIN + ATT_CHAIN * i)
                qr.at(Q4 + QA, QA, i)
                soft2_front(i, 0)
                soft2_front(i, 1)
                soft2_back(i, 0)
                if not last:
                    project_keys((i + 1) % 2)
                soft2_front(i, 2)
                if not last:
                    project_queries()
                soft2_back(i, 1)
                if not last:
                    centre(i + 1)
                else:
                    split_weights(0)
                soft2_front(i, 3)
                context_out(i, 0)
                soft2_back(i, 2)
                context_out(i, 1)
                if not last:
                    deviation(i + 1)
                    scale_keys()
                else:
                    split_xn(0)
                    split_weights(1)
                attention_out(i, 0)
                soft2_back(i, 3)
                if not last:
                    scale_queries()
                else:
                    split_weights(2)
                context_out(i, 2)
                attention_out(i, 1)
                if last:
                    split_weights(3)
                    split_weights(4)
                else:
                    if norm is not first_step:
                        dve.wait_ge(y2_used, G * (norm + 1))
                    row_stats(norm)
                context_out(i, 3)
                if not last:
                    row_roots(EPS0)
                attention_out(i, 2)
                if not last:
                    row_apply(norm)
                attention_out(i, 3)
                assert last or ch.k == ATT_CHAIN, ch.k

            ATT_BASE = ROUTE_BASE + ROUTE_CHAIN * NG - NORMED_CHAIN + 1 + 2 * G
            ATT_CHAIN = FRONT_CHAIN + 5 * G
            ch.at(ATT_BASE - 1 - 2 * G)
            for q in range(4):
                dve.wait_ge(y_stored[q], 32 * NQ)
            dve.wait_ge(w3_loaded, 16 * W3)
            ch.add(dve.memset(v_blocks[:], 0.0))
            ch.wait()
            qr.at(Q4)
            def add_up(j):
                dve.wait_ge(y2_loaded[j % 2], 16 * (j // 2 + 1))
                ch.add(dve.tensor_reduce(y2_sum[:, j % 2, :], y2_rows[:, j % 2].rearrange(
                    "p (k d) -> p d k", k=K0), AX.X, ALU.add))
                ch.wait()
                dve.scalar_tensor_tensor(out=x[:, j, :], in0=y2_sum[:, j % 2, :], scalar=gates[:, 2:3],
                                         in1=x[:, j, :], op0=ALU.mult, op1=ALU.add).then_inc(y2_used, 1)

            add_up(0)
            add_up(1)
            project_keys(0)
            for j in range(2, G):
                add_up(j)
            dve.wait_ge(y2_used, G)
            normed(0, EPS0)
            add_up(G)
            project_queries()
            centre(0)
            add_up(G + 1)
            deviation(0)
            scale_keys()
            scale_queries()
            for j in range(G + 2, 2 * G):
                add_up(j)
            dve.wait_ge(y2_used, 2 * G)
            normed(1, EPS0)
            assert ch.k == 1 + 2 * G + FRONT_CHAIN + NORMED_CHAIN
            with dve.Fori(0, NG - 2) as i:
                attention(i, i + 2, False)
            attention(NG - 2, 0, False)
            attention(NG - 1, None, True)

            GATE_CHAIN = 5 + 6

            def gating(i):
                t0, t1 = rank_t[:, 0, :], rank_t[:, 1, :]
                lg, mx, sm = gate_s[:, 0, :], gate_s[:, 1, 0:G], gate_s[:, 2, 0:G]

                def wide_(v):
                    return v.unsqueeze(2).to_broadcast([P, G, E1])

                dve.wait_ge(t_ring.free, T5 + TMF - 8 + TM * i)
                ch.add(dve.tensor_reduce(mx, by8(logits[:]), AX.X, ALU.max))
                ch.wait()
                dve.tensor_tensor(by8(lg), by8(logits[:]), wide_(mx), ALU.subtract).then_inc(gate_shifted, 1)
                dve.wait_ge(gate_exp, i + 1)
                ch.add(dve.tensor_reduce(sm, by8(lg), AX.X, ALU.add))
                ch.wait()
                ch.add(dve.reciprocal(sm, sm))
                ch.wait()
                ch.add(dve.tensor_tensor(by8(lg), by8(lg), wide_(sm), ALU.mult))
                ch.wait()
                rank_below(gate_s[:, 1, :], by8(lg), 2, t0, t1)
                ch.add(dve.tensor_tensor(combine_w[:, :, 0:E1], by8(lg), by8(gate_s[:, 1, :]), ALU.mult))
                ch.wait()

            def products(i, j):
                for p in range(5):
                    dve.wait_ge(s_ring.free, S5 + SM * i + 5 * j + p + 1)
                    b = qr.read(dve)
                    for e in range(2):
                        at = (2 * p + e) * F1
                        ins = dve.scalar_tensor_tensor(
                            out=act_v[:, j % 2, at:at + F1], in0=sg[:, (j + p) % 2, e * F1:(e + 1) * F1],
                            scalar=combine_w[:, j, 2 * p + e:2 * p + e + 1], in1=b[:, e * F1:(e + 1) * F1],
                            op0=ALU.mult, op1=ALU.mult)
                    ins.then_inc(q_ring.free, 1)

            def mixture(i, last):
                ch.at(MIX_BASE + MIX_CHAIN * i)
                qr.at(Q5, QM, i)
                products(i, 0)
                if not last:
                    row_stats(i + 1)
                products(i, 1)
                if not last:
                    row_roots(EPS0)
                residual(3 * NG + i, 0, i, 3)
                if not last:
                    row_apply(i + 1)
                products(i, 2)
                residual(3 * NG + i, 1, i, 3)
                products(i, 3)
                if not last:
                    split_xn(i + 1)
                    gating(i + 1)
                residual(3 * NG + i, 2, i, 3)
                residual(3 * NG + i, 3, i, 3)
                assert last or ch.k == MIX_CHAIN, ch.k

            MIX_BASE = ATT_BASE + ATT_CHAIN * NG + NORMED_CHAIN + 1 + GATE_CHAIN
            MIX_CHAIN = GATE_CHAIN + NORMED_CHAIN
            ch.at(MIX_BASE - GATE_CHAIN - 1)
            ch.add(dve.memset(combine_w[:, :, E1:E1 + 2], 1.0))
            ch.wait()
            gating(0)
            dve.wait_ge(o_read, 2 + 3 * NT)
            with dve.Fori(0, NG - 1) as i:
                mixture(i, False)
            mixture(NG - 1, True)
            dve.drain().then_inc(x_done, 1)

        @block.scalar
        def _(act):
            sr, tr, qr = s_ring.end(), t_ring.end(), q_ring.end()
            act.dma_start(gates[:, 0:2], a["g_xattn"].partition_broadcast(P)).then_inc(gates_loaded, 16)
            act.dma_start(gates[:, 2:4], a["g_ffn"].partition_broadcast(P)).then_inc(gates_loaded, 16)
            act.dma_start(gqk[:, 0:1], a["L0_xattn_gq"].unsqueeze(1)).then_inc(gqk_loaded, 16)
            act.dma_start(gqk[:, 1:2], a["L0_xattn_gk"].unsqueeze(1)).then_inc(gqk_loaded, 16)
            act.dma_start(rwT[:], a["L0_ffn_router_weightT"].rearrange("(c p) e -> p c e", p=P)).then_inc(r_loaded, 16)
            act.dma_start(e_bias[:], a["L0_ffn_e_bias"].partition_broadcast(P)).then_inc(r_loaded, 16)
            act.dma_start(sh_gu[:], a["L0_ffn_sh_gu"].rearrange("(c p) e -> p c e", p=P)).then_inc(r_loaded, 16)
            act.dma_start(sh_dn[:], a["L0_ffn_sh_down"]).then_inc(r_loaded, 16)

            def context_in(par):
                act.activation(ctxK[:], tr.read(act)[:, 0:P], ACT.Copy).then_inc(t_ring.free, 1)
                b = tr.read(act)
                act.activation(ctxV[:, par, 0:P], b[:, 0:P], ACT.Copy)
                act.activation(ctxV[:, par, P:P + SKV], b[:, 0:SKV], ACT.Copy).then_inc(t_ring.free, 1)

            def keys_in():
                for g in range(4):
                    act.activation(kT[:, 4 * g:4 * g + 4, :], tr.read(act)[:].rearrange(
                        "p (h k) -> p h k", h=4), ACT.Copy, scale=gscale[:]).then_inc(t_ring.free, 1)

            def values_in():
                for p in range(8):
                    b = sr.read(act)
                    lo = vw[0:SKV, :, p, :]
                    act.activation(lo, b[0:SKV, :].rearrange("p (b n) -> p b n", b=2), ACT.Copy)
                    act.activation(vw[SKV:P, 0, p, :], b[SKV:P, DIM:2 * DIM], ACT.Copy)
                    act.activation(vw[SKV:P, 1, p, :], b[SKV:P, 0:DIM], ACT.Copy).then_inc(s_ring.free, 1)

            def exponential(i, j, par):
                act.wait_ge(shifted, G * i + j + 1)
                v = raw[:, par, j, :]
                act.activation(v, v, ACT.Exp).then_inc(exp_done, 1)

            def attn_out(j):
                for g in range(2):
                    act.activation(attnT[:, j % 2, 4 * g:4 * g + 4, :], tr.read(act)[:].rearrange(
                        "p (h t) -> p h t", h=4), ACT.Copy).then_inc(t_ring.free, 1)

            def tokens_in():
                for c in range(C):
                    b = tr.read(act)
                    act.activation(xnT_top[:, c, :], b[:], ACT.Copy)
                    act.activation(xnT[:, c, :], b[:], ACT.Copy).then_inc(t_ring.free, 1)
                act.drain().then_inc(xnT_rounded, 1)

            context_in(0)
            tokens_in()
            act.wait_ge(gates_loaded, 32)
            act.activation(gates[:], gates[:], ACT.Tanh).then_inc(gates_ready, 1)
            act.wait_ge(gqk_ready, 1)
            keys_in()
            act.wait_ge(wq_loaded, 16)
            for g in range(4):
                w = slice(512 * g, 512 * (g + 1))
                act.activation(wq_hi[:, :, w], wq[:, :, w], ACT.Copy).then_inc(wq_rounded, 1)

            def step(i, first_, last):
                qr.at(Q_PREP, Q_STEP, i)
                sr.at(S_PREP, S_STEP, i)
                tr.at(T_PREP - (0 if first_ else T_HEADS), T_STEP, i)
                if not last:
                    context_in((i + 1) % 2)

                def scores_out(pair):
                    b = sr.read(act)
                    act.activation(raw[:, i % 2, :, 2 * pair * SKV:2 * (pair + 1) * SKV],
                                   b[:].rearrange("p (j n) -> p j n", j=G), ACT.Copy).then_inc(s_ring.free, 1)

                exps, outs = {2: 0, 3: 1, 8: 2, 12: 3}, {5: 0, 8: 1, 12: 2, 15: 3}
                for h in range(H0):
                    qr.skip(1)
                    qr.evacuated(act)
                    act.activation(q2_hi[:, h % 3, :], qT[:, h % 3, :], ACT.Square)
                    if not (first_ and h < 2):
                        act.wait_ge(q2_split, H0 * i + h - 1)
                    act.activation(q2[h % 2], qT[:, h % 3, :], ACT.Square).then_inc(q2_ready, 1)
                    if not first_ and h in outs:
                        attn_out(outs[h])
                    if not first_ and h in exps:
                        exponential(i - 1, exps[h], (i + 1) % 2)
                    if h >= 3 and h % 2:
                        scores_out((h - 3) // 2)
                scores_out(H0 // 2 - 1)
                values_in()
                if not last:
                    tokens_in()
                    keys_in()

            step(0, True, False)
            with act.Fori(1, NG - 1) as i:
                step(i, False, False)
            step(NG - 1, False, True)
            def route_front(i):
                sr.at(S2, SR, i)
                for c in range(C):
                    act.activation(xnT[:, c, :], tr.read(act)[:], ACT.Copy).then_inc(t_ring.free, 1)
                act.wait_ge(table_stored, 16 * i if i is not first_group else 16)
                act.activation(xw[:, i % 2, :, 0:DIM], xn[:], ACT.Copy)
                act.activation(sigs[:, i % 2, :], tr.read(act)[:, 0:G * E0], ACT.Sigmoid).then_inc(t_ring.free, 1)
                if i is not first_group:
                    act.wait_ge(q_ring.free, Q2 + QR * i)
                for half in range(2):
                    act.activation(sh_g[:, half * 2 * P:(half + 1) * 2 * P], sr.read(act)[0:I0, 0:2 * P],
                                   ACT.Silu).then_inc(s_ring.free, 1)

            first_group = 0
            exponential(NG - 1, 0, (NG - 1) % 2)
            tr.at(T2 - T_HEADS)
            route_front(first_group)
            for j in range(G):
                if j + 1 < G:
                    exponential(NG - 1, j + 1, (NG - 1) % 2)
                attn_out(j)
            act.drain().then_inc(done1["act"], 1)
            for e in done1.values():
                act.wait_ge(e, 1)

            def route(i, half, last):
                tr.at(T2 + TRF, TR, i)
                if not last:
                    route_front(i + 1)
                rows = slice(half * E0, (half + 1) * E0)
                act.activation(keyT[rows, bass.ds(G * P * (i - half * (NG // 2)), G * P)], tr.read(act)[rows, :],
                               ACT.Copy).then_inc(t_ring.free, 1)

            with act.Fori(0, NG // 2) as i:
                route(i, 0, False)
            with act.Fori(NG // 2, NG - 1) as i:
                route(i, 1, False)
            route(NG - 1, 1, True)
            tr.at(T2 + TR * NG)
            act.activation(slotsT[:], tr.read(act)[:, 0:E0], ACT.Copy).then_inc(t_ring.free, 1)

            def transposed(q):
                act.activation(xgT[:, q % 2], tr.read(act)[:].rearrange(
                    "p (e c t) -> p e c t", e=2, c=C), ACT.Copy).then_inc(t_ring.free, 1)

            def experts(i, last):
                tr.at(T3 + 1, 4, i)
                sr.at(S3, 4, i)
                for q in range(4):
                    act.activation(act_g[:, q % 2, :], sr.read(act)[0:I0, 0:2 * P],
                                   ACT.Silu).then_inc(s_ring.free, 1)
                    if not (last and q == 3):
                        transposed(q + 1)

            tr.at(T3)
            transposed(0)
            with act.Fori(0, NQ - 1) as i:
                experts(i, False)
            experts(NQ - 1, True)

            def front(i):
                b = tr.read(act)
                for kind, (lo, hi) in enumerate(((0, MAIN), (MAIN, SKV))):
                    dst = ctx1T[:, kind, :].rearrange("p (b k) -> p b k", b=3)
                    src = b[:, 0:P].rearrange("p (b k) -> p b k", b=2)
                    act.activation(dst[:, 0:2, lo:hi], src[:, :, lo:hi], ACT.Copy)
                    ins = act.activation(dst[:, 2, lo:hi], src[:, 0, lo:hi], ACT.Copy)
                ins.then_inc(t_ring.free, 1)
                for c in range(C):
                    act.activation(xnT[:, c, :], tr.read(act)[:], ACT.Copy).then_inc(t_ring.free, 1)

            def squares(i):
                act.wait_ge(q1_centred, i + 1)
                act.activation(qk1_sq[:], qk1[:], ACT.Square).then_inc(q1_squared, 1)

            def keys1_in():
                act.activation(k1T[:], tr.read(act)[:, 0:C * P].rearrange("p (c t) -> p c t", c=C),
                               ACT.Copy).then_inc(t_ring.free, 1)

            def queries1_in():
                for c in range(C):
                    act.activation(q1T[:, c, :], tr.read(act)[:], ACT.Copy).then_inc(t_ring.free, 1)

            def scores_in(i):
                for j in range(G):
                    for c in range(C):
                        act.activation(soft[:, j, c * 512:(c + 1) * 512], sr.read(act)[:], ACT.Copy,
                                       scale=float(D1) ** -0.5).then_inc(s_ring.free, 1)

            def mixture_front():
                for c in range(C):
                    b = tr.read(act)
                    act.activation(xnT_hi[:, c, :], b[:], ACT.Copy)
                    act.activation(xnT[:, c, :], b[:], ACT.Copy).then_inc(t_ring.free, 1)
                act.drain().then_inc(xn_rounded, 1)
                for half in range(2):
                    act.activation(logits[:, half * 2 * E1:(half + 1) * 2 * E1], tr.read(act)[:, 0:2 * E1],
                                   ACT.Copy).then_inc(t_ring.free, 1)

            def gate_exponential(i):
                act.wait_ge(gate_shifted, i + 1)
                act.activation(gate_s[:, 0, :], gate_s[:, 0, :], ACT.Exp).then_inc(gate_exp, 1)

            def attention(i, last):
                sr.at(S4 + SA, SA, i)
                tr.at(T4 + TF, TA, i)
                if not last:
                    front(i + 1)

                def exponential(j):
                    act.wait_ge(shifted, NT + 2 * (G * i + j) + 2)
                    act.activation(soft[:, j, :], soft[:, j, :], ACT.Exp).then_inc(exp_done, 1)

                def attn_out(j):
                    for g in range(2):
                        act.activation(attnT[:, j % 2, 4 * g:4 * g + 4, :], tr.read(act)[:].rearrange(
                            "p (h t) -> p h t", h=4), ACT.Copy).then_inc(t_ring.free, 1)

                def context_out(j):
                    act.activation(c1T[:, j % 2], tr.read(act)[:, 0:DIM].rearrange("p (c t) -> p c t", c=C),
                                   ACT.Copy).then_inc(t_ring.free, 1)

                def round_weights(p):
                    act.activation(gu_hi[:, :, p], gu1[:, :, p], ACT.Copy).then_inc(w_rounded, 1)

                exponential(0)
                exponential(1)
                if last:
                    mixture_front()
                    act.wait_ge(w4_loaded, 64)
                attn_out(0)
                exponential(2)
                if last:
                    round_weights(0)
                attn_out(1)
                if not last:
                    squares(i + 1)
                else:
                    round_weights(1)
                exponential(3)
                context_out(0)
                if last:
                    round_weights(2)
                attn_out(2)
                context_out(1)
                if not last:
                    keys1_in()
                else:
                    round_weights(3)
                    round_weights(4)
                attn_out(3)
                context_out(2)
                if not last:
                    queries1_in()
                context_out(3)
                if not last:
                    scores_in(i + 1)

            act.wait_ge(mask_step, 4)
            sr.at(S4)
            tr.at(T4)
            front(0)
            squares(0)
            keys1_in()
            queries1_in()
            scores_in(0)
            with act.Fori(0, NG - 1) as i:
                attention(i, False)
            attention(NG - 1, True)

            def mixture(i, last):
                sr.at(S5, SM, i)
                tr.at(T5 + TMF, TM, i)

                def silu(j):
                    for p in range(5):
                        b = sr.read(act)
                        act.wait_ge(q_ring.free, Q5 + QM * i + 5 * j + p - 1)
                        act.activation(sg[:, (j + p) % 2, :], b[:, 0:2 * F1], ACT.Silu).then_inc(s_ring.free, 1)

                def act_out(j):
                    for g in range(4):
                        n = min(4, FC - 4 * g)
                        act.activation(attn_flat[:, 4 * g:4 * g + n, :], tr.read(act)[:, 0:n * P].rearrange(
                            "p (f t) -> p f t", f=n), ACT.Copy).then_inc(t_ring.free, 1)

                silu(0)
                silu(1)
                act_out(0)
                silu(2)
                act_out(1)
                silu(3)
                if not last:
                    mixture_front()
                act_out(2)
                if not last:
                    gate_exponential(i + 1)
                act_out(3)

            attn_flat = attnT[:].rearrange("p b f t -> p (b f) t")
            gate_exponential(0)
            with act.Fori(0, NG - 1) as i:
                mixture(i, False)
            mixture(NG - 1, True)

        @block.tensor
        def _(pe):
            qr, sr, tr = q_ring.end(), s_ring.end(), t_ring.end()

            def context_in(m):
                pe.wait_ge(ctx_loaded, 16 * (m + 1))
                for _ in range(2):
                    pe.transpose(tr.fill(pe)[:, 0:P], ctx_rows[:], ident[:]).then_inc(t_ring.full, 1)

            def keys():
                for g in range(4):
                    pe.matmul(qr.fill(pe)[:], ctxK[:], wk[:, 512 * g:512 * (g + 1)],
                              start=True, stop=True).then_inc(q_ring.full, 1)

            def transpose_keys(m):
                pe.wait_ge(kn_ready, m + 1)
                for g in range(4):
                    b = tr.fill(pe)
                    for k in range(4):
                        mm = pe.transpose(b[:, k * P:(k + 1) * P], ksb[:, 4 * g + k, :], ident[:])
                    mm.then_inc(t_ring.full, 1)

            def values(par):
                for g in range(4):
                    b = qr.fill(pe)
                    for k in range(4):
                        h = 4 * g + k
                        at = SKV * (h % 2)
                        mm = pe.matmul(b[:, k * P:(k + 1) * P], wv[:, h * D0:(h + 1) * D0],
                                       ctxV[:, par, at:at + P], start=True, stop=True)
                    mm.then_inc(q_ring.full, 1)
                for p in range(8):
                    if p % 2 == 0:
                        qr.evacuated(pe, 4 - p // 2)
                    b = sr.fill(pe)
                    for o in range(2):
                        mm = pe.matmul(b[:, o * DIM:(o + 1) * DIM], vT[:, 2 * p + o, :], wo[:, 2 * p + o, :],
                                       start=True, stop=True)
                    mm.then_inc(s_ring.full, 1)

            def transpose_xn(m):
                pe.wait_ge(xn_ready, G * (m + 1))
                for c in range(C):
                    b = tr.fill(pe)
                    for j in range(G):
                        mm = pe.transpose(b[:, j * P:(j + 1) * P], xn[:, j, c * P:(c + 1) * P], ident[:])
                    mm.then_inc(t_ring.full, 1)
                tr.evacuated(pe)

            pe.wait_ge(const_ready, 2)
            context_in(0)
            tr.evacuated(pe)
            pe.wait_ge(wk_loaded, 16)
            keys()
            transpose_xn(0)
            transpose_keys(0)

            def transpose_attn(i, j):
                pe.wait_ge(attn_ready, G * i + j + 1)
                for g in range(2):
                    b = tr.fill(pe)
                    for k in range(4):
                        at = (4 * g + k) * P
                        mm = pe.transpose(b[:, k * P:(k + 1) * P], prob[:, at:at + P], ident[:])
                    mm.then_inc(t_ring.full, 1)

            def output(i, j):
                tr.evacuated(pe)
                pe.wait_ge(o_read, G * i + j + 2)
                for p in range(8):
                    mm = pe.matmul(o_banks[0][:, 0:DIM], attnT[:, j % 2, p, :], vw[:, j // 2, p, :],
                                   start=(p == 0), stop=(p == 7))
                mm.then_inc(o_full, 1)

            def step(i, first_, last):
                qr.at(Q_PREP, Q_STEP, i)
                sr.at(S_PREP, S_STEP, i)
                tr.at(T_PREP - (0 if first_ else T_HEADS), T_STEP, i)
                if not last:
                    context_in(i + 1)
                pe.wait_ge(xnT_ready, i + 1)
                s_bank = [None]

                def scores(h, done):
                    qr.evacuated(pe, done - h)
                    pe.wait_ge(q2_split, H0 * i + h + 1)
                    place = [(h ^ 1) if j >= 2 else h for j in range(G)]
                    for half in range(2):
                        at, row = slice(half * 2 * P, (half + 1) * 2 * P), place[2 * half]
                        for n, v in enumerate((q2_hi, q2_lo)):
                            mm = pe.matmul(n_bank[0:H0, at], band_r[:, H0 - 1 - row:2 * H0 - 1 - row],
                                           v[:, h % 3, at], start=(h == half == n == 0),
                                           stop=(h == H0 - 1 and half == n == 1))
                    if h == H0 - 1:
                        mm.then_inc(q_norm, 1)
                    if h % 2 == 0:
                        s_bank[0] = sr.fill(pe)
                    for j in range(G):
                        at = (2 * j + place[j] % 2) * SKV
                        mm = pe.matmul(s_bank[0][:, at:at + SKV], qT[:, h % 3, j * P:(j + 1) * P],
                                       kT[:, h, (j // 2) * SKV:(j // 2 + 1) * SKV], start=True, stop=True)
                    if h % 2:
                        mm.then_inc(s_ring.full, 1)

                turns, outs = {5: 0, 8: 1, 12: 2, 15: 3}, {6: 0, 9: 1, 13: 2}
                for h in range(H0):
                    b = qr.fill(pe)
                    if first_ and h % 4 == 0:
                        pe.wait_ge(wq_split, h // 4 + 1)
                    terms = [(w, v, c) for c in range(C) for w, v in (
                        (wq_hi, xnT_top), (wq_hi, xnT_rest), (wq_lo, xnT_top))]
                    for n, (w, v, c) in enumerate(terms):
                        mm = pe.matmul(b[:], w[:, c, h * D0:(h + 1) * D0], v[:, c, :],
                                       start=(n == 0), stop=(n == len(terms) - 1))
                    mm.then_inc(q_ring.full, 1)
                    if not first_ and h in turns:
                        transpose_attn(i - 1, turns[h])
                    if not first_ and h in outs:
                        output(i - 1, outs[h])
                    if h >= 2:
                        scores(h - 2, h + 1)
                scores(H0 - 2, H0)
                scores(H0 - 1, H0)
                if not first_:
                    output(i - 1, G - 1)
                if not last:
                    keys()
                pe.wait_ge(n_copied, i + 1)
                pe.sem_inc(pe_wait_done, 1)
                for j in range(G):
                    mm = pe.transpose(n_bank[:, j * H0:(j + 1) * H0], n_rows[:, j * P:(j + 1) * P],
                                      ident[0:H0, 0:H0])
                mm.then_inc(q_norm, 1)
                values(i % 2)
                if not last:
                    transpose_xn(i + 1)
                    transpose_keys(i + 1)

            pe.wait_ge(wv_loaded, 16)
            pe.wait_ge(wo_loaded, 16)
            step(0, True, False)
            with pe.Fori(1, NG - 1) as i:
                step(i, False, False)
            step(NG - 1, False, True)
            def route_front(i):
                qr.at(Q2, QR, i)
                sr.at(S2, SR, i)
                transpose_xn(NG + i)
                b = tr.fill(pe)
                for j in range(G):
                    for c in range(C):
                        mm = pe.matmul(b[:, j * E0:(j + 1) * E0], xnT[:, c, j * P:(j + 1) * P], rwT[:, c, :],
                                       start=(c == 0), stop=(c == C - 1))
                mm.then_inc(t_ring.full, 1)
                for half in range(2):
                    for ring, end, o in ((s_ring, sr, 0), (q_ring, qr, I0)):
                        b = end.fill(pe)
                        for c in range(C):
                            mm = pe.matmul(b[0:I0, 0:2 * P], sh_gu[:, c, o:o + I0],
                                           xnT[:, c, half * 2 * P:(half + 1) * 2 * P], start=(c == 0),
                                           stop=(c == C - 1))
                        mm.then_inc(ring.full, 1)

            pe.wait_ge(r_loaded, 64)
            tr.at(T2 - T_HEADS)
            route_front(0)
            for j in range(G):
                transpose_attn(NG - 1, j)
                output(NG - 1, j)
            pe.drain().then_inc(done1["pe"], 1)

            def route(i, last):
                tr.at(T2 + TRF, TR, i)
                if not last:
                    route_front(i + 1)
                pe.wait_ge(q_ring.free, Q2 + QR * (i + 1))
                for j in range(G):
                    pe.wait_ge(o_read, G * (NG + i) + j + 1)
                    pe.matmul(o_banks[j % 2][:, 0:DIM], sh_h[:, j * P:(j + 1) * P], sh_dn[:], start=True,
                              stop=True).then_inc(o_full, 1)
                pe.wait_ge(key_ready, 2 * (i + 1))
                b = tr.fill(pe)
                pe.sem_inc(pe_wait_done, 1)
                for j in range(G):
                    mm = pe.transpose(b[:, j * P:(j + 1) * P], keys2[:, j].rearrange("p h e -> p (h e)"), ident[:])
                mm.then_inc(t_ring.full, 1)

            with pe.Fori(0, NG - 1) as i:
                route(i, False)
            route(NG - 1, True)
            tr.at(T2 + TR * NG)
            pe.wait_ge(slots_ready, 1)
            pe.transpose(tr.fill(pe)[:, 0:E0], slots[:], ident[0:E0, 0:E0]).then_inc(t_ring.full, 1)

            def transpose_rows(i, q):
                pe.wait_ge(xg_loaded[q], 32 * (i + 1))
                b = tr.fill(pe)
                for e in range(2):
                    for c in range(C):
                        at = (2 * e + c) * P
                        mm = pe.transpose(b[:, at:at + P], xg[:, q, e, c * P:(c + 1) * P], ident[:])
                mm.then_inc(t_ring.full, 1)

            def experts(i, last):
                qr.at(Q3, 4, i)
                sr.at(S3, 4, i)
                tr.at(T3 + 1, 4, i)
                for q in range(4):
                    pe.wait_ge(w_loaded[q], 32 * (i + 1))
                    tr.evacuated(pe)
                    for ring, end, o in ((s_ring, sr, 0), (q_ring, qr, I0)):
                        b = end.fill(pe)
                        for e in range(2):
                            for c in range(C):
                                mm = pe.matmul(b[0:I0, e * P:(e + 1) * P], w_gu[:, q, e, c, o:o + I0],
                                               xgT[:, q % 2, e, c, :], start=(c == 0), stop=(c == C - 1))
                        mm.then_inc(ring.full, 1)
                    if not (last and q == 3):
                        transpose_rows(i + (q + 1) // 4, (q + 1) % 4)
                    qr.evacuated(pe)
                    if q < 2:
                        pe.wait_ge(y_ready if i is not first_step else o_read,
                                   4 * i + q - 1 if i is not first_step else 2 + 2 * NT)
                    else:
                        pe.wait_ge(y_ready, 4 * i + q - 1)
                    for e in range(2):
                        mm = pe.matmul(o_banks[q % 2][:, e * DIM:(e + 1) * DIM], act_h[:, q % 2, e * P:(e + 1) * P],
                                       w_dn[:, q, e, :], start=True, stop=True)
                    mm.then_inc(y_full, 1)

            first_step = 0
            tr.at(T3)
            transpose_rows(0, 0)
            experts(0, False)
            with pe.Fori(1, NQ - 1) as i:
                experts(i, False)
            experts(NQ - 1, True)

            first_group = 0

            def front(i):
                pe.wait_ge(ctx_loaded, 16 * (NG + i + 1))
                pe.transpose(tr.fill(pe)[:, 0:P], ctx_rows[:], ident[:]).then_inc(t_ring.full, 1)
                if i is not first_group:
                    transpose_xn(2 * NG + i)
                else:
                    tr.evacuated(pe)
                for swapped in range(2):
                    b = qr.fill(pe)[:, 0:DIM] if swapped else qr.fill(pe)[:]
                    for kind in range(2):
                        w = wkv1[:, kind, :]
                        mm = pe.matmul(b, ctx1T[:, kind, swapped * SKV:swapped * SKV + P],
                                       w[:, DIM:2 * DIM] if swapped else w, start=(kind == 0), stop=(kind == 1))
                    mm.then_inc(q_ring.full, 1)
                if i is first_group:
                    transpose_xn(2 * NG + i)

            def project_queries():
                for half in range(2):
                    b = qr.fill(pe)
                    for k in range(2):
                        j = 2 * half + k
                        for c in range(C):
                            mm = pe.matmul(b[:, k * DIM:(k + 1) * DIM], xnT[:, c, j * P:(j + 1) * P], wq1[:, c, :],
                                           start=(c == 0), stop=(c == C - 1))
                    mm.then_inc(q_ring.full, 1)

            def keys1(i):
                pe.wait_ge(k1_ready, i + 1)
                b = tr.fill(pe)
                for c in range(C):
                    at = G * H1 + 8 * c
                    mm = pe.transpose(b[:, c * P:(c + 1) * P], qk1[:, at:at + 8, :].rearrange("p h d -> p (h d)"),
                                      ident[:])
                mm.then_inc(t_ring.full, 1)

            def queries1(i):
                pe.wait_ge(q1_ready, i + 1)
                for c in range(C):
                    b = tr.fill(pe)
                    for j in range(G):
                        at = j * H1 + 8 * c
                        mm = pe.transpose(b[:, j * P:(j + 1) * P],
                                          qk1[:, at:at + 8, :].rearrange("p h d -> p (h d)"), ident[:])
                    mm.then_inc(t_ring.full, 1)

            def scores1(i):
                pe.wait_ge(t_ring.free, T4 + TF + TA * i)
                pe.wait_ge(k_blocks_ready, 4 * (i + 1))
                for j in range(G):
                    for c in range(C):
                        pe.matmul(sr.fill(pe)[:], q1T[:, c, j * P:(j + 1) * P],
                                  k_blocks[:, j // 2, c].rearrange("p h k -> p (h k)"), start=True,
                                  stop=True).then_inc(s_ring.full, 1)

            def mixture_front(i):
                transpose_xn(3 * NG + i)
                for half in range(2):
                    b = tr.fill(pe)
                    for k in range(2):
                        j = 2 * half + k
                        for c in range(C):
                            mm = pe.matmul(b[:, k * E1:(k + 1) * E1], xnT[:, c, j * P:(j + 1) * P], gate1[:, c, :],
                                           start=(c == 0), stop=(c == C - 1))
                    mm.then_inc(t_ring.full, 1)

            def attention(i, last):
                qr.at(Q4 + QA, QA, i)
                sr.at(S4 + SA, SA, i)
                tr.at(T4 + TF, TA, i)
                if not last:
                    front(i + 1)
                else:
                    pe.wait_ge(w4_loaded, 64)
                    mixture_front(0)
                place = {}

                def transpose_attn(j):
                    pe.wait_ge(attn_ready, NT + 2 * (G * i + j) + 2)
                    for g in range(2):
                        b = tr.fill(pe)
                        for k in range(4):
                            at = (4 * g + k) * P
                            mm = pe.transpose(b[:, k * P:(k + 1) * P], soft[:, j, at:at + P], ident[:])
                        mm.then_inc(t_ring.full, 1)
                    place["a", j] = tr.k

                def contexts(j):
                    tr.evacuated(pe, tr.k - place["a", j] + 1)
                    pe.wait_ge(o_read, G * (2 * NG + i) + j + 1)
                    for p in range(8):
                        mm = pe.matmul(o_banks[j % 2][:, 32 * p:32 * (p + 1)], attnT[:, j % 2, p, :],
                                       v_blocks[:, i % 2, j // 2, p].rearrange("p o d -> p (o d)"), start=True,
                                       stop=True)
                    mm.then_inc(c1_full, 1)

                def transpose_context(j):
                    pe.wait_ge(c1_ready, G * i + j + 1)
                    b = tr.fill(pe)
                    for c in range(C):
                        mm = pe.transpose(b[:, c * P:(c + 1) * P], c1[:, j % 2, c * P:(c + 1) * P], ident[:])
                    mm.then_inc(t_ring.full, 1)
                    place["c", j] = tr.k

                def output(j):
                    tr.evacuated(pe, tr.k - place["c", j] + 1)
                    b = o_banks[j % 2][:, DIM:2 * DIM]
                    for c in range(C):
                        pe.matmul(b, c1T[:, j % 2, c, :], wo1[:, c, :], start=(c == 0), stop=False)
                    pe.matmul(b, ones[0:1, 0:P], bo1[:], start=False, stop=True).then_inc(o_full, 1)

                transpose_attn(0)
                if not last:
                    project_queries()
                transpose_attn(1)
                contexts(0)
                transpose_context(0)
                contexts(1)
                transpose_attn(2)
                output(0)
                transpose_context(1)
                contexts(2)
                if not last:
                    keys1(i + 1)
                transpose_attn(3)
                output(1)
                transpose_context(2)
                contexts(3)
                output(2)
                if not last:
                    queries1(i + 1)
                transpose_context(3)
                output(3)
                if not last:
                    scores1(i + 1)

            pe.wait_ge(w3_loaded, 16 * W3)
            qr.at(Q4)
            sr.at(S4)
            tr.at(T4)
            front(0)
            project_queries()
            keys1(0)
            queries1(0)
            scores1(0)
            with pe.Fori(0, NG - 1) as i:
                attention(i, False)
            attention(NG - 1, True)

            def mixture(i, last):
                qr.at(Q5, QM, i)
                sr.at(S5, SM, i)
                tr.at(T5 + TMF, TM, i)

                def gates_ups(j):
                    for p in range(5):
                        for o, (ring, end) in enumerate(((s_ring, sr), (q_ring, qr))):
                            b = end.fill(pe)
                            terms = [(v, w, c) for c in range(C) for v, w in (
                                (xnT_hi, gu_hi), (xnT_hi, gu_lo), (xnT_lo, gu_hi))]
                            for n, (v, w, c) in enumerate(terms):
                                mm = pe.matmul(b[:, 0:2 * F1], v[:, c, j * P:(j + 1) * P], w[:, c, p, o, :],
                                               start=(n == 0), stop=(n == len(terms) - 1))
                            mm.then_inc(ring.full, 1)

                def down(j):
                    pe.wait_ge(q_ring.free, Q5 + QM * i + 5 * (j + 1))
                    for g in range(4):
                        b = tr.fill(pe)
                        for f in range(4 * g, min(4 * g + 4, FC)):
                            n = min(P, W1 - f * P)
                            mm = pe.transpose(b[0:n, (f % 4) * P:(f % 4 + 1) * P],
                                              act_v[:, j % 2, f * P:f * P + n], ident[:])
                        mm.then_inc(t_ring.full, 1)
                    pe.wait_ge(o_read, G * (3 * NG + i) + j + 1)
                    for f in range(FC):
                        n = min(P, W1 - f * P)
                        if f % 4 == 0:
                            tr.evacuated(pe, 4 - f // 4)
                        mm = pe.matmul(o_banks[j % 2][:, 0:DIM], attn_flat[0:n, f, :], dn1[0:n, f, :],
                                       start=(f == 0), stop=(f == FC - 1))
                    mm.then_inc(o_full, 1)

                pe.wait_ge(xn_split, i + 1)
                gates_ups(0)
                gates_ups(1)
                down(0)
                gates_ups(2)
                down(1)
                gates_ups(3)
                if not last:
                    mixture_front(i + 1)
                down(2)
                down(3)

            attn_flat = attnT[:].rearrange("p b f t -> p (b f) t")
            pe.wait_ge(w_split, 5)
            with pe.Fori(0, NG - 1) as i:
                mixture(i, False)
            mixture(NG - 1, True)


_INS = ["x", "ctx_1024", "g_xattn", "g_ffn", "L0_xattn_Wq", "L0_xattn_Wk", "L0_xattn_Wv", "L0_xattn_Wo",
        "L0_xattn_gq", "L0_xattn_gk", "L0_ffn_e_bias", "L0_ffn_w_down", "L0_ffn_sh_down",
        "L1_xattn_Wq", "L1_xattn_bq",
        "L1_xattn_Wkv_dca", "L1_xattn_bkv_dca", "L1_xattn_qn_w", "L1_xattn_qn_b", "L1_xattn_kn_w",
        "L1_xattn_kn_b", "L1_xattn_kn_dca_w", "L1_xattn_kn_dca_b", "L1_xattn_Wo", "L1_xattn_bo"]


def kernel(**inputs):
    import numpy as np
    import concourse.bacc as bacc
    from concourse.bass_utils import run_bass_kernel_spmd as run

    nc = bacc.Bacc("TRN2", target_bir_lowering=False, num_devices=1)
    arrays, args = {}, {}
    laid_out = {name: inputs[name] for name in _INS}
    laid_out["L0_ffn_router_weightT"] = np.asarray(inputs["L0_ffn_router_weight"]).T
    laid_out["L0_ffn_w_gu"] = np.concatenate([inputs["L0_ffn_w_gate"], inputs["L0_ffn_w_up"]], axis=2)
    laid_out["L0_ffn_sh_gu"] = np.concatenate([inputs["L0_ffn_sh_gate"], inputs["L0_ffn_sh_up"]], axis=1)
    gu = np.asarray(inputs["L1_ffn_gate_up_weights"]).reshape(E1, 2, F1, DIM)
    shared = np.asarray(inputs["L1_ffn_shared_gate_up"]).reshape(2, 2, F1, DIM).transpose(1, 0, 2, 3)
    gu = np.concatenate([gu, shared], axis=0).reshape(5, 2, 2, F1, DIM)
    laid_out["L1_gu"] = gu.transpose(4, 0, 2, 1, 3).reshape(DIM, 5, 2, 2 * F1)
    down = np.asarray(inputs["L1_ffn_down_weights"]).transpose(0, 2, 1).reshape(E1 * F1, DIM)
    laid_out["L1_down"] = np.concatenate([down, np.asarray(inputs["L1_ffn_shared_down"]).T], axis=0)
    for name, parts in (("L1_kv_main", ("L1_xattn_Wk", "L1_xattn_Wv")), ("L1_bkv_main", ("L1_xattn_bk", "L1_xattn_bv"))):
        kv = np.concatenate([np.asarray(inputs[p]) for p in parts], axis=-1)
        laid_out[name] = kv.reshape(-1, H1, 2, D1).transpose(0, 2, 1, 3).reshape(kv.shape)
    laid_out["L1_gateT"] = np.asarray(inputs["L1_ffn_gate_weight"]).T
    for name, v in laid_out.items():
        v = np.ascontiguousarray(v)
        arrays[f"in_{name}"] = v
        args[name] = nc.dram_tensor(f"in_{name}", v.shape, mybir.dt.from_np(v.dtype), kind="ExternalInput").ap()
    out = nc.dram_tensor("out_0", (B, SQ, DIM), F32, kind="ExternalOutput").ap()
    flamingo(nc, args, out)
    r = run(nc, [arrays], core_ids=[0])
    return r.results[0]["out_0"]
```
